# Optimizing a Trainium2 kernel written in Bass

```python
import numpy as np
import jax
import jax.numpy as jnp

def _softmax(x, axis=-1):
    return jax.nn.softmax(x, axis=axis)

def _gelu(x):
    return jax.nn.gelu(x, approximate=True)

def _silu(x):
    return jax.nn.silu(x)

def _sigmoid(x):
    return jax.nn.sigmoid(x)

def _layernorm(x, axis=-1, eps=1e-05):
    m = jnp.mean(x, axis=axis, keepdims=True)
    v = jnp.var(x, axis=axis, keepdims=True)
    return (x - m) / jnp.sqrt(v + eps)

def _scatter_add(tgt, idx, src, axis=0):
    return tgt.at[idx].add(src)

def _segment_sum(src, seg, n):
    return jax.ops.segment_sum(src, seg, n)
kernel_name = 'mk_perceiver_d1_seqx_r2_d8046d'

def setup_inputs(seed: int=0):
    np.random.seed(seed)
    _w = jnp.asarray

    def _rec_inputs():
        import jax
        import jax.numpy as jnp
        _rk = jax.random.key(seed)
        x = 7.22e-05 + 1 * jax.random.normal(jax.random.fold_in(_rk, 1), (8, 64, 512), jnp.float32)
        _lenS = 64 - jax.random.randint(jax.random.fold_in(_rk, 7), (8,), 0, max(1, 64 // 4) + 1, jnp.int32)
        _lenS2 = 512 - jax.random.randint(jax.random.fold_in(_rk, 8), (8,), 0, max(1, 512 // 4) + 1, jnp.int32)
        _ctx_1024P = jax.random.normal(jax.random.fold_in(_rk, 11), (8, 16, 512), jnp.float32)
        _ctx_1024c = jax.random.dirichlet(jax.random.fold_in(_rk, 511), 0.3 * jnp.ones((16,), jnp.float32), (8, 512))
        _ctx_1024t = jnp.einsum('bsk,bkd->bsd', _ctx_1024c, _ctx_1024P)
        _ctx_1024t = _ctx_1024t * jax.lax.rsqrt(jnp.mean(jnp.square(_ctx_1024t)) + 1e-12) * 0.953939
        ctx_1024 = 4.13588e-05 + 0.999923 * (_ctx_1024t + 0.3 * jax.random.normal(jax.random.fold_in(_rk, 611), (8, 512, 512), jnp.float32))
        return (x, ctx_1024)
    x, ctx_1024 = _rec_inputs()

    def _L0_xattn_setup():
        import jax, jax.numpy as jnp
        import numpy as np
        B, TQ, TK, DIM = (4, 1024, 1024, 512)
        key = jax.random.key(seed)
        k1, k2, k3, k4 = jax.random.split(key, 4)
        inputs = jax.random.normal(k1, (B, TQ, DIM), dtype=jnp.float32)
        context = jax.random.normal(k2, (B, TK, DIM), dtype=jnp.float32)
        scale = 1.0 / np.sqrt(DIM)
        Wg = jax.random.normal(k3, (DIM, DIM), dtype=jnp.float32) * scale
        bg = jnp.zeros((DIM,), dtype=jnp.float32)
        Wo = jax.random.normal(k4, (DIM, DIM), dtype=jnp.float32) * scale
        bo = jnp.zeros((DIM,), dtype=jnp.float32)
        return {'inputs': inputs, 'context': context, 'Wg': Wg, 'bg': bg, 'Wo': Wo, 'bo': bo}
    _L0_xattn_all = _L0_xattn_setup()
    _L0_xattn_in = {k: v for k, v in _L0_xattn_all.items() if k in ('Wg', 'bg', 'Wo', 'bo')}
    del _L0_xattn_all

    def _L0_attn_setup():
        import jax, jax.numpy as jnp
        import numpy as np
        from jax.scipy.linalg import solve_triangular
        B, L, D, H = (1, 1024, 512, 4)
        DK = DV = D // H
        CONV = 4
        FIR_S, FIR_M, FIR_L = (3, 15, 63)
        CHUNK = 32

        def _l2norm(x):
            return x * jax.lax.rsqrt(jnp.sum(x * x, -1, keepdims=True) + 1e-06)

        def _short_conv(x, w):
            K = w.shape[-1]
            l = x.shape[1]
            xp = jnp.pad(x, ((0, 0), (K - 1, 0), (0, 0)))
            y = sum((xp[:, j:j + l, :] * w[:, j] for j in range(K)))
            return jax.nn.silu(y)

        def _fir(x, filt):
            b, l, h, d = x.shape
            K = filt.shape[-1]
            xf = jnp.transpose(x.reshape(b, l, h * d), (0, 2, 1))
            y = jax.lax.conv_general_dilated(xf, filt.reshape(h * d, 1, K), (1,), [(K - 1, 0)], feature_group_count=h * d)
            return jnp.transpose(y, (0, 2, 1)).reshape(b, l, h, d)

        def _delta_rule_chunkwise(q, k, v, beta):
            b, h, Lq, dk = q.shape
            c = CHUNK
            n = Lq // c
            q = _l2norm(q)
            k = _l2norm(k)
            v = v * beta[..., None]
            kb = k * beta[..., None]
            rs = lambda t: t.reshape(b, h, n, c, t.shape[-1])
            qc, kc, vc, kbc = (rs(q), rs(k), rs(v), rs(kb))
            tri_strict = jnp.tril(jnp.ones((c, c), bool), -1)
            A = jnp.where(tri_strict, -(kbc @ jnp.swapaxes(kc, -1, -2)), 0.0)
            eye = jnp.eye(c, dtype=q.dtype)
            M = eye - A
            T = solve_triangular(M, jnp.broadcast_to(eye, M.shape), lower=True)
            u = T @ vc
            w = T @ kbc
            causal = jnp.tril(jnp.ones((c, c), bool))

            def step(S, inp):
                q_i, k_i, u_i, w_i = inp
                attn = jnp.where(causal, q_i @ jnp.swapaxes(k_i, -1, -2), 0.0)
                u_adj = u_i - w_i @ S
                o_i = q_i @ S + attn @ u_adj
                return (S + jnp.swapaxes(k_i, -1, -2) @ u_adj, o_i)
            S0 = jnp.zeros((b, h, dk, v.shape[-1]), q.dtype)
            mv = lambda t: jnp.moveaxis(t, 2, 0)
            _, o = jax.lax.scan(step, S0, (mv(qc), mv(kc), mv(u), mv(w)))
            return jnp.moveaxis(o, 0, 2).reshape(b, h, Lq, -1)

        def _rmsnorm(x, w, eps=1e-05):
            return x * jax.lax.rsqrt(jnp.mean(x * x, -1, keepdims=True) + eps) * w
        key = jax.random.key(seed)
        ks = jax.random.split(key, 16)
        wn = lambda k, shape, s: jax.random.normal(k, shape, jnp.float32) * s

        def fir_init(k, K):
            f = jnp.zeros((H, DV, K), jnp.float32).at[..., -1].set(1.0)
            return f + wn(k, (H, DV, K), 0.01)
        return {'hidden_states': jax.random.normal(ks[0], (B, L, D), jnp.float32), 'Wq': wn(ks[1], (D, D), 0.02), 'Wk': wn(ks[2], (D, D), 0.02), 'Wv': wn(ks[3], (D, D), 0.02), 'Wb': wn(ks[4], (H, D), 0.02), 'conv_q': wn(ks[5], (D, CONV), 0.1), 'conv_k': wn(ks[6], (D, CONV), 0.1), 'conv_v': wn(ks[7], (D, CONV), 0.1), 'fir_s': fir_init(ks[8], FIR_S), 'fir_m': fir_init(ks[9], FIR_M), 'fir_l': fir_init(ks[10], FIR_L), 'gate_w': wn(ks[11], (H, 5, D), 1.0 / np.sqrt(D)), 'gate_b': jnp.zeros((H, 5), jnp.float32), 'log_temp': jnp.zeros((H, 1), jnp.float32), 'eps_param': jnp.full((H, 1), 0.02, jnp.float32), 'norm_w': jnp.ones((DV,), jnp.float32), 'Wo': wn(ks[12], (D, D), 0.02)}
    _L0_attn_all = _L0_attn_setup()
    _L0_attn_in = {k: v for k, v in _L0_attn_all.items() if k in ('Wq', 'Wk', 'Wv', 'Wb', 'conv_q', 'conv_k', 'conv_v', 'fir_s', 'fir_m', 'fir_l', 'gate_w', 'gate_b', 'log_temp', 'eps_param', 'norm_w', 'Wo')}
    del _L0_attn_all

    def _L0_ffn_setup():
        import jax, jax.numpy as jnp
        import numpy as np
        DIM = 512
        INTER = 512
        N_EXPERTS = 8
        TOPK = 2
        N_SHARED = 2
        key = jax.random.key(seed)
        ks = jax.random.split(key, 10)
        s = 0.02
        return {'x': jax.random.normal(ks[0], (4, 1024, DIM), dtype=jnp.float32), 'gate_w': jax.random.normal(ks[1], (N_EXPERTS, DIM), dtype=jnp.float32) * s, 'gate_bias': jax.random.normal(ks[2], (N_EXPERTS,), dtype=jnp.float32) * s, 'w1': jax.random.normal(ks[3], (N_EXPERTS, INTER, DIM), dtype=jnp.float32) * s, 'w3': jax.random.normal(ks[4], (N_EXPERTS, INTER, DIM), dtype=jnp.float32) * s, 'w2': jax.random.normal(ks[5], (N_EXPERTS, DIM, INTER), dtype=jnp.float32) * s, 'sw1': jax.random.normal(ks[6], (N_SHARED * INTER, DIM), dtype=jnp.float32) * s, 'sw3': jax.random.normal(ks[7], (N_SHARED * INTER, DIM), dtype=jnp.float32) * s, 'sw2': jax.random.normal(ks[8], (DIM, N_SHARED * INTER), dtype=jnp.float32) * s}
    _L0_ffn_all = _L0_ffn_setup()
    _L0_ffn_in = {k: v for k, v in _L0_ffn_all.items() if k in ('gate_w', 'gate_bias', 'w1', 'w3', 'w2', 'sw1', 'sw3', 'sw2')}
    del _L0_ffn_all
    return {'x': x, 'ctx_1024': ctx_1024, 'L0_xattn_Wg': _L0_xattn_in['Wg'], 'L0_xattn_bg': _L0_xattn_in['bg'], 'L0_xattn_Wo': _L0_xattn_in['Wo'], 'L0_xattn_bo': _L0_xattn_in['bo'], 'L0_attn_Wq': _L0_attn_in['Wq'], 'L0_attn_Wk': _L0_attn_in['Wk'], 'L0_attn_Wv': _L0_attn_in['Wv'], 'L0_attn_Wb': _L0_attn_in['Wb'], 'L0_attn_conv_q': _L0_attn_in['conv_q'], 'L0_attn_conv_k': _L0_attn_in['conv_k'], 'L0_attn_conv_v': _L0_attn_in['conv_v'], 'L0_attn_fir_s': _L0_attn_in['fir_s'], 'L0_attn_fir_m': _L0_attn_in['fir_m'], 'L0_attn_fir_l': _L0_attn_in['fir_l'], 'L0_attn_gate_w': _L0_attn_in['gate_w'], 'L0_attn_gate_b': _L0_attn_in['gate_b'], 'L0_attn_log_temp': _L0_attn_in['log_temp'], 'L0_attn_eps_param': _L0_attn_in['eps_param'], 'L0_attn_norm_w': _L0_attn_in['norm_w'], 'L0_attn_Wo': _L0_attn_in['Wo'], 'L0_ffn_gate_w': _L0_ffn_in['gate_w'], 'L0_ffn_gate_bias': _L0_ffn_in['gate_bias'], 'L0_ffn_w1': _L0_ffn_in['w1'], 'L0_ffn_w3': _L0_ffn_in['w3'], 'L0_ffn_w2': _L0_ffn_in['w2'], 'L0_ffn_sw1': _L0_ffn_in['sw1'], 'L0_ffn_sw3': _L0_ffn_in['sw3'], 'L0_ffn_sw2': _L0_ffn_in['sw2']}

def reference(x, ctx_1024, L0_xattn_Wg, L0_xattn_bg, L0_xattn_Wo, L0_xattn_bo, L0_attn_Wq, L0_attn_Wk, L0_attn_Wv, L0_attn_Wb, L0_attn_conv_q, L0_attn_conv_k, L0_attn_conv_v, L0_attn_fir_s, L0_attn_fir_m, L0_attn_fir_l, L0_attn_gate_w, L0_attn_gate_b, L0_attn_log_temp, L0_attn_eps_param, L0_attn_norm_w, L0_attn_Wo, L0_ffn_gate_w, L0_ffn_gate_bias, L0_ffn_w1, L0_ffn_w3, L0_ffn_w2, L0_ffn_sw1, L0_ffn_sw3, L0_ffn_sw2):
    import jax
    import jax.numpy as jnp

    def _L0_xattn_ref(inputs, context, Wg, bg, Wo, bo):
        import jax, jax.numpy as jnp
        import numpy as np
        B, TQ, TK, DIM = (4, 1024, 1024, 512)
        gate_signal = jnp.einsum('bkd,de->bke', context, Wg) + bg
        attn = jnp.einsum('bkd,bqd->bkq', gate_signal, inputs)
        attn = jax.nn.softmax(attn, axis=1)
        out = jnp.einsum('bkq,bkd->bqd', attn, context)
        return jnp.einsum('bqd,de->bqe', out, Wo) + bo

    def _L0_attn_ref(hidden_states, Wq, Wk, Wv, Wb, conv_q, conv_k, conv_v, fir_s, fir_m, fir_l, gate_w, gate_b, log_temp, eps_param, norm_w, Wo):
        import jax, jax.numpy as jnp
        import numpy as np
        from jax.scipy.linalg import solve_triangular
        B, L, D, H = (1, 1024, 512, 4)
        DK = DV = D // H
        CONV = 4
        FIR_S, FIR_M, FIR_L = (3, 15, 63)
        CHUNK = 32

        def _l2norm(x):
            return x * jax.lax.rsqrt(jnp.sum(x * x, -1, keepdims=True) + 1e-06)

        def _short_conv(x, w):
            K = w.shape[-1]
            l = x.shape[1]
            xp = jnp.pad(x, ((0, 0), (K - 1, 0), (0, 0)))
            y = sum((xp[:, j:j + l, :] * w[:, j] for j in range(K)))
            return jax.nn.silu(y)

        def _fir(x, filt):
            b, l, h, d = x.shape
            K = filt.shape[-1]
            xf = jnp.transpose(x.reshape(b, l, h * d), (0, 2, 1))
            y = jax.lax.conv_general_dilated(xf, filt.reshape(h * d, 1, K), (1,), [(K - 1, 0)], feature_group_count=h * d)
            return jnp.transpose(y, (0, 2, 1)).reshape(b, l, h, d)

        def _delta_rule_chunkwise(q, k, v, beta):
            b, h, Lq, dk = q.shape
            c = CHUNK
            n = Lq // c
            q = _l2norm(q)
            k = _l2norm(k)
            v = v * beta[..., None]
            kb = k * beta[..., None]
            rs = lambda t: t.reshape(b, h, n, c, t.shape[-1])
            qc, kc, vc, kbc = (rs(q), rs(k), rs(v), rs(kb))
            tri_strict = jnp.tril(jnp.ones((c, c), bool), -1)
            A = jnp.where(tri_strict, -(kbc @ jnp.swapaxes(kc, -1, -2)), 0.0)
            eye = jnp.eye(c, dtype=q.dtype)
            M = eye - A
            T = solve_triangular(M, jnp.broadcast_to(eye, M.shape), lower=True)
            u = T @ vc
            w = T @ kbc
            causal = jnp.tril(jnp.ones((c, c), bool))

            def step(S, inp):
                q_i, k_i, u_i, w_i = inp
                attn = jnp.where(causal, q_i @ jnp.swapaxes(k_i, -1, -2), 0.0)
                u_adj = u_i - w_i @ S
                o_i = q_i @ S + attn @ u_adj
                return (S + jnp.swapaxes(k_i, -1, -2) @ u_adj, o_i)
            S0 = jnp.zeros((b, h, dk, v.shape[-1]), q.dtype)
            mv = lambda t: jnp.moveaxis(t, 2, 0)
            _, o = jax.lax.scan(step, S0, (mv(qc), mv(kc), mv(u), mv(w)))
            return jnp.moveaxis(o, 0, 2).reshape(b, h, Lq, -1)

        def _rmsnorm(x, w, eps=1e-05):
            return x * jax.lax.rsqrt(jnp.mean(x * x, -1, keepdims=True) + eps) * w
        b, l, d = hidden_states.shape
        q = _short_conv(hidden_states @ Wq.T, conv_q).reshape(b, l, H, DK)
        k = _short_conv(hidden_states @ Wk.T, conv_k).reshape(b, l, H, DK)
        v_direct = _short_conv(hidden_states @ Wv.T, conv_v).reshape(b, l, H, DV)
        beta = jax.nn.sigmoid(hidden_states @ Wb.T)
        tp = lambda t: jnp.transpose(t, (0, 2, 1, 3))
        delta_out = tp(_delta_rule_chunkwise(tp(q), tp(k), tp(v_direct), jnp.transpose(beta, (0, 2, 1))))
        local_s = _fir(v_direct, fir_s)
        local_m = _fir(v_direct, fir_m)
        local_l = _fir(v_direct, fir_l)
        logits = jnp.einsum('bld,hpd->blhp', hidden_states, gate_w) + gate_b
        temp = jnp.exp(log_temp).reshape(1, 1, H, 1)
        probs = jax.nn.softmax(logits / temp, -1)
        eps = jnp.clip(eps_param, 0.0, 0.2).reshape(1, 1, H, 1)
        probs = probs * (1.0 - 5.0 * eps) + eps
        o = probs[..., 0:1] * local_s + probs[..., 1:2] * local_m + probs[..., 2:3] * local_l + probs[..., 3:4] * delta_out + probs[..., 4:5] * v_direct
        o = _rmsnorm(o, norm_w)
        return o.reshape(b, l, H * DV) @ Wo.T

    def _L0_ffn_ref(x, gate_w, gate_bias, w1, w3, w2, sw1, sw3, sw2):
        import jax, jax.numpy as jnp
        import numpy as np
        DIM = 512
        INTER = 512
        N_EXPERTS = 8
        TOPK = 2
        N_SHARED = 2
        shape = x.shape
        xt = x.reshape(-1, shape[-1])
        scores = jax.nn.softmax((xt @ gate_w.T).astype(jnp.float32), axis=-1)
        _, idx = jax.lax.top_k(scores + gate_bias, TOPK)
        weights = jnp.take_along_axis(scores, idx, axis=1).astype(x.dtype)
        y = jnp.zeros_like(xt)
        for e in range(N_EXPERTS):
            gate_e = jnp.sum(jnp.where(idx == e, weights, 0.0), axis=1)
            h = jax.nn.silu(xt @ w1[e].T) * (xt @ w3[e].T)
            y = y + gate_e[:, None] * (h @ w2[e].T)
        z = jax.nn.silu(xt @ sw1.T) * (xt @ sw3.T) @ sw2.T
        return (y + z).reshape(shape)
    x = x + _L0_xattn_ref(_layernorm(x, axis=-1), ctx_1024, L0_xattn_Wg, L0_xattn_bg, L0_xattn_Wo, L0_xattn_bo)
    x = x + _L0_attn_ref(_layernorm(x, axis=-1), L0_attn_Wq, L0_attn_Wk, L0_attn_Wv, L0_attn_Wb, L0_attn_conv_q, L0_attn_conv_k, L0_attn_conv_v, L0_attn_fir_s, L0_attn_fir_m, L0_attn_fir_l, L0_attn_gate_w, L0_attn_gate_b, L0_attn_log_temp, L0_attn_eps_param, L0_attn_norm_w, L0_attn_Wo)
    x = x + _L0_ffn_ref(_layernorm(x, axis=-1), L0_ffn_gate_w, L0_ffn_gate_bias, L0_ffn_w1, L0_ffn_w3, L0_ffn_w2, L0_ffn_sw1, L0_ffn_sw3, L0_ffn_sw2)
    return x

_drawn_inputs = setup_inputs


def setup_inputs(seed=0):
    import zlib

    import numpy as np

    out = dict(_drawn_inputs(seed))
    spreads = {'L0_xattn_bg': (0.0, 2.0),
     'L0_xattn_bo': (0.0, 0.1),
     'L0_attn_gate_b': (0.0, 0.8),
     'L0_attn_log_temp': (0.0, 0.8),
     'L0_attn_eps_param': (0.019999999552965164, 0.6),
     'L0_attn_norm_w': (1.0, 0.2)}
    factors = {'L0_attn_Wb': 8.0,
     'L0_attn_fir_s': 8.0,
     'L0_ffn_gate_w': 7.224,
     'L0_ffn_gate_bias': 8.0,
     'L0_ffn_w1': 6.218,
     'L0_ffn_w3': 5.945,
     'L0_ffn_w2': 5.94,
     'L0_ffn_sw1': 8.0,
     'L0_ffn_sw3': 8.0,
     'L0_ffn_sw2': 8.0}
    for name, (base, spread) in spreads.items():
        noise = np.random.default_rng([zlib.crc32(name.encode()), seed]).standard_normal(out[name].shape)
        drawn = base * np.exp(spread * noise) if base else spread * noise
        out[name] = jnp.asarray(drawn.astype(out[name].dtype))
    for name, factor in factors.items():
        out[name] = (out[name] * factor).astype(out[name].dtype)
    return out
```

```python
from contextlib import ExitStack

import numpy as np
import concourse.bass as bass
from concourse import mybir

P = 128
B, L, D = 8, 64, 512
TK = 512
H, DV = 4, 128
NT = B * L // P
PAIR = P // L
DC = D // P
NTOK = B * L
KS, KM, KL, KC = 3, 15, 63, 4
NE, NSH, FF = 8, 2, 512
NX = NE + NSH
FC = FF // P
LEVELS = (2, 4, 8, 16, 32)
NPROB = 5

C_CONV = 0
C_FIR = C_CONV + 3 * H * KC
C_NORM = C_FIR + H * (KS + KM + KL)
C_BG = C_NORM + 1
C_GATE = C_BG + DC
C_ROUT = C_GATE + DC * 24
NCOL = C_ROUT + DC * NE
R_BO = 0
R_GB = R_BO + D
R_TEMP = R_GB + H * NPROB
R_EPS = R_TEMP + H
R_RB = R_EPS + H
NROW = R_RB + NE
M_ID, M_STRICT, M_INCL, M_L1 = 0, 1, 2, 3
NMASK = M_L1 + 1 + len(LEVELS)

F32 = mybir.dt.float32
ALU = mybir.AluOpType
ACT = mybir.ActivationFunctionType
AX = mybir.AxisListType.X
FIRS = ((KS, 0), (KM, KS), (KL, KS + KM))


def perceiver_block(nc, x_in, ctx_in, ctxT_in, wg_in, wox_in, wqkv_in, wod_in, wffn_in, cols_in, rows_in,
                    masks_in, out):
    with ExitStack() as stack:
        def sb(name, shape):
            return stack.enter_context(nc.sbuf_tensor(name, shape, F32))

        def sem(name):
            return stack.enter_context(nc.semaphore(name))

        x = sb("x", [P, NT, D])
        xnT = sb("xnT", [P, DC, NTOK])
        ring = sb("ring", [P, 4, 8192])
        part = sb("part", [P, 3, 4, 512])
        early = sb("early", [P, 3, 2048])
        cols = sb("cols", [P, NCOL])
        rows = sb("rows", [P, NROW])
        masks = sb("masks", [P, NMASK, P])
        small = sb("small", [P, 800])
        bank = [stack.enter_context(nc.psum_tensor(f"bank{i}", [P, 512], F32)) for i in range(8)]

        ident = masks[:, M_ID, :]
        ctxT = [ring[:, t, 0:4096].rearrange("p (b c k) -> p b c k", b=PAIR, c=DC) for t in range(NT)]
        ctx = [ring[:, t, 4096:8192].rearrange("p (b c d) -> p b c d", b=PAIR, c=TK // P) for t in range(NT)]
        wgT, wox, xn = part[:, 0], part[:, 1], part[:, 2]
        yT = early[:, 0, :].rearrange("p (c n) -> p c n", c=DC)
        probs_b = early[:, 1, 0:1024].rearrange("p (i n) -> p i n", i=2)
        probsT_b = early[:, 1, 1024:2048].rearrange("p (i n) -> p i n", i=2)
        oT_b = early[:, 2, 0:1024].rearrange("p (i n) -> p i n", i=2)
        sq_b = early[:, 2, 1024:2048].rearrange("p (i n) -> p i n", i=2)
        wqkv = ring[:, 0, 0:6144].rearrange("p (j c n) -> p j c n", j=3, c=DC)
        wod = ring[:, 0, 6144:8192].rearrange("p (h n) -> p h n", h=H)
        vP, kP, qP, kbP = (ring[:, 1, 2048 * i:2048 * i + 2048].rearrange("p (h n) -> p h n", h=H) for i in range(4))
        plane = [vP, kP, qP]
        mt, lt, tt, att = (ring[:, 2, 2048 * i:2048 * i + 2048].rearrange("p (h n) -> p h n", h=H) for i in range(4))
        tm, yy, bv = (ring[:, 3, 2048 * i:2048 * i + 2048].rearrange("p (h n) -> p h n", h=H) for i in range(3))
        sq2 = ring[:, 3, 6144:7168].rearrange("p (i n) -> p i n", i=2)
        ct = ring[0:24, 3, 7168:7680]
        branch = [part[:, i] for i in range(3)]
        slots = [early[:, :, :], ring[:, 2, 0:6144].rearrange("p (j n) -> p j n", j=3),
                 ring[:, 3, 0:6144].rearrange("p (j n) -> p j n", j=3),
                 ring[:, 0, 0:6144].rearrange("p (j n) -> p j n", j=3)]
        hT_b = [part[:, 1], part[:, 2]]
        silu_b = ring[:, 1, 0:1024].rearrange("p (i n) -> p i n", i=2)

        at = [0]

        def take(n):
            at[0] += n
            assert at[0] <= 800
            return small[:, at[0] - n:at[0]]
        stats = take(NT * 6).rearrange("p (t n) -> p t n", t=NT)
        mv = take(NT * 2).rearrange("p (t n) -> p t n", t=NT)
        rs_in, rs_y, rs_a, rs_b = take(32), take(32), take(32), take(32)
        half = take(32)
        ones = take(2)
        mx, mc, nb, c0s, sm, rsm = (take(NT) for _ in range(6))
        lg = take(NT * 24).rearrange("p (t n) -> p t n", t=NT)
        gt = take(NT * 20).rearrange("p (t n) -> p t n", t=NT)
        gtm = take(NT * H)
        beta = take(NT * H).rearrange("p (t h) -> p t h", t=NT)
        itemp, epsc, epsm = take(H), take(H), take(H)
        ktr = take(32)
        cc = take(NT * 24).rearrange("p (t n) -> p t n", t=NT)
        orr = take(H * NT)
        rl = take(NT * NE).rearrange("p (t n) -> p t n", t=NT)
        prio = take(NE)
        gate = take(NT * NX).rearrange("p (t n) -> p t n", t=NT)
        rw1, rw2 = (take(NT * NE).rearrange("p (t n) -> p t n", t=NT) for _ in range(2))
        rq = take(NT)

        ld_x = [sem(f"ld_x{t}") for t in range(NT)]
        ld_masks, ld_cols, ld_rows, ld_wg, ld_wox, ld_wqkv, ld_wod = (
            sem(n) for n in ("ld_masks", "ld_cols", "ld_rows", "ld_wg", "ld_wox", "ld_wqkv", "ld_wod"))
        ld_ctxT = [sem(f"ld_ctxT{t}") for t in range(NT)]
        ld_ctx = [sem(f"ld_ctx{t}") for t in range(NT)]
        ld_ffn = [sem(f"ld_ffn{i}") for i in range(4)]
        stored = sem("stored")
        dve_step, act_step, pool_step = sem("dve_step"), sem("act_step"), sem("pool_step")
        names = ("pow_wanted", "pow_done", "pool_consts", "xn_ready", "xT_done", "xnT_ready", "y_done", "yT_ready",
                 "c0_done", "c0_read", "s_done", "bias_ready", "exp_done", "p_ready", "pT_done", "pT_ready",
                 "oT_done", "oT_ready", "proj_done", "x1_done", "gate_done", "gate_read", "gate_exp_wanted",
                 "gate_exp_done", "qkv_done", "lag0_done", "conv_done", "silu_done", "sq_done", "sumsq_done",
                 "vt_done", "bv_ready", "cc_ready", "ct_done", "ct_ready", "kb_done", "kb_ready", "kk_done",
                 "mt_ready", "at_done", "at_ready", "tt1_ready", "t1_done", "t1_ready", "lt_ready", "yl_done",
                 "yl_ready", "z_done", "zt_done", "t_upd", "tt_upd", "u_done", "u_ready", "o_done", "d_ready",
                 "bc_done", "weighted", "o_ready", "osq_ready", "osum_done", "m_done", "x2_done", "rout_done",
                 "rout_read", "rexp_wanted", "rexp_done", "gates_ready", "h1_done", "h3_done", "fsilu_done",
                 "hT_ready", "ye_done", "acc_done", "wod_scaled")
        S = {n: sem(n) for n in names}
        for_count = {}

        def signal(ins, s):
            for_count[s.name] = for_count.get(s.name, 0) + 1
            ins.then_inc(s, 1)
            return for_count[s.name]

        def after(eng, ins, s):
            eng.wait_ge(s, signal(ins, s))

        block = stack.enter_context(nc.Block())

        @block.sync
        def _(sp):
            sp.dma_start(x[:, 0], x_in[0]).then_inc(ld_x[0], 16)
            sp.dma_start(masks[:], masks_in).then_inc(ld_masks, 16)
            for t in range(1, NT):
                sp.dma_start(x[:, t], x_in[t]).then_inc(ld_x[t], 16)
            sp.dma_start(wgT, wg_in).then_inc(ld_wg, 16)
            sp.dma_start(cols[:], cols_in).then_inc(ld_cols, 16)
            sp.dma_start(rows[:], rows_in).then_inc(ld_rows, 16)
            for t in range(NT):
                sp.dma_start(ring[:, t, 0:4096], ctxT_in[t]).then_inc(ld_ctxT[t], 16)
                sp.dma_start(ring[:, t, 4096:8192], ctx_in[t]).then_inc(ld_ctx[t], 16)
                if t == 0:
                    sp.dma_start(wox, wox_in).then_inc(ld_wox, 16)
            sp.wait_ge(S["oT_done"], 1)
            sp.dma_start(ring[:, 0, 0:6144], wqkv_in).then_inc(ld_wqkv, 16)
            sp.dma_start(ring[:, 0, 6144:8192], wod_in).then_inc(ld_wod, 16)
            free = {0: [("osum_first", 0)], }
            sp.wait_ge(S["sumsq_done"], 2 * H)
            sp.wait_ge(S["proj_done"], NT)
            for e in range(NX):
                if e == 1:
                    sp.wait_ge(S["o_done"], H)
                if e == 2:
                    sp.wait_ge(S["o_ready"], H)
                    sp.wait_ge(S["osum_done"], H)
                if e == 3:
                    sp.wait_ge(S["m_done"], NT * H)
                if e >= 4:
                    sp.wait_ge(S["ye_done"], NT * (e - 3))
                sp.dma_start(slots[e % 4], wffn_in[e].rearrange("p (j n) -> p j n", j=3)).then_inc(ld_ffn[e % 4], 16)
            for t in range(NT):
                sp.wait_ge(S["acc_done"], NT * (NX - 1) + t + 1)
                sp.dma_start(out[t], x[:, t]).then_inc(stored, 16)
            sp.wait_ge(stored, 16 * NT)

        @block.gpsimd
        def _(pool):
            pool.memset(half[:], -0.5).then_inc(S["pool_consts"], 1)
            pool.memset(ones[:], 1.0).then_inc(S["pool_consts"], 1)
            pool.wait_ge(S["pool_consts"], 2)

            def power(n, width):
                pool.wait_ge(S["pow_wanted"], n)
                pool.tensor_tensor(rs_y[:, 0:width], rs_in[:, 0:width], half[:, 0:width],
                                   ALU.pow).then_inc(S["pow_done"], 1)
            for t in range(2 * NT):
                power(t + 1, 1)
            power(2 * NT + 1, 32)
            for l in range(len(LEVELS)):
                for h in range(H):
                    if l == 0:
                        pool.wait_ge(S["mt_ready"], h + 1)
                    else:
                        pool.wait_ge(S["yl_done"], H * (l - 1) + h + 1)
                    m = masks[:, M_L1 + 1 + l, :].unsqueeze(1).broadcast_to([P, NT, P])
                    pool.tensor_tensor(lt[:, h].rearrange("p (t n) -> p t n", t=NT),
                                       mt[:, h].rearrange("p (t n) -> p t n", t=NT), m,
                                       ALU.mult).then_inc(S["lt_ready"], 1)
            for h in range(H):
                pool.wait_ge(S["weighted"], NPROB * (h + 1))
                after(pool, pool.tensor_tensor(branch[0][:, h], branch[0][:, h], branch[1][:, h], ALU.add), pool_step)
                after(pool, pool.tensor_tensor(branch[2][:, h], branch[2][:, h], tm[:, h], ALU.add), pool_step)
                after(pool, pool.tensor_tensor(branch[0][:, h], branch[0][:, h], branch[2][:, h], ALU.add), pool_step)
                pool.tensor_tensor(branch[0][:, h], branch[0][:, h], vP[:, h], ALU.add).then_inc(S["o_ready"], 1)
            power(2 * NT + 2, 16)
            for t in range(NT):
                power(2 * NT + 3 + t, 1)

        @block.tensor
        def _(pe):
            def transpose_tile(layer, t):
                pe.wait_ge(S["xn_ready"], layer * NT + t + 1)
                if layer == 0 and t == 0:
                    pe.wait_ge(ld_masks, 16)
                if t >= 2:
                    pe.wait_ge(S["xnT_ready"], layer * NT + t - 1)
                for c in range(DC):
                    last = pe.transpose(bank[t % 2][:, c * P:(c + 1) * P], xn[:, t, c * P:(c + 1) * P], ident)
                last.then_inc(S["xT_done"], 1)

            for t in range(NT):
                transpose_tile(0, t)
            pe.wait_ge(ld_wg, 16)
            pe.wait_ge(ld_cols, 16)
            for t in range(NT):
                pe.wait_ge(S["xnT_ready"], t + 1)
                if t >= 2:
                    pe.wait_ge(S["yT_ready"], t - 1)
                for c in range(DC):
                    for e in range(DC):
                        last = pe.matmul(bank[2 + t % 2][:, c * P:(c + 1) * P], wgT[:, e, c * P:(c + 1) * P],
                                         xnT[:, e, t * P:(t + 1) * P], start=(e == 0), stop=(e == DC - 1))
                last.then_inc(S["y_done"], 1)
            for t in range(NT):
                for e in range(DC):
                    last = pe.matmul(bank[4][:, t:t + 1], xnT[:, e, t * P:(t + 1) * P], cols[:, C_BG + e:C_BG + e + 1],
                                     start=(e == 0), stop=(e == DC - 1))
                last.then_inc(S["c0_done"], 1)

            def scores(t):
                pe.wait_ge(S["yT_ready"], t + 1)
                pe.wait_ge(ld_ctxT[t], 16)
                if t >= 2:
                    pe.wait_ge(S["exp_done"], t - 1)
                for c in range(DC):
                    for b in range(PAIR):
                        last = pe.matmul(bank[5 + t % 2][b * L:(b + 1) * L, :],
                                         yT[:, c, t * P + b * L:t * P + (b + 1) * L], ctxT[t][:, b, c, :],
                                         start=(c == 0), stop=(c == DC - 1))
                last.then_inc(S["s_done"], 1)

            def values(t):
                pe.wait_ge(S["p_ready"], t + 1)
                if t >= 1:
                    pe.wait_ge(S["pT_ready"], t)
                for k in range(TK // P):
                    last = pe.transpose(bank[7][:, k * P:(k + 1) * P], probs_b[:, t % 2, k * P:(k + 1) * P], ident)
                last.then_inc(S["pT_done"], 1)
                pe.wait_ge(S["pT_ready"], t + 1)
                pe.wait_ge(ld_ctx[t], 16)
                if t < 2:
                    pe.wait_ge(S["xnT_ready"], NT)
                else:
                    pe.wait_ge(S["oT_ready"], t - 1)
                for c in range(DC):
                    for b in range(PAIR):
                        for k in range(TK // P):
                            last = pe.matmul(bank[t % 2][:, c * P + b * L:c * P + (b + 1) * L],
                                             ctx[t][:, b, k, c * P:(c + 1) * P],
                                             probsT_b[:, t % 2, k * P + b * L:k * P + (b + 1) * L],
                                             start=(k == 0), stop=(k == TK // P - 1))
                last.then_inc(S["oT_done"], 1)

            def project(t):
                pe.wait_ge(S["oT_ready"], t + 1)
                pe.wait_ge(ld_wox, 16)
                if t < 2:
                    pe.wait_ge(S["yT_ready"], NT)
                else:
                    pe.wait_ge(S["x1_done"], t - 1)
                for c in range(DC):
                    last = pe.matmul(bank[2 + t % 2][:, :], oT_b[:, t % 2, c * P:(c + 1) * P], wox[:, c, :],
                                     start=(c == 0), stop=(c == DC - 1))
                last.then_inc(S["proj_done"], 1)

            scores(0)
            scores(1)
            for t in range(NT):
                values(t)
                if t + 2 < NT:
                    scores(t + 2)
                if t >= 1:
                    project(t - 1)
            project(NT - 1)

            pe.wait_ge(S["oT_ready"], NT)
            for t in range(NT):
                transpose_tile(1, t)
            for t in range(NT):
                pe.wait_ge(S["xnT_ready"], NT + t + 1)
                for c in range(DC):
                    last = pe.matmul(bank[4][:, 32 + 24 * t:56 + 24 * t], xnT[:, c, t * P:(t + 1) * P],
                                     cols[:, C_GATE + 24 * c:C_GATE + 24 * (c + 1)], start=(c == 0), stop=(c == DC - 1))
                last.then_inc(S["gate_done"], 1)
            pe.wait_ge(ld_wqkv, 16)

            def sumsq(i):
                pe.wait_ge(S["sq_done"], i + 1)
                for t in range(NT):
                    last = pe.matmul(bank[4][:, 256 + NT * i + t:257 + NT * i + t], sq_b[:, i % 2, t * P:(t + 1) * P],
                                     ones[:, 0:1], start=True, stop=True)
                last.then_inc(S["sumsq_done"], 1)

            for g in range(3 * H):
                j, h = g // H, g % H
                if g >= 3:
                    pe.wait_ge(S["conv_done"], g - 2)
                for c in range(DC):
                    last = pe.matmul(bank[5 + g % 3][:, :], wqkv[:, j, c, h * P:(h + 1) * P], xnT[:, c, :],
                                     start=(c == 0), stop=(c == DC - 1))
                last.then_inc(S["qkv_done"], 1)
                if g >= H + 2:
                    sumsq(g - H - 2)
            for h in range(H):
                pe.wait_ge(S["silu_done"], h + 1)
                if h >= 2:
                    pe.wait_ge(S["bv_ready"], h - 1)
                for t in range(NT):
                    last = pe.transpose(bank[h % 2][:, t * P:(t + 1) * P], vP[:, h, t * P:(t + 1) * P], ident)
                last.then_inc(S["vt_done"], 1)
            sumsq(2 * H - 2)
            sumsq(2 * H - 1)
            pe.wait_ge(S["cc_ready"], 1)
            for t in range(NT):
                last = pe.transpose(bank[3][0:24, t * P:(t + 1) * P], cc[:, t, :], ident)
            last.then_inc(S["ct_done"], 1)
            pe.wait_ge(S["ct_ready"], 1)

            def spread(dst, row):
                return pe.matmul(dst, masks[0:24, M_ID, row:row + 1].broadcast_to([24, P]), ct, start=True, stop=True)

            for h in range(H):
                pe.wait_ge(S["conv_done"], 3 * H)
                if h >= 3:
                    pe.wait_ge(S["kb_ready"], h - 2)
                spread(bank[5 + h % 3][:, :], H * NPROB + h).then_inc(S["kb_done"], 1)
            pe.wait_ge(S["bv_ready"], H)
            for h in range(H):
                pe.wait_ge(S["kb_ready"], h + 1)
                for t in range(NT):
                    s = slice(t * P, (t + 1) * P)
                    last = pe.matmul(bank[h][:, s], kP[:, h, s], kbP[:, h, s], start=True, stop=True)
                last.then_inc(S["kk_done"], 1)
            pe.wait_ge(S["kb_ready"], H)
            for h in range(H):
                for t in range(NT):
                    s = slice(t * P, (t + 1) * P)
                    last = pe.matmul(bank[4 + h][:, s], kP[:, h, s], qP[:, h, s], start=True, stop=True)
                last.then_inc(S["at_done"], 1)
            for h in range(H):
                pe.wait_ge(S["tt1_ready"], h + 1)
                for t in range(NT):
                    s = slice(t * P, (t + 1) * P)
                    last = pe.transpose(bank[h][:, s], tt[:, h, s], ident)
                last.then_inc(S["t1_done"], 1)
            pe.wait_ge(S["at_ready"], H)
            for l in range(len(LEVELS)):
                final = l == len(LEVELS) - 1
                for h in range(H):
                    pe.wait_ge(S["lt_ready"], H * l + h + 1)
                    if l == 0:
                        pe.wait_ge(S["t1_ready"], h + 1)
                    else:
                        pe.wait_ge(S["t_upd"], H * (l - 1) + h + 1)
                    for t in range(NT):
                        s = slice(t * P, (t + 1) * P)
                        last = pe.matmul(bank[h][:, s], lt[:, h, s], tm[:, h, s], start=True, stop=True)
                    last.then_inc(S["yl_done"], 1)
                for h in range(H):
                    n = H * l + h
                    pe.wait_ge(S["yl_ready"], n + 1)
                    if n >= 2:
                        pe.wait_ge(S["tt_upd"], n - 1)
                    for t in range(NT):
                        s = slice(t * P, (t + 1) * P)
                        last = pe.matmul(bank[5 + 2 * (h % 2)][:, s], yy[:, h, s], tt[:, h, s], start=True, stop=True)
                    last.then_inc(S["zt_done"], 1)
                    if not final:
                        for t in range(NT):
                            s = slice(t * P, (t + 1) * P)
                            last = pe.matmul(bank[4 + 2 * (h % 2)][:, s], tt[:, h, s], yy[:, h, s],
                                             start=True, stop=True)
                        last.then_inc(S["z_done"], 1)
            for h in range(H):
                pe.wait_ge(S["tt_upd"], H * (len(LEVELS) - 1) + h + 1)
                for t in range(NT):
                    s = slice(t * P, (t + 1) * P)
                    last = pe.matmul(bank[h][:, s], tt[:, h, s], bv[:, h, s], start=True, stop=True)
                last.then_inc(S["u_done"], 1)
            for h in range(H):
                pe.wait_ge(S["u_ready"], h + 1)
                for t in range(NT):
                    s = slice(t * P, (t + 1) * P)
                    last = pe.matmul(bank[4 + h][:, s], yy[:, h, s], att[:, h, s], start=True, stop=True)
                last.then_inc(S["o_done"], 1)
            for n in range(H * NPROB):
                if n >= 4:
                    pe.wait_ge(S["weighted"], n - 3)
                else:
                    pe.wait_ge(S["u_ready"], H)
                spread(bank[n % 4][:, :], n).then_inc(S["bc_done"], 1)
            pe.wait_ge(S["d_ready"], H)
            for h in range(H):
                pe.wait_ge(S["osq_ready"], h + 1)
                for t in range(NT):
                    last = pe.matmul(bank[7][:, H * t + h:H * t + h + 1], sq2[:, h % 2, t * P:(t + 1) * P],
                                     ones[:, 0:1], start=True, stop=True)
                last.then_inc(S["osum_done"], 1)
            pe.wait_ge(S["wod_scaled"], H)
            for n in range(NT * H):
                t, h = n // H, n % H
                if n >= 3:
                    pe.wait_ge(S["x2_done"], n - 2)
                pe.matmul(bank[4 + n % 3][:, :], branch[0][:, h, t * P:(t + 1) * P], wod[:, h, :],
                          start=True, stop=True).then_inc(S["m_done"], 1)

            pe.wait_ge(S["weighted"], H * NPROB)
            for t in range(NT):
                transpose_tile(2, t)
            for t in range(NT):
                pe.wait_ge(S["xnT_ready"], 2 * NT + t + 1)
                for c in range(DC):
                    last = pe.matmul(bank[3][:, NE * t:NE * (t + 1)], xnT[:, c, t * P:(t + 1) * P],
                                     cols[:, C_ROUT + NE * c:C_ROUT + NE * (c + 1)], start=(c == 0), stop=(c == DC - 1))
                last.then_inc(S["rout_done"], 1)
            pe.wait_ge(S["x2_done"], NT * H)

            def up(e):
                pe.wait_ge(ld_ffn[e % 4], 16 * (e // 4 + 1))
                w = slots[e % 4].rearrange("p j (c n) -> p j c n", c=DC)
                for f in range(FC):
                    n = e * FC + f
                    if n == 1:
                        pe.wait_ge(S["rout_read"], 1)
                    if n >= 2:
                        pe.wait_ge(S["hT_ready"], n - 1)
                    for j, name in ((0, "h1_done"), (1, "h3_done")):
                        for c in range(DC):
                            last = pe.matmul(bank[2 * (n % 2) + j][:, :], w[:, j, c, f * P:(f + 1) * P], xnT[:, c, :],
                                             start=(c == 0), stop=(c == DC - 1))
                        last.then_inc(S[name], 1)

            def down(e):
                w = slots[e % 4].rearrange("p j (c n) -> p j c n", c=DC)
                pe.wait_ge(S["hT_ready"], FC * (e + 1))
                for t in range(NT):
                    if e >= 1:
                        pe.wait_ge(S["acc_done"], NT * (e - 1) + t + 1)
                    for f in range(FC):
                        last = pe.matmul(bank[4 + t][:, :], hT_b[e % 2][:, f, t * P:(t + 1) * P], w[:, 2, f, :],
                                         start=(f == 0), stop=(f == FC - 1))
                    last.then_inc(S["ye_done"], 1)

            for e in range(NX):
                up(e)
                if e >= 1:
                    down(e - 1)
            down(NX - 1)

        @block.scalar
        def _(act):
            def store_xnT(layer, t):
                act.wait_ge(S["xT_done"], layer * NT + t + 1)
                if layer == 1:
                    act.wait_ge(S["c0_done"], NT)
                if layer == 2:
                    act.wait_ge(S["qkv_done"], 3 * H)
                act.activation(xnT[:, :, t * P:(t + 1) * P], bank[t % 2][:, :].rearrange("p (c n) -> p c n", c=DC),
                               ACT.Copy).then_inc(S["xnT_ready"], 1)

            for t in range(NT):
                store_xnT(0, t)
            for t in range(NT):
                act.wait_ge(S["bias_ready"], t + 1)
                if t >= 2:
                    act.wait_ge(S["pT_done"], t - 1)
                act.activation(probs_b[:, t % 2, :], bank[5 + t % 2][:, :], ACT.Exp, bias=nb[:, t:t + 1],
                               accum_out=sm[:, t:t + 1]).then_inc(S["exp_done"], 1)
                act.wait_ge(S["pT_done"], t + 1)
                if t >= 2:
                    act.wait_ge(S["oT_done"], t - 1)
                act.activation(probsT_b[:, t % 2, :], bank[7][:, :], ACT.Copy).then_inc(S["pT_ready"], 1)
            for t in range(NT):
                store_xnT(1, t)
            act.wait_ge(S["gate_exp_wanted"], 1)
            after(act, act.activation(itemp, rows[:, R_TEMP:R_TEMP + H], ACT.Exp, scale=-1.0), act_step)
            act.activation(beta, lg[:, :, 20:24], ACT.Exp, scale=-1.0).then_inc(S["gate_exp_done"], 1)
            act.wait_ge(S["gate_exp_wanted"], 2)
            act.activation(gt, gt, ACT.Exp).then_inc(S["gate_exp_done"], 1)

            def lag0(g):
                act.wait_ge(S["qkv_done"], g + 1)
                if g == 0:
                    act.wait_ge(S["oT_done"], NT)
                j, h = g // H, g % H
                w = C_CONV + (j * H + h) * KC + KC - 1
                act.activation(plane[j][:, h], bank[5 + g % 3][:, :], ACT.Copy,
                               scale=cols[:, w:w + 1]).then_inc(S["lag0_done"], 1)

            def silu(g):
                j, h = g // H, g % H
                act.wait_ge(S["conv_done"], g + 1)
                act.activation(plane[j][:, h], plane[j][:, h], ACT.Silu).then_inc(S["silu_done"], 1)
                if j > 0:
                    i = g - H
                    act.wait_ge(S["silu_done"], g + 1)
                    if i >= 2:
                        act.wait_ge(S["sumsq_done"], i - 1)
                    act.activation(sq_b[:, i % 2, :], plane[j][:, h], ACT.Square).then_inc(S["sq_done"], 1)

            lag0(0)
            for g in range(1, 3 * H):
                lag0(g)
                silu(g - 1)
            silu(3 * H - 1)
            act.wait_ge(S["ct_done"], 1)
            act.activation(ct, bank[3][0:24, :], ACT.Copy).then_inc(S["ct_ready"], 1)
            for h in range(H):
                act.wait_ge(S["t1_done"], h + 1)
                act.activation(tm[:, h], bank[h][:, :], ACT.Copy).then_inc(S["t1_ready"], 1)
            for l in range(len(LEVELS)):
                for h in range(H):
                    n = H * l + h
                    act.wait_ge(S["yl_done"], n + 1)
                    if l >= 1:
                        act.wait_ge(S["z_done"], n - H + 1)
                    act.activation(yy[:, h], bank[h][:, :], ACT.Copy).then_inc(S["yl_ready"], 1)
            for h in range(H):
                act.wait_ge(S["u_done"], h + 1)
                act.wait_ge(S["zt_done"], H * len(LEVELS))
                act.activation(yy[:, h], bank[h][:, :], ACT.Copy).then_inc(S["u_ready"], 1)
            for h in range(H):
                act.wait_ge(S["o_done"], h + 1)
                act.activation(tm[:, h], bank[4 + h][:, :], ACT.Copy).then_inc(S["d_ready"], 1)
            for h in range(H):
                act.wait_ge(S["o_ready"], h + 1)
                if h >= 2:
                    act.wait_ge(S["osum_done"], h - 1)
                act.activation(sq2[:, h % 2, :], branch[0][:, h], ACT.Square).then_inc(S["osq_ready"], 1)
            for t in range(NT):
                store_xnT(2, t)
            act.wait_ge(S["rexp_wanted"], 1)
            act.activation(rl, rl, ACT.Exp).then_inc(S["rexp_done"], 1)
            for n in range(NX * FC):
                act.wait_ge(S["h1_done"], n + 1)
                if n < 2:
                    act.wait_ge(S["o_ready"], H)
                else:
                    act.wait_ge(S["hT_ready"], n - 1)
                act.activation(silu_b[:, n % 2, :], bank[2 * (n % 2)][:, :], ACT.Silu).then_inc(S["fsilu_done"], 1)

        @block.vector
        def _(dve):
            pow_count = [0]

            def do(ins):
                after(dve, ins, dve_step)

            def rsqrt(dst, width):
                a, b, v, y = (r[:, 0:width] for r in (rs_a, rs_b, rs_in, rs_y))
                pow_count[0] += 1
                dve.wait_ge(S["pow_done"], pow_count[0])
                do(dve.tensor_tensor(a, v, y, ALU.mult))
                do(dve.tensor_tensor(b, a, y, ALU.mult))
                do(dve.tensor_scalar(a, b, -0.5, 1.5, ALU.mult, ALU.add))
                do(dve.tensor_tensor(dst, a, y, ALU.mult))

            def layernorm(layer, t):
                do(dve.bn_stats(stats[:, t, :], x[:, t, :]))
                do(dve.bn_aggr(mv[:, t, :], stats[:, t, :]))
                after(dve, dve.tensor_scalar(rs_in[:, 0:1], mv[:, t, 1:2], 1e-5, None, ALU.add), S["pow_wanted"])
                rsqrt(rq[:, t:t + 1], 1)
                if layer >= 1:
                    dve.wait_ge(S["xT_done"], (layer - 1) * NT + t + 1)
                dve.tensor_scalar(xn[:, t, :], x[:, t, :], mv[:, t, 0:1], rq[:, t:t + 1], ALU.subtract,
                                  ALU.mult).then_inc(S["xn_ready"], 1)

            for t in range(NT):
                dve.wait_ge(ld_x[t], 16)
                layernorm(0, t)
            for t in range(NT):
                dve.wait_ge(S["y_done"], t + 1)
                dve.tensor_copy(yT[:, :, t * P:(t + 1) * P],
                                bank[2 + t % 2][:, :].rearrange("p (c n) -> p c n", c=DC)).then_inc(S["yT_ready"], 1)
            dve.wait_ge(S["c0_done"], NT)
            after(dve, dve.tensor_copy(c0s, bank[4][:, 0:NT]), S["c0_read"])
            dve.wait_ge(ld_rows, 16)
            for t in range(NT):
                dve.wait_ge(S["xn_ready"], NT)
                do(dve.tensor_tensor(x[:, t, :], x[:, t, :], rows[:, R_BO:R_BO + D], ALU.add))

            def score_bias(t):
                dve.wait_ge(S["s_done"], t + 1)
                do(dve.tensor_reduce(mx[:, t:t + 1], bank[5 + t % 2][:, :], AX, ALU.max))
                do(dve.tensor_tensor(mc[:, t:t + 1], mx[:, t:t + 1], c0s[:, t:t + 1], ALU.add))
                dve.tensor_tensor(nb[:, t:t + 1], c0s[:, t:t + 1], mc[:, t:t + 1],
                                  ALU.subtract).then_inc(S["bias_ready"], 1)

            def add_projection(t):
                dve.wait_ge(S["proj_done"], t + 1)
                after(dve, dve.tensor_tensor(x[:, t, :], x[:, t, :], bank[2 + t % 2][:, :], ALU.add), S["x1_done"])
                layernorm(1, t)

            score_bias(0)
            for t in range(NT):
                dve.wait_ge(S["exp_done"], t + 1)
                do(dve.reciprocal(rsm[:, t:t + 1], sm[:, t:t + 1]))
                dve.tensor_scalar(probs_b[:, t % 2, :], probs_b[:, t % 2, :], rsm[:, t:t + 1], None,
                                  ALU.mult).then_inc(S["p_ready"], 1)
                if t + 1 < NT:
                    score_bias(t + 1)
                dve.wait_ge(S["oT_done"], t + 1)
                if t >= 2:
                    dve.wait_ge(S["proj_done"], t - 1)
                dve.tensor_copy(oT_b[:, t % 2, :], bank[t % 2][:, :]).then_inc(S["oT_ready"], 1)
                if t >= 1:
                    add_projection(t - 1)
            add_projection(NT - 1)

            dve.wait_ge(S["gate_done"], NT)
            after(dve, dve.tensor_copy(lg, bank[4][:, 32:32 + 24 * NT].rearrange("p (t n) -> p t n", t=NT)),
                  S["gate_exp_wanted"])
            dve.wait_ge(S["gate_exp_done"], 1)
            do(dve.tensor_scalar(beta, beta, 1.0, None, ALU.add))
            do(dve.reciprocal(beta, beta))
            gt4 = gt.rearrange("p t (h n) -> p t h n", h=H)

            def over_tokens(ap, n):
                return ap.unsqueeze(1).broadcast_to([P, NT, n])
            do(dve.tensor_tensor(gt, lg[:, :, 0:20], over_tokens(rows[:, R_GB:R_GB + 20], 20), ALU.add))
            for t in range(NT):
                g3 = gt[:, t, :].rearrange("p (h n) -> p h n", h=H)
                do(dve.tensor_tensor(g3, g3, itemp.unsqueeze(2).broadcast_to([P, H, NPROB]), ALU.mult))
            gth = gt.rearrange("p t (h n) -> p (t h) n", h=H)
            do(dve.tensor_reduce(gtm, gth, AX, ALU.max))
            spreadm = gtm.unsqueeze(2).broadcast_to([P, NT * H, NPROB])
            after(dve, dve.tensor_tensor(gth, gth, spreadm, ALU.subtract), S["gate_exp_wanted"])
            dve.wait_ge(S["gate_exp_done"], 2)
            do(dve.tensor_reduce(gtm, gth, AX, ALU.add))
            do(dve.reciprocal(gtm, gtm))
            do(dve.tensor_tensor(gth, gth, spreadm, ALU.mult))
            do(dve.tensor_scalar(epsc, rows[:, R_EPS:R_EPS + H], 0.0, 0.2, ALU.max, ALU.min))
            do(dve.tensor_scalar(epsm, epsc, -float(NPROB), 1.0, ALU.mult, ALU.add))
            for t in range(NT):
                g3 = gt[:, t, :].rearrange("p (h n) -> p h n", h=H)
                do(dve.tensor_tensor(g3, g3, epsm.unsqueeze(2).broadcast_to([P, H, NPROB]), ALU.mult))
                do(dve.tensor_tensor(g3, g3, epsc.unsqueeze(2).broadcast_to([P, H, NPROB]), ALU.add))

            for h in range(H):
                dve.wait_ge(ld_wod, 16)
                dve.tensor_scalar(wod[:, h, :], wod[:, h, :], cols[:, C_NORM:C_NORM + 1], None,
                                  ALU.mult).then_inc(S["wod_scaled"], 1)

            def lagged(dst, src, w, lag):
                d = dst.rearrange("p (b l) -> p b l", b=B)[:, :, lag:L]
                s = src.rearrange("p (b l) -> p b l", b=B)[:, :, 0:L - lag]
                return dve.scalar_tensor_tensor(out=d, in0=s, scalar=w, in1=d, op0=ALU.mult, op1=ALU.add)

            def fir_steps():
                for h in range(H):
                    dve.wait_ge(S["silu_done"], h + 1)
                    for i, (taps, off) in enumerate(FIRS):
                        if h == 0:
                            dve.wait_ge(S["xT_done"], 2 * NT)
                        w0 = C_FIR + h * (KS + KM + KL) + off
                        for lag in range(taps):
                            w = cols[:, w0 + taps - 1 - lag:w0 + taps - lag]
                            if lag == 0:
                                do(dve.tensor_scalar(branch[i][:, h], vP[:, h], w, None, ALU.mult))
                            else:
                                do(lagged(branch[i][:, h], vP[:, h], w, lag))
                            yield
            firs = fir_steps()

            def fir(n):
                for _ in range(n):
                    next(firs, None)

            for g in range(3 * H):
                j, h = g // H, g % H
                dve.wait_ge(S["lag0_done"], g + 1)
                for lag in range(1, KC):
                    w = C_CONV + (j * H + h) * KC + KC - 1 - lag
                    ins = lagged(plane[j][:, h], bank[5 + g % 3][:, :], cols[:, w:w + 1], lag)
                    if lag < KC - 1:
                        do(ins)
                    else:
                        ins.then_inc(S["conv_done"], 1)
                if g >= 2:
                    fir(2)
            for h in range(H):
                dve.wait_ge(S["vt_done"], h + 1)
                dve.tensor_tensor(bv[:, h].rearrange("p (t n) -> p t n", t=NT),
                                  bank[h % 2][:, :].rearrange("p (t n) -> p t n", t=NT),
                                  beta[:, :, h:h + 1].broadcast_to([P, NT, P]), ALU.mult).then_inc(S["bv_ready"], 1)
            dve.wait_ge(S["sumsq_done"], 2 * H)
            after(dve, dve.tensor_scalar(rs_in[:, 0:32], bank[4][:, 256:288], 1e-6, None, ALU.add), S["pow_wanted"])
            rsqrt(ktr, 32)
            ktr3 = ktr.rearrange("p (i t) -> p t i", t=NT)
            for t in range(NT):
                do(dve.tensor_tensor(cc[:, t, 20:24], beta[:, t, :], ktr3[:, t, 0:H], ALU.mult))
                do(dve.tensor_copy(cc[:, t, 0:20], gt[:, t, :]))
                ins = dve.tensor_tensor(cc[:, t, 3:20:NPROB], gt[:, t, 3:20:NPROB], ktr3[:, t, H:2 * H], ALU.mult)
                if t < NT - 1:
                    do(ins)
                else:
                    ins.then_inc(S["cc_ready"], 1)
            for h in range(H):
                dve.wait_ge(S["kb_done"], h + 1)
                dve.tensor_tensor(kbP[:, h], kP[:, h], bank[5 + h % 3][:, :], ALU.mult).then_inc(S["kb_ready"], 1)
            for h in range(H):
                dve.wait_ge(S["kk_done"], h + 1)
                for t in range(NT):
                    s = slice(t * P, (t + 1) * P)
                    ins = dve.scalar_tensor_tensor(out=mt[:, h, s], in0=bank[h][:, s],
                                                   scalar=ktr[:, NT * h + t:NT * h + t + 1],
                                                   in1=masks[:, M_STRICT, :], op0=ALU.mult, op1=ALU.mult)
                    if t < NT - 1:
                        do(ins)
                    else:
                        after(dve, ins, S["mt_ready"])
                m1 = masks[:, M_L1, :].unsqueeze(1).broadcast_to([P, NT, P])
                eye = ident.unsqueeze(1).broadcast_to([P, NT, P])
                t3 = tt[:, h].rearrange("p (t n) -> p t n", t=NT)
                do(dve.tensor_tensor(t3, mt[:, h].rearrange("p (t n) -> p t n", t=NT), m1, ALU.mult))
                dve.tensor_tensor(t3, eye, t3, ALU.subtract).then_inc(S["tt1_ready"], 1)
                fir(2)
            for h in range(H):
                dve.wait_ge(S["at_done"], h + 1)
                for t in range(NT):
                    s = slice(t * P, (t + 1) * P)
                    ins = dve.scalar_tensor_tensor(out=att[:, h, s], in0=bank[4 + h][:, s],
                                                   scalar=ktr[:, NT * h + t:NT * h + t + 1],
                                                   in1=masks[:, M_INCL, :], op0=ALU.mult, op1=ALU.mult)
                    if t < NT - 1:
                        do(ins)
                    else:
                        ins.then_inc(S["at_ready"], 1)
            for l in range(len(LEVELS)):
                for h in range(H):
                    fir(11)
                    n = H * l + h
                    if l < len(LEVELS) - 1:
                        dve.wait_ge(S["z_done"], n + 1)
                        dve.tensor_tensor(tm[:, h], tm[:, h], bank[4 + 2 * (h % 2)][:, :],
                                          ALU.subtract).then_inc(S["t_upd"], 1)
                    dve.wait_ge(S["zt_done"], n + 1)
                    dve.tensor_tensor(tt[:, h], tt[:, h], bank[5 + 2 * (h % 2)][:, :],
                                      ALU.subtract).then_inc(S["tt_upd"], 1)
            fir(10 ** 6)
            for h in range(H):
                for i, dst in enumerate((branch[0], branch[1], branch[2], tm, vP)):
                    if i == 3:
                        dve.wait_ge(S["d_ready"], h + 1)
                    dve.wait_ge(S["bc_done"], h * NPROB + i + 1)
                    dve.tensor_tensor(dst[:, h], dst[:, h], bank[(h * NPROB + i) % 4][:, :],
                                      ALU.mult).then_inc(S["weighted"], 1)
            dve.wait_ge(S["osum_done"], H)
            after(dve, dve.tensor_scalar(rs_in[:, 0:16], bank[7][:, 0:16], 1.0 / DV, 1e-5, ALU.mult, ALU.add),
                  S["pow_wanted"])
            rsqrt(orr, 16)
            for t in range(NT):
                for h in range(H):
                    n = t * H + h
                    dve.wait_ge(S["m_done"], n + 1)
                    after(dve, dve.scalar_tensor_tensor(out=x[:, t, :], in0=bank[4 + n % 3][:, :],
                                                        scalar=orr[:, n:n + 1], in1=x[:, t, :], op0=ALU.mult,
                                                        op1=ALU.add), S["x2_done"])
                layernorm(2, t)

            dve.wait_ge(S["rout_done"], NT)
            after(dve, dve.tensor_copy(rl, bank[3][:, 0:NT * NE].rearrange("p (t n) -> p t n", t=NT)), S["rout_read"])
            do(dve.tensor_reduce(mx, rl, AX, ALU.max))

            def per_tile(ap):
                return ap.unsqueeze(2).broadcast_to([P, NT, NE])
            after(dve, dve.tensor_tensor(rl, rl, per_tile(mx), ALU.subtract), S["rexp_wanted"])
            for e in range(NE):
                do(dve.memset(prio[:, e:e + 1], float(NE - e)))
            do(dve.memset(gate[:, :, :], 1.0))
            dve.wait_ge(S["rexp_done"], 1)
            do(dve.tensor_reduce(sm, rl, AX, ALU.add))
            do(dve.reciprocal(rsm, sm))
            do(dve.tensor_tensor(rl, rl, per_tile(rsm), ALU.mult))
            do(dve.tensor_tensor(rw1, rl, over_tokens(rows[:, R_RB:R_RB + NE], NE), ALU.add))
            for k in range(2):
                do(dve.tensor_reduce(mx, rw1, AX, ALU.max))
                do(dve.tensor_tensor(rw2, rw1, per_tile(mx), ALU.is_equal))
                do(dve.tensor_tensor(rw2, rw2, over_tokens(prio, NE), ALU.mult))
                do(dve.tensor_reduce(mx, rw2, AX, ALU.max))
                do(dve.tensor_tensor(rw2, rw2, per_tile(mx), ALU.is_equal))
                if k == 0:
                    do(dve.tensor_copy(gate[:, :, 0:NE], rw2))
                    do(dve.scalar_tensor_tensor(out=rw1, in0=rw2, scalar=-1e30, in1=rw1, op0=ALU.mult, op1=ALU.add))
                else:
                    do(dve.tensor_tensor(gate[:, :, 0:NE], gate[:, :, 0:NE], rw2, ALU.add))
            do(dve.tensor_tensor(gate[:, :, 0:NE], gate[:, :, 0:NE], rl, ALU.mult))

            def hidden(e):
                for f in range(FC):
                    n = e * FC + f
                    dve.wait_ge(S["fsilu_done"], n + 1)
                    dve.wait_ge(S["h3_done"], n + 1)
                    if e >= 2:
                        dve.wait_ge(S["ye_done"], NT * (e - 1))
                    elif e == 0:
                        dve.wait_ge(S["xT_done"], 3 * NT)
                        dve.wait_ge(S["o_ready"], H)
                    dve.tensor_tensor(hT_b[e % 2][:, f, :], silu_b[:, n % 2, :], bank[2 * (n % 2) + 1][:, :],
                                      ALU.mult).then_inc(S["hT_ready"], 1)

            def accumulate(e):
                for t in range(NT):
                    dve.wait_ge(S["ye_done"], NT * e + t + 1)
                    dve.scalar_tensor_tensor(out=x[:, t, :], in0=bank[4 + t][:, :], scalar=gate[:, t, e:e + 1],
                                             in1=x[:, t, :], op0=ALU.mult, op1=ALU.add).then_inc(S["acc_done"], 1)
            hidden(0)
            for e in range(1, NX):
                hidden(e)
                if e >= 2:
                    dve.wait_ge(S["acc_done"], NT * (e - 1))
                accumulate(e - 1)
            dve.wait_ge(S["acc_done"], NT * (NX - 1))
            accumulate(NX - 1)


def kernel(**inputs):
    import concourse.bacc as bacc
    from concourse.bass_utils import run_bass_kernel_spmd

    a = {k: np.asarray(v) for k, v in inputs.items()}

    def chunks(w):
        return w.reshape(-1, P, w.shape[1]).transpose(1, 0, 2).reshape(P, -1)

    ctx = a["ctx_1024"]
    by_tile = ctx.reshape(NT, PAIR, TK // P, P, D).transpose(0, 3, 1, 2, 4).reshape(NT, P, -1)
    byT = ctx.transpose(0, 2, 1).reshape(NT, PAIR, DC, P, TK).transpose(0, 3, 1, 2, 4).reshape(NT, P, -1)
    fir = np.concatenate([a[f"L0_attn_fir_{s}"].transpose(1, 0, 2) for s in "sml"], axis=2)
    conv = np.stack([a[f"L0_attn_conv_{s}"].reshape(H, P, KC) for s in "vkq"]).transpose(2, 0, 1, 3)
    wgate = np.concatenate([a["L0_attn_gate_w"].reshape(H * NPROB, D), a["L0_attn_Wb"]]).T
    cols = np.concatenate([conv.reshape(P, -1), fir.reshape(P, -1), a["L0_attn_norm_w"].reshape(P, 1),
                           a["L0_xattn_bg"].reshape(DC, P).T, chunks(wgate), chunks(a["L0_ffn_gate_w"].T)], axis=1)
    row = np.concatenate([a["L0_xattn_bo"], a["L0_attn_gate_b"].ravel(), a["L0_attn_log_temp"].ravel(),
                          a["L0_attn_eps_param"].ravel(), a["L0_ffn_gate_bias"]])
    w1 = list(a["L0_ffn_w1"]) + list(a["L0_ffn_sw1"].reshape(NSH, FF, D))
    w3 = list(a["L0_ffn_w3"]) + list(a["L0_ffn_sw3"].reshape(NSH, FF, D))
    w2 = list(a["L0_ffn_w2"]) + list(a["L0_ffn_sw2"].reshape(D, NSH, FF).transpose(1, 0, 2))
    i, j = np.meshgrid(np.arange(P), np.arange(P), indexing="ij")
    same = i // L == j // L
    merge = [(i // (2 * m) == j // (2 * m)) & (i // m % 2 == 0) & (j // m % 2 == 1) for m in (1,) + LEVELS]
    masks = np.stack([i == j, same & (i < j), same & (i <= j)] + merge, axis=1).astype(np.float32)
    arrays = {
        "x_in": a["x"].reshape(NT, P, D),
        "ctx_in": by_tile,
        "ctxT_in": byT,
        "wg_in": chunks(a["L0_xattn_Wg"].T).reshape(P, DC, D),
        "wox_in": chunks(a["L0_xattn_Wo"]).reshape(P, DC, D),
        "wqkv_in": np.concatenate([chunks(a[f"L0_attn_W{s}"].T) for s in "vkq"], axis=1),
        "wod_in": chunks(a["L0_attn_Wo"].T),
        "wffn_in": np.stack([np.concatenate([chunks(p.T), chunks(q.T), chunks(r.T)], axis=1)
                             for p, q, r in zip(w1, w3, w2)]),
        "cols_in": cols,
        "rows_in": np.broadcast_to(row, (P, NROW)),
        "masks_in": masks,
    }
    arrays = {k: np.ascontiguousarray(v) for k, v in arrays.items()}
    nc = bacc.Bacc("TRN2", target_bir_lowering=False, num_devices=1)
    args = [nc.dram_tensor(k, v.shape, mybir.dt.from_np(v.dtype), kind="ExternalInput").ap() for k, v in arrays.items()]
    args.append(nc.dram_tensor("out", (NT, P, D), F32, kind="ExternalOutput").ap())
    perceiver_block(nc, *args)
    r = run_bass_kernel_spmd(nc, [arrays], core_ids=[0])
    return r.results[0]["out"].reshape(B, L, D)
```

```python
from contextlib import ExitStack

import numpy as np
import concourse.bass as bass
from concourse import mybir

P = 128
B, L, D = 8, 64, 512
TK = 512
H, DV = 4, 128
NT = B * L // P
PAIR = P // L
DC = D // P
NTOK = B * L
KS, KM, KL, KC = 3, 15, 63, 4
NE, NSH, FF = 8, 2, 512
NX = NE + NSH
FC = FF // P
LAGS_PE = 16
FIR_PACE = 6
LEVELS = (2, 4, 8, 16, 32)
NPROB = 5

C_CONV = 0
C_FIR = C_CONV + 3 * H * KC
C_NORM = C_FIR + H * (KS + KM + KL)
C_GATE = C_NORM + 1
C_ROUT = C_GATE + DC * 24
NCOL = C_ROUT + DC * NE
R_BO = 0
R_GB = R_BO + D
R_TEMP = R_GB + H * NPROB
R_EPS = R_TEMP + H
R_RB = R_EPS + H
NROW = R_RB + NE
M_ID, M_STRICT, M_INCL, M_L1 = 0, 1, 2, 3
M_BEFORE = M_L1 + 1 + len(LEVELS)
NMASK = M_BEFORE + 1
TOPK = 2
NBLK = NTOK * TOPK // P + NE - 1
GB = 4
NG = -(-NBLK // GB)
K_THR = NMASK * P
K_NUM = K_THR + NTOK // P
K_SLOT = K_NUM + NBLK
NCONST = K_SLOT + NBLK

F32 = mybir.dt.float32
F32R = mybir.dt.float32r
I32 = mybir.dt.int32
ALU = mybir.AluOpType
ACT = mybir.ActivationFunctionType
AX = mybir.AxisListType.X
FIRS = ((KS, 0), (KM, KS), (KL, KS + KM))


def perceiver_block(nc, x_in, ctx_in, ctxT_in, wg_in, wox_in, wqkv_in, wod_in, wffn_in, cols_in, rows_in,
                    masks_in, iota_in, bg_in, out):
    with ExitStack() as stack:
        def sb(name, shape, dt=F32, held=stack):
            return held.enter_context(nc.sbuf_tensor(name, shape, dt))

        def sem(name):
            return stack.enter_context(nc.semaphore(name))

        x = sb("x", [P, NT, D])
        xnT = sb("xnT", [P, DC, NTOK])
        early = sb("early", [P, 3, 2048])
        cols = sb("cols", [P, NCOL])
        rows = sb("rows", [P, NROW])
        consts = sb("consts", [P, NCONST])
        small = sb("small", [P, 1330])
        gate_r = sb("gate_r", [P, NT, 2 * NE], F32R)
        ident_r = sb("ident_r", [P, 24], F32R)
        expert_i = sb("expert_i", [P, NBLK], I32)
        with ExitStack() as before:
            ring = sb("ring", [P, 4, 8192], held=before)
            part = sb("part", [P, 3, 4, 512], held=before)
        xe = sb("xe", [P, 2, 2, DC, 512], F32R)
        wsp = sb("wsp", [P, 4, 2, 2048], F32R)
        xnr = sb("xnr", [P, 2, NT, D], F32R)
        hTs = sb("hTs", [P, 2, 2, 512], F32R)
        planes = sb("planes", [P, TOPK, NTOK])
        back = sb("back", [P, 2, NTOK], F32R)
        pick = sb("pick", [P, NT, 512], F32R)
        yes = sb("yes", [P, 2, 2, D], F32R)
        hraw = sb("hraw", [P, 2, 512])
        sil = sb("sil", [P, 512])
        iota = sb("iota", [P, 512])
        masks = consts[:, 0:NMASK * P].rearrange("p (m n) -> p m n", n=P)
        bank = [stack.enter_context(nc.psum_tensor(f"bank{i}", [P, 512], F32)) for i in range(8)]

        ident = masks[:, M_ID, :]
        ctxT = [ring[:, t, 0:4096].rearrange("p (b c k) -> p b c k", b=PAIR, c=DC) for t in range(NT)]
        ctx = [ring[:, t, 4096:8192].rearrange("p (b c d) -> p b c d", b=PAIR, c=TK // P) for t in range(NT)]
        wgT, wox, xn = part[:, 0], part[:, 1], part[:, 2]
        yT = early[:, 0, :].rearrange("p (c n) -> p c n", c=DC)
        probs_b = early[:, 1, 0:1024].rearrange("p (i n) -> p i n", i=2)
        probsT_b = early[:, 1, 1024:2048].rearrange("p (i n) -> p i n", i=2)
        oT_b = early[:, 2, 0:1024].rearrange("p (i n) -> p i n", i=2)
        o_b = early[:, 2, 1024:2048].rearrange("p (i n) -> p i n", i=2)
        bgrow, bgprod = o_b[:, 0, :], o_b[:, 1, :]
        sq_b = early[:, 2, 1024:2048].rearrange("p (i n) -> p i n", i=2)
        wqkv = ring[:, 0, 0:6144].rearrange("p (j c n) -> p j c n", j=3, c=DC)
        wod = ring[:, 0, 6144:8192].rearrange("p (h n) -> p h n", h=H)
        vP, kP, qP, kbP = (ring[:, 1, 2048 * i:2048 * i + 2048].rearrange("p (h n) -> p h n", h=H) for i in range(4))
        plane = [vP, kP, qP]
        mt, lt, tt, att = (ring[:, 2, 2048 * i:2048 * i + 2048].rearrange("p (h n) -> p h n", h=H) for i in range(4))
        tm, yy, bv = (ring[:, 3, 2048 * i:2048 * i + 2048].rearrange("p (h n) -> p h n", h=H) for i in range(3))
        sq2 = ring[:, 3, 6144:7168].rearrange("p (i n) -> p i n", i=2)
        ct = back[0:24]
        diag = rows[:, R_BO:R_BO + 512].rearrange("p (i n) -> p i n", i=4)
        branch = [part[:, i] for i in range(3)]

        at = [0]

        def take(n):
            at[0] += n
            assert at[0] <= 1330
            return small[:, at[0] - n:at[0]]
        stats = take(NT * 6).rearrange("p (t n) -> p t n", t=NT)
        mv = take(NT * 2).rearrange("p (t n) -> p t n", t=NT)
        rs_in, rs_y, rs_a, rs_b = take(32), take(32), take(32), take(32)
        half = take(32)
        ones = take(2)
        mx, mc, nb, c0s, sm, rsm = (take(NT) for _ in range(6))
        lg = take(NT * 24).rearrange("p (t n) -> p t n", t=NT)
        gt = take(NT * 20).rearrange("p (t n) -> p t n", t=NT)
        gtm = take(NT * H)
        beta = take(NT * H).rearrange("p (t h) -> p t h", t=NT)
        itemp, epsc, epsm = take(H), take(H), take(H)
        ktr = take(32)
        cc = take(NT * 24).rearrange("p (t n) -> p t n", t=NT)
        orr = take(H * NT)
        rl = take(NT * NE).rearrange("p (t n) -> p t n", t=NT)
        prio = take(NE)
        hot = [take(NT * NE).rearrange("p (t n) -> p t n", t=NT) for _ in range(TOPK)]
        sel, base = (take(NT * NE).rearrange("p (t n) -> p t n", t=NT) for _ in range(2))
        gated = take(NT * NE).rearrange("p (t n) -> p t n", t=NT)
        cnt, nblk, end, start_b = (take(NE) for _ in range(4))
        over = take(NE * NT).rearrange("p (e n) -> p e n", e=NE)
        slot = take(TOPK * NT).rearrange("p (k t) -> p k t", k=TOPK)
        slotg = take(NG * TOPK * NT).rearrange("p (g k t) -> p g k t", g=NG, k=TOPK)
        owner = take(NBLK * NE).rearrange("p (j e) -> p j e", j=NBLK)
        expert = take(NBLK)
        gg = take(2 * GB * 2 * NE).rearrange("p (i n) -> p i n", i=2)
        gw2 = take(2 * NE).rearrange("p (i n) -> p i n", i=2)
        gw = take(NBLK)
        rw1, rw2 = (take(NT * NE).rearrange("p (t n) -> p t n", t=NT) for _ in range(2))
        rq = take(NT)

        ld_x = [sem(f"ld_x{t}") for t in range(NT)]
        ld_masks, ld_cols, ld_rows, ld_wg, ld_wox, ld_wqkv, ld_wod = (
            sem(n) for n in ("ld_masks", "ld_cols", "ld_rows", "ld_wg", "ld_wox", "ld_wqkv", "ld_wod"))
        ld_ctxT = [sem(f"ld_ctxT{t}") for t in range(NT)]
        ld_ctx = [sem(f"ld_ctx{t}") for t in range(NT)]
        ld_bg = sem("ld_bg")
        ld_raw = [sem(f"ld_raw{i}") for i in range(3)]
        ld_iota = sem("ld_iota")
        stored = sem("stored")
        dve_step, act_step, pool_step = sem("dve_step"), sem("act_step"), sem("pool_step")
        names = ("pow_wanted", "pow_done", "pool_consts", "xn_ready", "xT_done", "xnT_ready", "y_done", "yT_ready",
                 "s_done", "bias_ready", "exp_done", "pT_done", "pT_ready",
                 "oT_done", "oT_ready", "proj_done", "x1_done", "gate_done", "gate_read", "gate_exp_wanted",
                 "gate_exp_done", "qkv_done", "lag0_done", "conv_done", "silu_done", "sq_done", "sumsq_done",
                 "vt_done", "bv_ready", "cc_ready", "ct_done", "ct_ready", "kb_done", "kb_ready", "kk_done",
                 "mt_ready", "at_done", "at_ready", "tt1_ready", "t1_done", "t1_ready", "lt_ready", "yl_done",
                 "yl_ready", "z_done", "zt_done", "t_upd", "tt_upd", "u_done", "u_ready", "o_done", "d_ready",
                 "bc_done", "weighted", "o_ready", "osq_ready", "osum_done", "m_done", "x2_done", "rout_done",
                 "rout_read", "rexp_wanted", "rexp_done", "h1_done", "h3_done", "fsilu_done", "wod_scaled",
                 "w_hi", "w_lo", "xr_hi", "xr_lo", "sel_ready", "pos_done", "expert_ready", "slot_ready",
                 "plane_done", "plane_ready", "prod_ready", "sh_hi", "sh_lo", "sd_done", "pick_ready", "gx_done",
                 "gx_ready", "hr_done", "hT_hi", "hT_lo", "ye_done", "gw_ready", "ye_hi", "ye_lo", "back_ready",
                 "c_done", "acc_done", "c0_ready", "identr_ready", "rs_ready", "pv_done", "o_kept", "ct_lo", "fir_even", "fir_odd", "firpe_kept", "firpe_added", "diag_ready", "diag_used")
        S = {n: sem(n) for n in names}
        for_count = {}

        def signal(ins, s):
            for_count[s.name] = for_count.get(s.name, 0) + 1
            ins.then_inc(s, 1)
            return for_count[s.name]

        def after(eng, ins, s):
            eng.wait_ge(s, signal(ins, s))

        PIECES = [("shared", w, e) for e in range(NSH) for w in range(3)]
        for j in range(NBLK + 1):
            if j < NBLK:
                PIECES += [("routed", 0, j), ("routed", 1, j)]
            if j >= 1:
                PIECES += [("routed", 2, j - 1)]
        number = {p: i for i, p in enumerate(PIECES)}

        def piece(p):
            return wsp[:, (number[p] + 2) % 4].rearrange("p i (c n) -> p i c n", c=DC)

        def wait_piece_free(eng, i):
            kind, which, n = PIECES[i]
            if kind == "shared":
                s, v = (S["h1_done"], FC * (n + 1)), (S["h3_done"], FC * (n + 1))
                s, v = (s, v)[which] if which < 2 else (S["sd_done"], n + 1)
            else:
                s, v = ((S["h1_done"], NSH * FC + n + 1), (S["h3_done"], NSH * FC + n + 1),
                        (S["ye_done"], n + 1))[which]
            eng.wait_ge(s, v)

        def fir_diags(n):
            steps = H * len(LEVELS)
            return range(H * LAGS_PE * n // steps, H * LAGS_PE * (n + 1) // steps)

        experts = {}

        def expert_of(eng, j):
            if j not in experts:
                experts[j] = eng.value_load(expert_i[0:1, j:j + 1], min_val=0, max_val=NE - 1)
            return experts[j]

        block = stack.enter_context(nc.Block())

        @block.sync
        def _(sp):
            sp.dma_start(x[:, 0], x_in[0]).then_inc(ld_x[0], 16)
            sp.dma_start(consts[:], masks_in).then_inc(ld_masks, 16)
            for t in range(1, NT):
                sp.dma_start(x[:, t], x_in[t]).then_inc(ld_x[t], 16)
            sp.dma_start(wgT, wg_in).then_inc(ld_wg, 16)
            sp.dma_start(cols[:], cols_in).then_inc(ld_cols, 16)
            sp.dma_start(rows[:], rows_in).then_inc(ld_rows, 16)
            sp.dma_start(bgrow, bg_in).then_inc(ld_bg, 16)
            for t in range(NT):
                sp.dma_start(ring[:, t, 0:4096], ctxT_in[t]).then_inc(ld_ctxT[t], 16)
                sp.dma_start(ring[:, t, 4096:8192], ctx_in[t]).then_inc(ld_ctx[t], 16)
                if t == 0:
                    sp.dma_start(wox, wox_in).then_inc(ld_wox, 16)
            sp.wait_ge(S["oT_done"], 1)
            sp.dma_start(ring[:, 0, 0:6144], wqkv_in).then_inc(ld_wqkv, 16)
            sp.dma_start(ring[:, 0, 6144:8192], wod_in).then_inc(ld_wod, 16)
            sp.wait_ge(S["sumsq_done"], 2 * H)
            sp.wait_ge(S["proj_done"], NT)
            for i, (kind, which, n) in enumerate(PIECES):
                if i >= 3:
                    sp.wait_ge(S["w_hi"], i - 2)
                    sp.wait_ge(S["w_lo"], i - 2)
                if kind == "shared":
                    src = wffn_in[NE + n, :, 2048 * which:2048 * (which + 1)]
                else:
                    if i == 2 * NSH + NSH:
                        sp.wait_ge(S["expert_ready"], 1)
                    src = wffn_in[bass.ds(expert_of(sp, n), 1), :, 2048 * which:2048 * (which + 1)]
                    src = src.rearrange("o p n -> (o p) n")
                sp.dma_start(early[:, i % 3, :], src).then_inc(ld_raw[i % 3], 16)
                if i == 3:
                    sp.wait_ge(S["xr_lo"], 2 * NT)
                    sp.dma_start(iota[:], iota_in).then_inc(ld_iota, 16)
            for t in range(NT):
                sp.wait_ge(S["acc_done"], t + 1)
                sp.dma_start(out[t], x[:, t]).then_inc(stored, 16)
            sp.wait_ge(stored, 16 * NT)

        @block.gpsimd
        def _(pool):
            pool.memset(half[:], -0.5).then_inc(S["pool_consts"], 1)
            pool.memset(ones[:], 1.0).then_inc(S["pool_consts"], 1)
            pool.wait_ge(S["pool_consts"], 2)

            def power(n, lo, width):
                pool.wait_ge(S["pow_wanted"], n)
                pool.tensor_tensor(rs_y[:, lo:lo + width], rs_in[:, lo:lo + width], half[:, 0:width],
                                   ALU.pow).then_inc(S["pow_done"], 1)
            for t in range(2 * NT):
                power(t + 1, t % NT, 1)
            power(2 * NT + 1, 0, 32)
            for l in range(len(LEVELS)):
                for h in range(H):
                    if l == 0:
                        pool.wait_ge(S["mt_ready"], h + 1)
                    else:
                        pool.wait_ge(S["yl_done"], H * (l - 1) + h + 1)
                    m = masks[:, M_L1 + 1 + l, :].unsqueeze(1).broadcast_to([P, NT, P])
                    pool.tensor_tensor(lt[:, h].rearrange("p (t n) -> p t n", t=NT),
                                       mt[:, h].rearrange("p (t n) -> p t n", t=NT), m,
                                       ALU.mult).then_inc(S["lt_ready"], 1)
            for h in range(H):
                pool.wait_ge(S["weighted"], NPROB * (h + 1))
                after(pool, pool.tensor_tensor(branch[0][:, h], branch[0][:, h], branch[1][:, h], ALU.add), pool_step)
                after(pool, pool.tensor_tensor(branch[2][:, h], branch[2][:, h], tm[:, h], ALU.add), pool_step)
                after(pool, pool.tensor_tensor(branch[0][:, h], branch[0][:, h], branch[2][:, h], ALU.add), pool_step)
                pool.tensor_tensor(branch[0][:, h], branch[0][:, h], vP[:, h], ALU.add).then_inc(S["o_ready"], 1)
            power(2 * NT + 2, 0, 16)
            for t in range(NT):
                power(2 * NT + 3 + t, t, 1)

        @block.tensor
        def _(pe):
            def transpose_tile(layer, t):
                pe.wait_ge(S["xn_ready"], layer * NT + t + 1)
                if layer == 0 and t == 0:
                    pe.wait_ge(ld_masks, 16)
                if t >= 2:
                    pe.wait_ge(S["xnT_ready"], layer * NT + t - 1)
                for c in range(DC):
                    last = pe.transpose(bank[t % 2][:, c * P:(c + 1) * P], xn[:, t, c * P:(c + 1) * P], ident)
                last.then_inc(S["xT_done"], 1)

            for t in range(NT):
                transpose_tile(0, t)
            pe.wait_ge(ld_wg, 16)
            pe.wait_ge(ld_cols, 16)
            for t in range(NT):
                pe.wait_ge(S["xnT_ready"], t + 1)
                if t >= 2:
                    pe.wait_ge(S["yT_ready"], t - 1)
                for c in range(DC):
                    for e in range(DC):
                        last = pe.matmul(bank[2 + t % 2][:, c * P:(c + 1) * P], wgT[:, e, c * P:(c + 1) * P],
                                         xnT[:, e, t * P:(t + 1) * P], start=(e == 0), stop=(e == DC - 1))
                last.then_inc(S["y_done"], 1)
            def scores(t):
                pe.wait_ge(S["yT_ready"], t + 1)
                pe.wait_ge(ld_ctxT[t], 16)
                if t >= 2:
                    pe.wait_ge(S["exp_done"], t - 1)
                for c in range(DC):
                    for b in range(PAIR):
                        last = pe.matmul(bank[5 + t % 2][b * L:(b + 1) * L, :],
                                         yT[:, c, t * P + b * L:t * P + (b + 1) * L], ctxT[t][:, b, c, :],
                                         start=(c == 0), stop=(c == DC - 1))
                last.then_inc(S["s_done"], 1)

            def values(t):
                pe.wait_ge(S["exp_done"], t + 1)
                if t >= 1:
                    pe.wait_ge(S["pT_ready"], t)
                for k in range(TK // P):
                    last = pe.transpose(bank[7][:, k * P:(k + 1) * P], probs_b[:, t % 2, k * P:(k + 1) * P], ident)
                last.then_inc(S["pT_done"], 1)
                pe.wait_ge(S["pT_ready"], t + 1)
                pe.wait_ge(ld_ctx[t], 16)
                if t < 2:
                    pe.wait_ge(S["xnT_ready"], NT)
                else:
                    pe.wait_ge(S["o_kept"], t - 1)
                for k in range(TK // P):
                    for b in range(PAIR):
                        last = pe.matmul(bank[t % 2][b * L:(b + 1) * L, :],
                                         probsT_b[:, t % 2, k * P + b * L:k * P + (b + 1) * L], ctx[t][:, b, k, :],
                                         start=(k == 0), stop=(k == TK // P - 1))
                last.then_inc(S["pv_done"], 1)

            def turn_values(t):
                pe.wait_ge(S["o_kept"], t + 1)
                if t >= 1:
                    pe.wait_ge(S["oT_ready"], t)
                for c in range(DC):
                    last = pe.transpose(bank[4][:, c * P:(c + 1) * P], o_b[:, t % 2, c * P:(c + 1) * P], ident)
                last.then_inc(S["oT_done"], 1)

            def project(t):
                pe.wait_ge(S["oT_ready"], t + 1)
                pe.wait_ge(ld_wox, 16)
                if t < 2:
                    pe.wait_ge(S["yT_ready"], NT)
                else:
                    pe.wait_ge(S["x1_done"], t - 1)
                for c in range(DC):
                    last = pe.matmul(bank[2 + t % 2][:, :], oT_b[:, t % 2, c * P:(c + 1) * P], wox[:, c, :],
                                     start=(c == 0), stop=(c == DC - 1))
                last.then_inc(S["proj_done"], 1)

            scores(0)
            scores(1)
            for t in range(NT):
                values(t)
                if t + 2 < NT:
                    scores(t + 2)
                if t >= 1:
                    project(t - 1)
                turn_values(t)
            project(NT - 1)

            pe.wait_ge(S["o_kept"], NT)
            for t in range(NT):
                transpose_tile(1, t)
            pe.wait_ge(S["xnT_ready"], 2 * NT)

            def gate_logits():
                pe.wait_ge(S["x1_done"], NT)
                for t in range(NT):
                    for c in range(DC):
                        last = pe.matmul(bank[3][:, 24 * t:24 * (t + 1)], xnT[:, c, t * P:(t + 1) * P],
                                         cols[:, C_GATE + 24 * c:C_GATE + 24 * (c + 1)],
                                         start=(c == 0), stop=(c == DC - 1))
                    last.then_inc(S["gate_done"], 1)

            pe.wait_ge(ld_wqkv, 16)

            def sumsq(i):
                pe.wait_ge(S["sq_done"], i + 1)
                for t in range(NT):
                    last = pe.matmul(bank[4][:, 256 + NT * i + t:257 + NT * i + t], sq_b[:, i % 2, t * P:(t + 1) * P],
                                     ones[:, 0:1], start=True, stop=True)
                last.then_inc(S["sumsq_done"], 1)

            for g in range(3 * H):
                j, h = g // H, g % H
                if g >= 3:
                    pe.wait_ge(S["conv_done"], g - 2)
                for c in range(DC):
                    last = pe.matmul(bank[5 + g % 3][:, :], wqkv[:, j, c, h * P:(h + 1) * P], xnT[:, c, :],
                                     start=(c == 0), stop=(c == DC - 1))
                last.then_inc(S["qkv_done"], 1)
                if g == H:
                    gate_logits()
                if g >= H + 2:
                    sumsq(g - H - 2)
            for h in range(H):
                pe.wait_ge(S["silu_done"], h + 1)
                if h >= 2:
                    pe.wait_ge(S["bv_ready"], h - 1)
                for t in range(NT):
                    last = pe.transpose(bank[h % 2][:, t * P:(t + 1) * P], vP[:, h, t * P:(t + 1) * P], ident)
                last.then_inc(S["vt_done"], 1)
            sumsq(2 * H - 2)
            sumsq(2 * H - 1)
            pe.wait_ge(S["cc_ready"], 1)
            for t in range(NT):
                last = pe.transpose(bank[3][0:24, t * P:(t + 1) * P], cc[:, t, :], ident)
            last.then_inc(S["ct_done"], 1)
            pe.wait_ge(S["ct_lo"], 1)

            def spread(dst, row):
                pick_row = ident_r[0:24, row:row + 1].broadcast_to([24, P])
                pe.wait_ge(S["identr_ready"], 1)
                pe.matmul(dst, pick_row, ct[:, 0, :], start=True, stop=False)
                return pe.matmul(dst, pick_row, ct[:, 1, :], start=False, stop=True)

            for h in range(H):
                pe.wait_ge(S["conv_done"], 3 * H)
                if h >= 3:
                    pe.wait_ge(S["kb_ready"], h - 2)
                spread(bank[5 + h % 3][:, :], H * NPROB + h).then_inc(S["kb_done"], 1)
            pe.wait_ge(S["bv_ready"], H)
            for h in range(H):
                pe.wait_ge(S["kb_ready"], h + 1)
                for t in range(NT):
                    s = slice(t * P, (t + 1) * P)
                    last = pe.matmul(bank[h][:, s], kP[:, h, s], kbP[:, h, s], start=True, stop=True)
                last.then_inc(S["kk_done"], 1)
            pe.wait_ge(S["kb_ready"], H)
            for h in range(H):
                for t in range(NT):
                    s = slice(t * P, (t + 1) * P)
                    last = pe.matmul(bank[4 + h][:, s], kP[:, h, s], qP[:, h, s], start=True, stop=True)
                last.then_inc(S["at_done"], 1)
            for h in range(H):
                pe.wait_ge(S["tt1_ready"], h + 1)
                for t in range(NT):
                    s = slice(t * P, (t + 1) * P)
                    last = pe.transpose(bank[h][:, s], tt[:, h, s], ident)
                last.then_inc(S["t1_done"], 1)
            pe.wait_ge(S["at_ready"], H)
            for l in range(len(LEVELS)):
                final = l == len(LEVELS) - 1
                for h in range(H):
                    pe.wait_ge(S["lt_ready"], H * l + h + 1)
                    if l == 0:
                        pe.wait_ge(S["t1_ready"], h + 1)
                    else:
                        pe.wait_ge(S["t_upd"], H * (l - 1) + h + 1)
                    n = H * l + h
                    if n >= 3:
                        pe.wait_ge(S["yl_ready"], n - 2)
                    for t in range(NT):
                        s = slice(t * P, (t + 1) * P)
                        last = pe.matmul(bank[n % 3][:, s], lt[:, h, s], tm[:, h, s], start=True, stop=True)
                    last.then_inc(S["yl_done"], 1)
                for h in range(H):
                    n = H * l + h
                    pe.wait_ge(S["yl_ready"], n + 1)
                    if n >= 2:
                        pe.wait_ge(S["tt_upd"], n - 1)
                    else:
                        pe.wait_ge(S["t1_ready"], H)
                    for t in range(NT):
                        s = slice(t * P, (t + 1) * P)
                        last = pe.matmul(bank[4 + 2 * (h % 2)][:, s], yy[:, h, s], tt[:, h, s], start=True, stop=True)
                    last.then_inc(S["zt_done"], 1)
                    if not final:
                        for t in range(NT):
                            s = slice(t * P, (t + 1) * P)
                            last = pe.matmul(bank[3 + 2 * (h % 2)][:, s], tt[:, h, s], yy[:, h, s],
                                             start=True, stop=True)
                        last.then_inc(S["z_done"], 1)
                    for k in fir_diags(n):
                        hh, lag = k // LAGS_PE, k % LAGS_PE + 1
                        if lag == 1 and hh > 0:
                            pe.wait_ge(S["firpe_kept"], hh)
                        pe.wait_ge(S["diag_ready"], k + 1)
                        d = bank[7][:, :].rearrange("p (b l) -> p b l", b=B)[:, :, lag:L]
                        v = vP[:, hh].rearrange("p (b l) -> p b l", b=B)[:, :, 0:L - lag]
                        last = pe.matmul(d, diag[:, k % 4, :], v, start=(lag == 1), stop=(lag == LAGS_PE))
                        last.then_inc(S["diag_used"], 1)
            for h in range(H):
                pe.wait_ge(S["tt_upd"], H * (len(LEVELS) - 1) + h + 1)
                for t in range(NT):
                    s = slice(t * P, (t + 1) * P)
                    last = pe.matmul(bank[h][:, s], tt[:, h, s], bv[:, h, s], start=True, stop=True)
                last.then_inc(S["u_done"], 1)
            pe.wait_ge(S["firpe_kept"], H)
            for h in range(H):
                pe.wait_ge(S["u_ready"], h + 1)
                for t in range(NT):
                    s = slice(t * P, (t + 1) * P)
                    last = pe.matmul(bank[4 + h][:, s], yy[:, h, s], att[:, h, s], start=True, stop=True)
                last.then_inc(S["o_done"], 1)
            for n in range(H * NPROB):
                if n >= 4:
                    pe.wait_ge(S["weighted"], n - 3)
                else:
                    pe.wait_ge(S["u_ready"], H)
                spread(bank[n % 4][:, :], n).then_inc(S["bc_done"], 1)
            pe.wait_ge(S["d_ready"], H)
            for h in range(H):
                pe.wait_ge(S["osq_ready"], h + 1)
                for t in range(NT):
                    last = pe.matmul(bank[7][:, H * t + h:H * t + h + 1], sq2[:, h % 2, t * P:(t + 1) * P],
                                     ones[:, 0:1], start=True, stop=True)
                last.then_inc(S["osum_done"], 1)
            pe.wait_ge(S["wod_scaled"], H)
            for n in range(NT * H):
                t, h = n // H, n % H
                if n >= 4:
                    pe.wait_ge(S["x2_done"], n - 3)
                pe.matmul(bank[3 + n % 4][:, :], branch[0][:, h, t * P:(t + 1) * P], wod[:, h, :],
                          start=True, stop=True).then_inc(S["m_done"], 1)

            pe.wait_ge(S["weighted"], H * NPROB)
            for t in range(NT):
                transpose_tile(2, t)
            pe.wait_ge(S["x2_done"], NT * H)
            for t in range(NT):
                pe.wait_ge(S["xnT_ready"], 2 * NT + t + 1)
                for c in range(DC):
                    last = pe.matmul(bank[4][:, NE * t:NE * (t + 1)], xnT[:, c, t * P:(t + 1) * P],
                                     cols[:, C_ROUT + NE * c:C_ROUT + NE * (c + 1)], start=(c == 0), stop=(c == DC - 1))
                last.then_inc(S["rout_done"], 1)

            def products(dst, terms, first=True, final=True):
                for n, (lhsT, rhs) in enumerate(terms):
                    last = pe.matmul(dst, lhsT, rhs, start=(first and n == 0), stop=(final and n == len(terms) - 1))
                return last

            def wait_piece(p):
                pe.wait_ge(S["w_hi"], number[p] + 1)
                pe.wait_ge(S["w_lo"], number[p] + 1)

            def shared_up(e, f):
                n = e * FC + f
                if n >= 2:
                    pe.wait_ge(S["prod_ready"], n - 1)
                for j, name in ((0, "h1_done"), (1, "h3_done")):
                    wait_piece(("shared", j, e))
                    w = piece(("shared", j, e))
                    fs = slice(f * P, (f + 1) * P)
                    products(bank[2 * (n % 2) + j][:, :],
                             [(w[:, wi, c, fs], xe[:, 0, xi, c, :]) for wi, xi in ((0, 0), (0, 1), (1, 0))
                              for c in range(DC)]).then_inc(S[name], 1)

            def shared_down(e):
                wait_piece(("shared", 2, e))
                w = piece(("shared", 2, e))
                pe.wait_ge(S["sh_lo"], FC * (e + 1))
                for t in range(NT):
                    ts = slice(t * P, (t + 1) * P)
                    last = products(bank[4 + t][:, :],
                                    [(xe[:, 1, hi, f, ts], w[:, wi, f, :]) for f in range(FC)
                                     for hi, wi in ((0, 0), (0, 1), (1, 0))], first=(e == 0), final=False)
                last.then_inc(S["sd_done"], 1)

            pe.wait_ge(S["xr_lo"], 2 * NT)
            shared_up(0, 0)
            shared_up(0, 1)
            pe.wait_ge(S["sel_ready"], 1)
            anyone = ones[:, 0:1].broadcast_to([P, P])
            for t in range(NT):
                products(bank[5][:, NE * t:NE * (t + 1)],
                         [(masks[:, M_BEFORE, :], sel[:, t, :])] + [(anyone, sel[:, i, :]) for i in range(t)])
            products(bank[5][:, NE * NT:NE * (NT + 1)],
                     [(anyone, sel[:, i, :]) for i in range(NT)]).then_inc(S["pos_done"], 1)
            shared_up(0, 2)
            shared_up(0, 3)
            pe.wait_ge(S["slot_ready"], 1)
            for k in range(TOPK):
                for t in range(NT):
                    last = pe.matmul(bank[6 + k][:, t * P:(t + 1) * P], slot[:, k, t:t + 1].broadcast_to([P, P]), ident,
                                     start=True, stop=True)
                last.then_inc(S["plane_done"], 1)
            pe.wait_ge(S["plane_ready"], TOPK)
            shared_down(0)
            for f in range(FC):
                if f == 0:
                    pe.wait_ge(S["sd_done"], 1)
                shared_up(1, f)
            shared_down(1)

            def gather(g):
                blocks = min(GB, NBLK - g * GB)
                width = blocks * P
                pe.wait_ge(S["pick_ready"], g + 1)
                if g == 0:
                    pe.wait_ge(S["prod_ready"], NSH * FC)
                for u in range(2 * DC):
                    c, i = u // 2, u % 2
                    if u >= 2:
                        pe.wait_ge(S["gx_ready"], (2 * DC + 1) * g + u - 1)
                    elif g > 0:
                        pe.wait_ge(*((S["hT_lo"], GB * g - 2 + 1), (S["ye_lo"], GB * g - 2 + 1))[u])
                    products(bank[2 + i][:, 0:width],
                             [(xnr[:, i, t, c * P:(c + 1) * P], pick[:, t, 0:width])
                              for t in range(NT)]).then_inc(S["gx_done"], 1)
                pe.wait_ge(S["gx_ready"], (2 * DC + 1) * g + 2 * DC - 1)
                for b in range(blocks):
                    last = products(bank[2][:, 2 * NE * b:2 * NE * (b + 1)],
                                    [(pick[:, t, b * P:(b + 1) * P], gate_r[:, t, :]) for t in range(NT)])
                last.then_inc(S["gx_done"], 1)

            def routed_up(j, which, name):
                wait_piece(("routed", which, j))
                w = piece(("routed", which, j))
                bs = slice((j % GB) * P, (j % GB + 1) * P)
                if which == 0:
                    pe.wait_ge(S["fsilu_done"], NSH * FC + j)
                    if j % GB == 0:
                        pe.wait_ge(S["gx_ready"], (2 * DC + 1) * (j // GB + 1))
                else:
                    pe.wait_ge(S["prod_ready"], NSH * FC + j)
                products(bank[which][:, :],
                         [(xe[:, (j // GB) % 2, xi, c, bs], w[:, wi, c, :]) for c in range(DC)
                          for xi, wi in ((0, 0), (0, 1), (1, 0))]).then_inc(S[name], 1)

            def turn(j):
                pe.wait_ge(S["prod_ready"], NSH * FC + j + 1)
                if j >= 1:
                    pe.wait_ge(S["hT_lo"], j)
                if (j + 1) % GB == 0:
                    pe.wait_ge(S["gx_ready"], (2 * DC + 1) * ((j + 1) // GB + 1))
                for f in range(FC):
                    last = pe.transpose(bank[2][:, f * P:(f + 1) * P], hraw[:, j % 2, f * P:(f + 1) * P], ident)
                last.then_inc(S["hr_done"], 1)

            def routed_down(j):
                wait_piece(("routed", 2, j))
                w = piece(("routed", 2, j))
                pe.wait_ge(S["hT_lo"], j + 1)
                if j >= 1:
                    pe.wait_ge(S["ye_lo"], j)
                products(bank[3][:, :],
                         [(hTs[:, j % 2, hi, f * P:(f + 1) * P], w[:, wi, f, :]) for f in range(FC)
                          for hi, wi in ((0, 0), (0, 1), (1, 0))]).then_inc(S["ye_done"], 1)

            def give_back(j):
                pe.wait_ge(S["ye_lo"], j + 1)
                pe.wait_ge(S["back_ready"], j + 1)
                for t in range(NT):
                    last = products(bank[4 + t][:, :],
                                    [(back[:, j % 2, t * P:(t + 1) * P], yes[:, j % 2, i, :]) for i in range(2)],
                                    first=False, final=(j == NBLK - 1))
                last.then_inc(S["c_done"], 1)

            gather(0)
            for j in range(NBLK + 2):
                if j < NBLK:
                    routed_up(j, 0, "h1_done")
                if 1 <= j <= NBLK:
                    turn(j - 1)
                if j < NBLK:
                    routed_up(j, 1, "h3_done")
                if 1 <= j <= NBLK:
                    routed_down(j - 1)
                if j >= 2:
                    give_back(j - 2)
                if (j + 1) % GB == 0 and j + 1 < NBLK:
                    gather((j + 1) // GB)

        @block.scalar
        def _(act):
            def store_xnT(layer, t):
                act.wait_ge(S["xT_done"], layer * NT + t + 1)
                if layer == 1:
                    act.wait_ge(S["y_done"], NT)
                if layer == 2:
                    act.wait_ge(S["qkv_done"], 3 * H)
                act.activation(xnT[:, :, t * P:(t + 1) * P], bank[t % 2][:, :].rearrange("p (c n) -> p c n", c=DC),
                               ACT.Copy).then_inc(S["xnT_ready"], 1)

            for t in range(NT):
                store_xnT(0, t)

            def exponentials(t):
                act.wait_ge(S["bias_ready"], t + 1)
                if t >= 2:
                    act.wait_ge(S["pT_done"], t - 1)
                act.activation(probs_b[:, t % 2, :], bank[5 + t % 2][:, :], ACT.Exp, bias=nb[:, t:t + 1],
                               accum_out=sm[:, t:t + 1]).then_inc(S["exp_done"], 1)

            exponentials(0)
            for t in range(NT):
                if t + 1 < NT:
                    exponentials(t + 1)
                act.wait_ge(S["pT_done"], t + 1)
                if t >= 2:
                    act.wait_ge(S["pv_done"], t - 1)
                act.activation(probsT_b[:, t % 2, :], bank[7][:, :], ACT.Copy).then_inc(S["pT_ready"], 1)
                act.wait_ge(S["pv_done"], t + 1)
                act.wait_ge(S["rs_ready"], t + 1)
                if t >= 2:
                    act.wait_ge(S["oT_done"], t - 1)
                act.activation(o_b[:, t % 2, :], bank[t % 2][:, :], ACT.Copy,
                               scale=rsm[:, t:t + 1]).then_inc(S["o_kept"], 1)
            for t in range(NT):
                store_xnT(1, t)

            def gate_exp(n):
                act.wait_ge(S["gate_exp_wanted"], n)
                if n == 1:
                    after(act, act.activation(itemp, rows[:, R_TEMP:R_TEMP + H], ACT.Exp, scale=-1.0), act_step)
                    act.activation(beta, lg[:, :, 20:24], ACT.Exp, scale=-1.0).then_inc(S["gate_exp_done"], 1)
                else:
                    act.activation(gt, gt, ACT.Exp).then_inc(S["gate_exp_done"], 1)

            def lag0(g):
                act.wait_ge(S["qkv_done"], g + 1)
                if g == 0:
                    act.wait_ge(S["oT_done"], NT)
                j, h = g // H, g % H
                w = C_CONV + (j * H + h) * KC + KC - 1
                act.activation(plane[j][:, h], bank[5 + g % 3][:, :], ACT.Copy,
                               scale=cols[:, w:w + 1]).then_inc(S["lag0_done"], 1)

            def silu(g):
                j, h = g // H, g % H
                act.wait_ge(S["conv_done"], g + 1)
                act.activation(plane[j][:, h], plane[j][:, h], ACT.Silu).then_inc(S["silu_done"], 1)
                if j > 0:
                    i = g - H
                    act.wait_ge(S["silu_done"], g + 1)
                    if i >= 2:
                        act.wait_ge(S["sumsq_done"], i - 1)
                    act.activation(sq_b[:, i % 2, :], plane[j][:, h], ACT.Square).then_inc(S["sq_done"], 1)

            lag0(0)
            for g in range(1, 3 * H):
                lag0(g)
                silu(g - 1)
                if g in (H + 2, H + 3):
                    gate_exp(g - H - 1)
            silu(3 * H - 1)
            act.wait_ge(S["ct_done"], 1)
            act.activation(ct[:, 0, :], bank[3][0:24, :], ACT.Copy).then_inc(S["ct_ready"], 1)
            for h in range(H):
                act.wait_ge(S["t1_done"], h + 1)
                act.activation(tm[:, h], bank[h][:, :], ACT.Copy).then_inc(S["t1_ready"], 1)
            for l in range(len(LEVELS)):
                for h in range(H):
                    n = H * l + h
                    act.wait_ge(S["yl_done"], n + 1)
                    if l >= 1:
                        act.wait_ge(S["z_done"], n - H + 1)
                    act.activation(yy[:, h], bank[n % 3][:, :], ACT.Copy).then_inc(S["yl_ready"], 1)
                    for k in fir_diags(n):
                        hh, lag = k // LAGS_PE, k % LAGS_PE + 1
                        w = C_FIR + hh * (KS + KM + KL) + KS + KM + KL - 1 - lag
                        if k >= 4:
                            act.wait_ge(S["diag_used"], k - 3)
                        act.activation(diag[:, k % 4, :], ident, ACT.Copy,
                                       scale=cols[:, w:w + 1]).then_inc(S["diag_ready"], 1)
                        if lag == LAGS_PE:
                            act.wait_ge(S["diag_used"], k + 1)
                            act.wait_ge(S["kk_done"], H)
                            act.activation(kbP[:, hh], bank[7][:, :], ACT.Copy).then_inc(S["firpe_kept"], 1)
            for h in range(H):
                act.wait_ge(S["u_done"], h + 1)
                act.wait_ge(S["zt_done"], H * len(LEVELS))
                act.activation(yy[:, h], bank[h][:, :], ACT.Copy).then_inc(S["u_ready"], 1)
            for h in range(H):
                act.wait_ge(S["o_done"], h + 1)
                act.activation(tm[:, h], bank[4 + h][:, :], ACT.Copy).then_inc(S["d_ready"], 1)
            for h in range(H):
                act.wait_ge(S["o_ready"], h + 1)
                if h >= 2:
                    act.wait_ge(S["osum_done"], h - 1)
                act.activation(sq2[:, h % 2, :], branch[0][:, h], ACT.Square).then_inc(S["osq_ready"], 1)

            def high(p):
                i = number[p]
                act.wait_ge(ld_raw[i % 3], 16 * (i // 3 + 1))
                if i >= 4:
                    wait_piece_free(act, i - 4)
                elif i == 0:
                    act.wait_ge(S["o_done"], H)
                act.activation(wsp[:, (i + 2) % 4, 0, :], early[:, i % 3, :], ACT.Copy).then_inc(S["w_hi"], 1)

            high(PIECES[0])
            high(PIECES[1])
            act.wait_ge(S["osum_done"], H)
            act.wait_ge(S["m_done"], NT * H)
            for t in range(NT):
                act.wait_ge(S["xn_ready"], 2 * NT + t + 1)
                act.activation(xnr[:, 0, t, :], xn[:, t, :], ACT.Copy).then_inc(S["xr_hi"], 1)
                store_xnT(2, t)
                act.wait_ge(S["xnT_ready"], 2 * NT + t + 1)
                act.activation(xe[:, 0, 0, :, t * P:(t + 1) * P], xnT[:, :, t * P:(t + 1) * P],
                               ACT.Copy).then_inc(S["xr_hi"], 1)
            high(PIECES[2])
            high(PIECES[3])
            act.wait_ge(S["rexp_wanted"], 1)
            act.activation(rl, rl, ACT.Exp).then_inc(S["rexp_done"], 1)

            def silu_of(n, b):
                act.wait_ge(S["h1_done"], n + 1)
                if n >= 1:
                    act.wait_ge(S["prod_ready"], n)
                else:
                    act.wait_ge(S["xr_lo"], 2 * NT)
                act.activation(sil[:], bank[b][:, :], ACT.Silu).then_inc(S["fsilu_done"], 1)

            for e in range(NSH):
                for f in range(FC):
                    n = e * FC + f
                    silu_of(n, 2 * (n % 2))
                    act.wait_ge(S["prod_ready"], n + 1)
                    if e == 1:
                        act.wait_ge(S["sd_done"], 1)
                    act.activation(xe[:, 1, 0, f, :], hraw[:, n % 2, :], ACT.Copy).then_inc(S["sh_hi"], 1)
                if e == 0:
                    high(PIECES[4])
                    high(PIECES[5])
            high(("routed", 0, 0))
            high(("routed", 1, 0))

            def keep_gathered(g):
                width = min(GB, NBLK - g * GB) * P
                for u in range(2 * DC):
                    act.wait_ge(S["gx_done"], (2 * DC + 1) * g + u + 1)
                    act.activation(xe[:, g % 2, u % 2, u // 2, 0:width], bank[2 + u % 2][:, 0:width],
                                   ACT.Copy).then_inc(S["gx_ready"], 1)
                act.wait_ge(S["gx_done"], (2 * DC + 1) * (g + 1))
                w = width // P * 2 * NE
                if g >= 2:
                    act.wait_ge(S["gw_ready"], GB * (g - 1))
                act.activation(gg[:, g % 2, 0:w], bank[2][:, 0:w], ACT.Copy).then_inc(S["gx_ready"], 1)

            keep_gathered(0)
            for j in range(NBLK + 1):
                if j + 1 < NBLK:
                    high(("routed", 0, j + 1))
                if j < NBLK:
                    silu_of(NSH * FC + j, 0)
                if j >= 1:
                    act.wait_ge(S["hr_done"], j)
                    if j >= 3:
                        act.wait_ge(S["ye_done"], j - 2)
                    act.activation(hTs[:, (j - 1) % 2, 0, :], bank[2][:, :], ACT.Copy).then_inc(S["hT_hi"], 1)
                if j + 1 < NBLK:
                    high(("routed", 1, j + 1))
                if j >= 1:
                    act.wait_ge(S["ye_done"], j)
                    act.wait_ge(S["gw_ready"], j)
                    if j >= 3:
                        act.wait_ge(S["c_done"], j - 2)
                    act.activation(yes[:, (j - 1) % 2, 0, :], bank[3][:, :], ACT.Copy,
                                   scale=gw[:, j - 1:j]).then_inc(S["ye_hi"], 1)
                if j < NBLK:
                    high(("routed", 2, j))
                if (j + 1) % GB == 0 and j + 1 < NBLK:
                    keep_gathered((j + 1) // GB)

        @block.vector
        def _(dve):
            pow_count = [0]

            def do(ins):
                after(dve, ins, dve_step)

            def rsqrt(dst, lo, width):
                a, b, v, y = (r[:, lo:lo + width] for r in (rs_a, rs_b, rs_in, rs_y))
                pow_count[0] += 1
                dve.wait_ge(S["pow_done"], pow_count[0])
                do(dve.tensor_tensor(a, v, y, ALU.mult))
                do(dve.tensor_tensor(b, a, y, ALU.mult))
                do(dve.tensor_scalar(a, b, -0.5, 1.5, ALU.mult, ALU.add))
                do(dve.tensor_tensor(dst, a, y, ALU.mult))

            def begin_norm(t):
                do(dve.bn_stats(stats[:, t, :], x[:, t, :]))
                do(dve.bn_aggr(mv[:, t, :], stats[:, t, :]))
                dve.tensor_scalar(rs_in[:, t:t + 1], mv[:, t, 1:2], 1e-5, None, ALU.add).then_inc(S["pow_wanted"], 1)

            def end_norm(layer, t):
                rsqrt(rq[:, t:t + 1], t, 1)
                if layer >= 1:
                    dve.wait_ge(S["xT_done"], (layer - 1) * NT + t + 1)
                dve.tensor_scalar(xn[:, t, :], x[:, t, :], mv[:, t, 0:1], rq[:, t:t + 1], ALU.subtract,
                                  ALU.mult).then_inc(S["xn_ready"], 1)

            for t in range(NT):
                dve.wait_ge(ld_x[t], 16)
                begin_norm(t)
                if t >= 1:
                    end_norm(0, t - 1)
            end_norm(0, NT - 1)
            dve.wait_ge(ld_bg, 16)
            dve.wait_ge(S["xn_ready"], NT)
            for t in range(NT):
                after(dve, dve.tensor_tensor_reduce(out=bgprod, in0=xn[:, t, :], in1=bgrow, scale=1.0, scalar=0.0,
                                                    op0=ALU.mult, op1=ALU.add, accum_out=c0s[:, t:t + 1]),
                      S["c0_ready"])
            dve.wait_ge(ld_masks, 16)
            dve.tensor_copy(ident_r[:], ident[:, 0:24]).then_inc(S["identr_ready"], 1)
            for t in range(NT):
                dve.wait_ge(S["y_done"], t + 1)
                dve.tensor_copy(yT[:, :, t * P:(t + 1) * P],
                                bank[2 + t % 2][:, :].rearrange("p (c n) -> p c n", c=DC)).then_inc(S["yT_ready"], 1)
            dve.wait_ge(ld_rows, 16)
            for t in range(NT):
                dve.wait_ge(S["xn_ready"], NT)
                do(dve.tensor_tensor(x[:, t, :], x[:, t, :], rows[:, R_BO:R_BO + D], ALU.add))

            def score_bias(t):
                dve.wait_ge(S["s_done"], t + 1)
                do(dve.tensor_reduce(mx[:, t:t + 1], bank[5 + t % 2][:, :], AX, ALU.max))
                do(dve.tensor_tensor(mc[:, t:t + 1], mx[:, t:t + 1], c0s[:, t:t + 1], ALU.add))
                dve.tensor_tensor(nb[:, t:t + 1], c0s[:, t:t + 1], mc[:, t:t + 1],
                                  ALU.subtract).then_inc(S["bias_ready"], 1)

            def add_projection(t):
                dve.wait_ge(S["proj_done"], t + 1)
                after(dve, dve.tensor_tensor(x[:, t, :], x[:, t, :], bank[2 + t % 2][:, :], ALU.add), S["x1_done"])
                begin_norm(t)

            def normalise(t):
                dve.wait_ge(S["exp_done"], t + 1)
                dve.reciprocal(rsm[:, t:t + 1], sm[:, t:t + 1]).then_inc(S["rs_ready"], 1)

            score_bias(0)
            normalise(0)
            score_bias(1)
            for t in range(NT):
                if t + 1 < NT:
                    normalise(t + 1)
                if t + 2 < NT:
                    score_bias(t + 2)
                dve.wait_ge(S["oT_done"], t + 1)
                if t >= 2:
                    dve.wait_ge(S["proj_done"], t - 1)
                dve.tensor_copy(oT_b[:, t % 2, :], bank[4][:, :]).then_inc(S["oT_ready"], 1)
                if t >= 1:
                    add_projection(t - 1)
                if t >= 2:
                    end_norm(1, t - 2)
            add_projection(NT - 1)
            end_norm(1, NT - 2)
            end_norm(1, NT - 1)

            def over_tokens(ap, n):
                return ap.unsqueeze(1).broadcast_to([P, NT, n])
            gth = gt.rearrange("p t (h n) -> p (t h) n", h=H)
            spreadm = gtm.unsqueeze(2).broadcast_to([P, NT * H, NPROB])

            def gating_1():
                dve.wait_ge(S["gate_done"], NT)
                after(dve, dve.tensor_copy(lg, bank[3][:, 0:24 * NT].rearrange("p (t n) -> p t n", t=NT)),
                      S["gate_exp_wanted"])

            def gating_2():
                dve.wait_ge(S["gate_exp_done"], 1)
                do(dve.tensor_scalar(beta, beta, 1.0, None, ALU.add))
                do(dve.reciprocal(beta, beta))
                do(dve.tensor_tensor(gt, lg[:, :, 0:20], over_tokens(rows[:, R_GB:R_GB + 20], 20), ALU.add))
                for t in range(NT):
                    g3 = gt[:, t, :].rearrange("p (h n) -> p h n", h=H)
                    do(dve.tensor_tensor(g3, g3, itemp.unsqueeze(2).broadcast_to([P, H, NPROB]), ALU.mult))
                do(dve.tensor_reduce(gtm, gth, AX, ALU.max))
                after(dve, dve.tensor_tensor(gth, gth, spreadm, ALU.subtract), S["gate_exp_wanted"])

            def gating_3():
                dve.wait_ge(S["gate_exp_done"], 2)
                do(dve.tensor_reduce(gtm, gth, AX, ALU.add))
                do(dve.reciprocal(gtm, gtm))
                do(dve.tensor_tensor(gth, gth, spreadm, ALU.mult))
                do(dve.tensor_scalar(epsc, rows[:, R_EPS:R_EPS + H], 0.0, 0.2, ALU.max, ALU.min))
                do(dve.tensor_scalar(epsm, epsc, -float(NPROB), 1.0, ALU.mult, ALU.add))
                for t in range(NT):
                    g3 = gt[:, t, :].rearrange("p (h n) -> p h n", h=H)
                    do(dve.tensor_tensor(g3, g3, epsm.unsqueeze(2).broadcast_to([P, H, NPROB]), ALU.mult))
                    do(dve.tensor_tensor(g3, g3, epsc.unsqueeze(2).broadcast_to([P, H, NPROB]), ALU.add))

            for h in range(H):
                dve.wait_ge(ld_wod, 16)
                dve.tensor_scalar(wod[:, h, :], wod[:, h, :], cols[:, C_NORM:C_NORM + 1], None,
                                  ALU.mult).then_inc(S["wod_scaled"], 1)

            def lagged(dst, src, w, lag):
                d = dst.rearrange("p (b l) -> p b l", b=B)[:, :, lag:L]
                s = src.rearrange("p (b l) -> p b l", b=B)[:, :, 0:L - lag]
                return dve.scalar_tensor_tensor(out=d, in0=s, scalar=w, in1=d, op0=ALU.mult, op1=ALU.add)

            def fir_steps(step, heads):
                n = 0
                dve.wait_ge(S["xT_done"], 2 * NT)
                for h in heads:
                    dve.wait_ge(S["silu_done"], h + 1)
                    for i, (taps, off) in enumerate(FIRS):
                        w0 = C_FIR + h * (KS + KM + KL) + off
                        for lag in range(taps):
                            if i == 2 and 1 <= lag <= LAGS_PE:
                                continue
                            if n:
                                dve.wait_ge(step, n)
                            w = cols[:, w0 + taps - 1 - lag:w0 + taps - lag]
                            if lag == 0:
                                ins = dve.tensor_scalar(branch[i][:, h], vP[:, h], w, None, ALU.mult)
                            else:
                                ins = lagged(branch[i][:, h], vP[:, h], w, lag)
                            ins.then_inc(step, 1)
                            n += 1
                            yield
                    fir_end[h] = (step, n)
            fir_end = {}
            streams = [fir_steps(S["fir_even"], (0, 2)), fir_steps(S["fir_odd"], (1, 3))]

            def fir(n):
                for _ in range(n):
                    for stream in streams:
                        next(stream, None)

            def add_fir_pe(h):
                dve.wait_ge(S["firpe_kept"], h + 1)
                dve.wait_ge(*fir_end[h])
                d, src = (v.rearrange("p (b l) -> p b l", b=B)[:, :, 1:] for v in (branch[2][:, h], kbP[:, h]))
                dve.tensor_tensor(d, d, src, ALU.add).then_inc(S["firpe_added"], 1)

            for g in range(3 * H):
                j, h = g // H, g % H
                dve.wait_ge(S["lag0_done"], g + 1)
                for lag in range(1, KC):
                    w = C_CONV + (j * H + h) * KC + KC - 1 - lag
                    ins = lagged(plane[j][:, h], bank[5 + g % 3][:, :], cols[:, w:w + 1], lag)
                    if lag < KC - 1:
                        do(ins)
                    else:
                        ins.then_inc(S["conv_done"], 1)
                if g >= 3:
                    fir(1)
                if g == H + 1:
                    gating_1()
                if g == H + 2:
                    gating_2()
                if g == H + 3:
                    gating_3()
            fir(4)
            for h in range(H):
                dve.wait_ge(S["vt_done"], h + 1)
                dve.tensor_tensor(bv[:, h].rearrange("p (t n) -> p t n", t=NT),
                                  bank[h % 2][:, :].rearrange("p (t n) -> p t n", t=NT),
                                  beta[:, :, h:h + 1].broadcast_to([P, NT, P]), ALU.mult).then_inc(S["bv_ready"], 1)
            dve.wait_ge(S["sumsq_done"], 2 * H)
            after(dve, dve.tensor_scalar(rs_in[:, 0:32], bank[4][:, 256:288], 1e-6, None, ALU.add), S["pow_wanted"])
            fir(5)
            rsqrt(ktr, 0, 32)
            ktr3 = ktr.rearrange("p (i t) -> p t i", t=NT)
            for t in range(NT):
                do(dve.tensor_tensor(cc[:, t, 20:24], beta[:, t, :], ktr3[:, t, 0:H], ALU.mult))
                do(dve.tensor_copy(cc[:, t, 0:20], gt[:, t, :]))
                ins = dve.tensor_tensor(cc[:, t, 3:20:NPROB], gt[:, t, 3:20:NPROB], ktr3[:, t, H:2 * H], ALU.mult)
                if t < NT - 1:
                    do(ins)
                else:
                    ins.then_inc(S["cc_ready"], 1)
            for h in range(H):
                if h == 0:
                    dve.wait_ge(S["ct_ready"], 1)
                    dve.tensor_tensor(ct[:, 1, :], bank[3][0:24, :], ct[:, 0, :].bitcast(F32),
                                      ALU.subtract).then_inc(S["ct_lo"], 1)
                    fir(2)
                dve.wait_ge(S["kb_done"], h + 1)
                dve.tensor_tensor(kbP[:, h], kP[:, h], bank[5 + h % 3][:, :], ALU.mult).then_inc(S["kb_ready"], 1)
            for h in range(H):
                dve.wait_ge(S["kk_done"], h + 1)
                for t in range(NT):
                    s = slice(t * P, (t + 1) * P)
                    ins = dve.scalar_tensor_tensor(out=mt[:, h, s], in0=bank[h][:, s],
                                                   scalar=ktr[:, NT * h + t:NT * h + t + 1],
                                                   in1=masks[:, M_STRICT, :], op0=ALU.mult, op1=ALU.mult)
                    if t < NT - 1:
                        do(ins)
                    else:
                        after(dve, ins, S["mt_ready"])
                m1 = masks[:, M_L1, :].unsqueeze(1).broadcast_to([P, NT, P])
                eye = ident.unsqueeze(1).broadcast_to([P, NT, P])
                t3 = tt[:, h].rearrange("p (t n) -> p t n", t=NT)
                do(dve.tensor_tensor(t3, mt[:, h].rearrange("p (t n) -> p t n", t=NT), m1, ALU.mult))
                dve.tensor_tensor(t3, eye, t3, ALU.subtract).then_inc(S["tt1_ready"], 1)
            for h in range(H):
                dve.wait_ge(S["at_done"], h + 1)
                for t in range(NT):
                    s = slice(t * P, (t + 1) * P)
                    ins = dve.scalar_tensor_tensor(out=att[:, h, s], in0=bank[4 + h][:, s],
                                                   scalar=ktr[:, NT * h + t:NT * h + t + 1],
                                                   in1=masks[:, M_INCL, :], op0=ALU.mult, op1=ALU.mult)
                    if t < NT - 1:
                        do(ins)
                    else:
                        ins.then_inc(S["at_ready"], 1)
            for l in range(len(LEVELS)):
                for h in range(H):
                    fir(FIR_PACE)
                    n = H * l + h
                    if l < len(LEVELS) - 1:
                        dve.wait_ge(S["z_done"], n + 1)
                        dve.tensor_tensor(tm[:, h], tm[:, h], bank[3 + 2 * (h % 2)][:, :],
                                          ALU.subtract).then_inc(S["t_upd"], 1)
                    dve.wait_ge(S["zt_done"], n + 1)
                    dve.tensor_tensor(tt[:, h], tt[:, h], bank[4 + 2 * (h % 2)][:, :],
                                      ALU.subtract).then_inc(S["tt_upd"], 1)
            fir(10 ** 6)
            for h in range(H):
                add_fir_pe(h)
            dve.wait_ge(S["firpe_added"], H)
            for h in range(H):
                for i, dst in enumerate((branch[0], branch[1], branch[2], tm, vP)):
                    if i == 3:
                        dve.wait_ge(S["d_ready"], h + 1)
                    dve.wait_ge(S["bc_done"], h * NPROB + i + 1)
                    dve.tensor_tensor(dst[:, h], dst[:, h], bank[(h * NPROB + i) % 4][:, :],
                                      ALU.mult).then_inc(S["weighted"], 1)

            def low(p):
                i = number[p]
                dve.wait_ge(S["w_hi"], i + 1)
                dve.tensor_tensor(wsp[:, (i + 2) % 4, 1, :], early[:, i % 3, :], wsp[:, (i + 2) % 4, 0, :].bitcast(F32),
                                  ALU.subtract).then_inc(S["w_lo"], 1)

            dve.wait_ge(S["osum_done"], H)
            after(dve, dve.tensor_scalar(rs_in[:, 0:16], bank[7][:, 0:16], 1.0 / DV, 1e-5, ALU.mult, ALU.add),
                  S["pow_wanted"])
            rsqrt(orr, 0, 16)
            for t in range(NT):
                for h in range(H):
                    n = t * H + h
                    dve.wait_ge(S["m_done"], n + 1)
                    after(dve, dve.scalar_tensor_tensor(out=x[:, t, :], in0=bank[3 + n % 4][:, :],
                                                        scalar=orr[:, n:n + 1], in1=x[:, t, :], op0=ALU.mult,
                                                        op1=ALU.add), S["x2_done"])
                begin_norm(t)
                if t >= 1:
                    end_norm(2, t - 1)
            low(PIECES[0])
            end_norm(2, NT - 1)
            low(PIECES[1])

            for t in range(NT):
                ts = slice(t * P, (t + 1) * P)
                dve.wait_ge(S["xr_hi"], 2 * t + 1)
                dve.tensor_tensor(xnr[:, 1, t, :], xn[:, t, :], xnr[:, 0, t, :].bitcast(F32),
                                  ALU.subtract).then_inc(S["xr_lo"], 1)
                dve.wait_ge(S["xr_hi"], 2 * t + 2)
                dve.tensor_tensor(xe[:, 0, 1, :, ts], xnT[:, :, ts], xe[:, 0, 0, :, ts].bitcast(F32),
                                  ALU.subtract).then_inc(S["xr_lo"], 1)
            low(PIECES[2])
            low(PIECES[3])
            dve.wait_ge(S["rout_done"], NT)
            after(dve, dve.tensor_copy(rl, bank[4][:, 0:NT * NE].rearrange("p (t n) -> p t n", t=NT)), S["rout_read"])
            do(dve.tensor_reduce(mx, rl, AX, ALU.max))

            def per_tile(ap):
                return ap.unsqueeze(2).broadcast_to([P, NT, NE])
            after(dve, dve.tensor_tensor(rl, rl, per_tile(mx), ALU.subtract), S["rexp_wanted"])
            for e in range(NE):
                do(dve.memset(prio[:, e:e + 1], float(NE - e)))
            dve.wait_ge(S["rexp_done"], 1)
            do(dve.tensor_reduce(sm, rl, AX, ALU.add))
            do(dve.reciprocal(rsm, sm))
            do(dve.tensor_tensor(rl, rl, per_tile(rsm), ALU.mult))
            do(dve.tensor_tensor(rw1, rl, over_tokens(rows[:, R_RB:R_RB + NE], NE), ALU.add))
            for k in range(TOPK):
                do(dve.tensor_reduce(mx, rw1, AX, ALU.max))
                do(dve.tensor_tensor(rw2, rw1, per_tile(mx), ALU.is_equal))
                do(dve.tensor_tensor(rw2, rw2, over_tokens(prio, NE), ALU.mult))
                do(dve.tensor_reduce(mx, rw2, AX, ALU.max))
                do(dve.tensor_tensor(hot[k], rw2, per_tile(mx), ALU.is_equal))
                if k == 0:
                    do(dve.scalar_tensor_tensor(out=rw1, in0=hot[k], scalar=-1e30, in1=rw1, op0=ALU.mult, op1=ALU.add))
            after(dve, dve.tensor_tensor(sel, hot[0], hot[1], ALU.add), S["sel_ready"])

            def product(n, b):
                dve.wait_ge(S["fsilu_done"], n + 1)
                dve.wait_ge(S["h3_done"], n + 1)
                if NSH * FC > n >= 2:
                    dve.wait_ge(S["sh_lo"], n - 1)
                if n >= NSH * FC + 2:
                    dve.wait_ge(S["hr_done"], n - NSH * FC - 1)
                dve.tensor_tensor(hraw[:, n % 2, :], sil[:], bank[b][:, :], ALU.mult).then_inc(S["prod_ready"], 1)

            def shared_hidden(n):
                product(n, 2 * (n % 2) + 1)
                dve.wait_ge(S["sh_hi"], n + 1)
                dve.tensor_tensor(xe[:, 1, 1, n % FC, :], hraw[:, n % 2, :], xe[:, 1, 0, n % FC, :].bitcast(F32),
                                  ALU.subtract).then_inc(S["sh_lo"], 1)

            shared_hidden(0)
            do(dve.tensor_tensor(gated, sel, rl, ALU.mult))
            do(dve.tensor_copy(gate_r[:, :, 0:NE], gated))
            do(dve.tensor_tensor(gate_r[:, :, NE:2 * NE], gated, gate_r[:, :, 0:NE].bitcast(F32), ALU.subtract))
            shared_hidden(1)
            dve.wait_ge(S["pos_done"], 1)
            do(dve.tensor_copy(cnt, bank[5][:, NE * NT:NE * (NT + 1)]))
            thr = consts[:, K_THR:K_THR + NT].unsqueeze(1).broadcast_to([P, NE, NT])
            do(dve.tensor_tensor(over, cnt.unsqueeze(2).broadcast_to([P, NE, NT]), thr, ALU.is_gt))
            do(dve.tensor_reduce(nblk, over, AX, ALU.add))
            do(dve.tensor_copy(end, nblk))
            for e in range(1, NE):
                do(dve.tensor_tensor(end[:, e:e + 1], end[:, e:e + 1], end[:, e - 1:e], ALU.add))
            do(dve.tensor_tensor(start_b, end, nblk, ALU.subtract))
            do(dve.scalar_tensor_tensor(out=base, in0=over_tokens(start_b, NE), scalar=float(P),
                                        in1=bank[5][:, 0:NE * NT].rearrange("p (t n) -> p t n", t=NT),
                                        op0=ALU.mult, op1=ALU.add))
            for k in range(TOPK):
                do(dve.tensor_tensor(rw1, hot[k], base, ALU.mult))
                ins = dve.tensor_reduce(slot[:, k, :], rw1, AX, ALU.add)
                if k == 0:
                    do(ins)
                else:
                    after(dve, ins, S["slot_ready"])
            nums = consts[:, K_NUM:K_NUM + NBLK]
            do(dve.tensor_tensor(owner, end.unsqueeze(1).broadcast_to([P, NBLK, NE]),
                                 nums.unsqueeze(2).broadcast_to([P, NBLK, NE]), ALU.is_le))
            do(dve.tensor_reduce(expert, owner, AX, ALU.add))
            do(dve.tensor_scalar(expert, expert, float(NE - 1), None, ALU.min))
            after(dve, dve.tensor_copy(expert_i[:], expert), S["expert_ready"])
            do(dve.tensor_tensor(owner, expert.unsqueeze(2).broadcast_to([P, NBLK, NE]),
                                 nums[:, 0:NE].unsqueeze(1).broadcast_to([P, NBLK, NE]), ALU.is_equal))
            for g in range(NG):
                do(dve.tensor_scalar(slotg[:, g], slot, -float(GB * P * g), None, ALU.add))
            shared_hidden(2)
            shared_hidden(3)
            for k in range(TOPK):
                dve.wait_ge(S["plane_done"], k + 1)
                after(dve, dve.tensor_copy(planes[:, k, :], bank[6 + k][:, :]), S["plane_ready"])

            def make_pick(g):
                width = min(GB, NBLK - g * GB) * P
                dve.wait_ge(ld_iota, 16)
                if g >= 1:
                    dve.wait_ge(S["gx_done"], (2 * DC + 1) * g)
                for t in range(NT):
                    do(dve.tensor_scalar(pick[:, t, 0:width], iota[:, 0:width], slotg[:, g, 0, t:t + 1], None,
                                         ALU.is_equal))
                    ins = dve.scalar_tensor_tensor(out=pick[:, t, 0:width], in0=iota[:, 0:width],
                                                   scalar=slotg[:, g, 1, t:t + 1],
                                                   in1=pick[:, t, 0:width].bitcast(F32), op0=ALU.is_equal, op1=ALU.add)
                    if t < NT - 1:
                        do(ins)
                    else:
                        ins.then_inc(S["pick_ready"], 1)

            def make_back(j):
                if j >= 2:
                    dve.wait_ge(S["c_done"], j - 1)
                own = consts[:, K_SLOT + j:K_SLOT + j + 1]
                do(dve.tensor_scalar(back[:, j % 2, :], planes[:, 0, :], own, None, ALU.is_equal))
                dve.scalar_tensor_tensor(out=back[:, j % 2, :], in0=planes[:, 1, :], scalar=own,
                                         in1=back[:, j % 2, :].bitcast(F32), op0=ALU.is_equal,
                                         op1=ALU.add).then_inc(S["back_ready"], 1)

            def make_gate(j):
                g = j // GB
                dve.wait_ge(S["gx_ready"], (2 * DC + 1) * (g + 1))
                b = j % GB
                do(dve.tensor_tensor(gw2, gg[:, g % 2, 2 * NE * b:2 * NE * (b + 1)].rearrange("p (i n) -> p i n", i=2),
                                     owner[:, j, :].unsqueeze(1).broadcast_to([P, 2, NE]), ALU.mult))
                dve.tensor_reduce(gw[:, j:j + 1], gw2.rearrange("p i n -> p (i n)"), AX,
                                  ALU.add).then_inc(S["gw_ready"], 1)

            make_pick(0)
            low(PIECES[4])
            low(PIECES[5])
            for n in range(FC, 2 * FC):
                shared_hidden(n)
            low(("routed", 0, 0))
            low(("routed", 1, 0))
            for j in range(NBLK + 1):
                if j + 1 < NBLK:
                    low(("routed", 0, j + 1))
                if j < NBLK:
                    make_gate(j)
                if j >= 1:
                    dve.wait_ge(S["hT_hi"], j)
                    dve.tensor_tensor(hTs[:, (j - 1) % 2, 1, :], bank[2][:, :], hTs[:, (j - 1) % 2, 0, :].bitcast(F32),
                                      ALU.subtract).then_inc(S["hT_lo"], 1)
                if j + 1 < NBLK:
                    low(("routed", 1, j + 1))
                if j < NBLK:
                    product(NSH * FC + j, 1)
                if j >= 1:
                    dve.wait_ge(S["ye_hi"], j)
                    dve.scalar_tensor_tensor(out=yes[:, (j - 1) % 2, 1, :], in0=bank[3][:, :], scalar=gw[:, j - 1:j],
                                             in1=yes[:, (j - 1) % 2, 0, :].bitcast(F32), op0=ALU.mult,
                                             op1=ALU.subtract).then_inc(S["ye_lo"], 1)
                if j < NBLK:
                    make_back(j)
                    low(("routed", 2, j))
                if j % GB == 0 and j // GB + 1 < NG:
                    make_pick(j // GB + 1)
            dve.wait_ge(S["c_done"], NBLK)
            for t in range(NT):
                dve.tensor_tensor(x[:, t, :], x[:, t, :], bank[4 + t][:, :], ALU.add).then_inc(S["acc_done"], 1)


def kernel(**inputs):
    import concourse.bacc as bacc
    from concourse.bass_utils import run_bass_kernel_spmd

    a = {k: np.asarray(v) for k, v in inputs.items()}

    def chunks(w):
        return w.reshape(-1, P, w.shape[1]).transpose(1, 0, 2).reshape(P, -1)

    ctx = a["ctx_1024"]
    by_tile = ctx.reshape(NT, PAIR, TK // P, P, D).transpose(0, 3, 1, 2, 4).reshape(NT, P, -1)
    byT = ctx.transpose(0, 2, 1).reshape(NT, PAIR, DC, P, TK).transpose(0, 3, 1, 2, 4).reshape(NT, P, -1)
    fir = np.concatenate([a[f"L0_attn_fir_{s}"].transpose(1, 0, 2) for s in "sml"], axis=2)
    conv = np.stack([a[f"L0_attn_conv_{s}"].reshape(H, P, KC) for s in "vkq"]).transpose(2, 0, 1, 3)
    wgate = np.concatenate([a["L0_attn_gate_w"].reshape(H * NPROB, D), a["L0_attn_Wb"]]).T
    cols = np.concatenate([conv.reshape(P, -1), fir.reshape(P, -1), a["L0_attn_norm_w"].reshape(P, 1),
                           chunks(wgate), chunks(a["L0_ffn_gate_w"].T)], axis=1)
    row = np.concatenate([a["L0_xattn_bo"], a["L0_attn_gate_b"].ravel(), a["L0_attn_log_temp"].ravel(),
                          a["L0_attn_eps_param"].ravel(), a["L0_ffn_gate_bias"]])
    w1 = list(a["L0_ffn_w1"]) + list(a["L0_ffn_sw1"].reshape(NSH, FF, D))
    w3 = list(a["L0_ffn_w3"]) + list(a["L0_ffn_sw3"].reshape(NSH, FF, D))
    w2 = list(a["L0_ffn_w2"]) + list(a["L0_ffn_sw2"].reshape(D, NSH, FF).transpose(1, 0, 2))
    i, j = np.meshgrid(np.arange(P), np.arange(P), indexing="ij")
    same = i // L == j // L
    merge = [(i // (2 * m) == j // (2 * m)) & (i // m % 2 == 0) & (j // m % 2 == 1) for m in (1,) + LEVELS]
    masks = np.stack([i == j, same & (i < j), same & (i <= j)] + merge + [i < j], axis=1).reshape(P, -1)
    row_no = np.arange(P)[:, None]
    masks = np.concatenate([masks, np.broadcast_to(P * np.arange(NT), (P, NT)),
                            np.broadcast_to(np.arange(NBLK), (P, NBLK)),
                            row_no + P * np.arange(NBLK)[None, :]], axis=1).astype(np.float32)
    arrays = {
        "x_in": a["x"].reshape(NT, P, D),
        "ctx_in": by_tile,
        "ctxT_in": byT,
        "wg_in": chunks(a["L0_xattn_Wg"].T).reshape(P, DC, D),
        "wox_in": chunks(a["L0_xattn_Wo"]).reshape(P, DC, D),
        "wqkv_in": np.concatenate([chunks(a[f"L0_attn_W{s}"].T) for s in "vkq"], axis=1),
        "wod_in": chunks(a["L0_attn_Wo"].T),
        "wffn_in": np.stack([np.concatenate([chunks(p.T), chunks(q.T), chunks(r.T)], axis=1)
                             for p, q, r in zip(w1, w3, w2)]),
        "cols_in": cols,
        "rows_in": np.broadcast_to(row, (P, NROW)),
        "masks_in": masks,
        "iota_in": np.broadcast_to(np.arange(512, dtype=np.float32), (P, 512)),
        "bg_in": np.broadcast_to(a["L0_xattn_bg"], (P, D)),
    }
    arrays = {k: np.ascontiguousarray(v) for k, v in arrays.items()}
    nc = bacc.Bacc("TRN2", target_bir_lowering=False, num_devices=1)
    args = [nc.dram_tensor(k, v.shape, mybir.dt.from_np(v.dtype), kind="ExternalInput").ap() for k, v in arrays.items()]
    args.append(nc.dram_tensor("out", (NT, P, D), F32, kind="ExternalOutput").ap())
    perceiver_block(nc, *args)
    r = run_bass_kernel_spmd(nc, [arrays], core_ids=[0])
    return r.results[0]["out"].reshape(B, L, D)
```

```python
from contextlib import ExitStack

import numpy as np
import concourse.bass as bass
from concourse import mybir

P = 128
B, L, D = 8, 64, 512
TK = 512
H, DV = 4, 128
NT = B * L // P
PAIR = P // L
DC = D // P
NTOK = B * L
KS, KM, KL, KC = 3, 15, 63, 4
NE, NSH, FF = 8, 2, 512
NX = NE + NSH
FC = FF // P
LAGS_PE = 16
FIR_PACE = 6
LEVELS = (2, 4, 8, 16, 32)
NPROB = 5

C_CONV = 0
C_FIR = C_CONV + 3 * H * KC
C_NORM = C_FIR + H * (KS + KM + KL)
C_GATE = C_NORM + 1
C_ROUT = C_GATE + DC * 24
NCOL = C_ROUT + DC * NE
R_BO = 0
R_GB = R_BO + D
R_TEMP = R_GB + H * NPROB
R_EPS = R_TEMP + H
R_RB = R_EPS + H
NROW = R_RB + NE
M_ID, M_STRICT, M_INCL, M_L1 = 0, 1, 2, 3
M_BEFORE = M_L1 + 1 + len(LEVELS)
NMASK = M_BEFORE + 1
TOPK = 2
GB = 4
MINB = NTOK * TOPK // P
MAXB = -(-(MINB + NE - 1) // GB) * GB
K_THR = NMASK * P
K_NUM = K_THR + NTOK // P
K_TURN = K_NUM + MAXB
K_SLOT = K_TURN + GB
NCONST = K_SLOT + GB

F32 = mybir.dt.float32
F32R = mybir.dt.float32r
I32 = mybir.dt.int32
ALU = mybir.AluOpType
ACT = mybir.ActivationFunctionType
AX = mybir.AxisListType.X
FIRS = ((KS, 0), (KM, KS), (KL, KS + KM))


def perceiver_block(nc, x_in, ctx_in, ctxT_in, wg_in, wox_in, wqkv_in, wod_in, wffn_in, cols_in, rows_in,
                    masks_in, iota_in, bg_in, out):
    with ExitStack() as stack:
        def sb(name, shape, dt=F32, held=stack):
            return held.enter_context(nc.sbuf_tensor(name, shape, dt))

        def sem(name):
            return stack.enter_context(nc.semaphore(name))

        x = sb("x", [P, NT, D])
        xnT = sb("xnT", [P, DC, NTOK])
        early = sb("early", [P, 3, 2048])
        cols = sb("cols", [P, NCOL])
        rows = sb("rows", [P, NROW])
        consts = sb("consts", [P, NCONST])
        small = sb("small", [P, 1330])
        gate_r = sb("gate_r", [P, NT, 2 * NE], F32R)
        ident_r = sb("ident_r", [P, 24], F32R)
        expert_i = sb("expert_i", [P, MAXB + GB], I32)
        with ExitStack() as before:
            ring = sb("ring", [P, 4, 8192], held=before)
            part = sb("part", [P, 3, 4, 512], held=before)
        xe = sb("xe", [P, 2, 2, DC, 512], F32R)
        wsp = sb("wsp", [P, 4, 2, 2048], F32R)
        xnr = sb("xnr", [P, 2, NT, D], F32R)
        hTs = sb("hTs", [P, 2, 2, 512], F32R)
        planes = sb("planes", [P, TOPK, NTOK])
        back = sb("back", [P, 2, NTOK], F32R)
        pick = sb("pick", [P, NT, 512], F32R)
        yes = sb("yes", [P, 2, 2, D], F32R)
        hraw = sb("hraw", [P, 2, 512])
        sil = sb("sil", [P, 512])
        iota = sb("iota", [P, 512])
        masks = consts[:, 0:NMASK * P].rearrange("p (m n) -> p m n", n=P)
        bank = [stack.enter_context(nc.psum_tensor(f"bank{i}", [P, 512], F32)) for i in range(8)]

        ident = masks[:, M_ID, :]
        ctxT = [ring[:, t, 0:4096].rearrange("p (b c k) -> p b c k", b=PAIR, c=DC) for t in range(NT)]
        ctx = [ring[:, t, 4096:8192].rearrange("p (b c d) -> p b c d", b=PAIR, c=TK // P) for t in range(NT)]
        wgT, wox, xn = part[:, 0], part[:, 1], part[:, 2]
        yT = early[:, 0, :].rearrange("p (c n) -> p c n", c=DC)
        probs_b = early[:, 1, 0:1024].rearrange("p (i n) -> p i n", i=2)
        probsT_b = early[:, 1, 1024:2048].rearrange("p (i n) -> p i n", i=2)
        oT_b = early[:, 2, 0:1024].rearrange("p (i n) -> p i n", i=2)
        o_b = early[:, 2, 1024:2048].rearrange("p (i n) -> p i n", i=2)
        bgrow, bgprod = o_b[:, 0, :], o_b[:, 1, :]
        sq_b = early[:, 2, 1024:2048].rearrange("p (i n) -> p i n", i=2)
        wqkv = ring[:, 0, 0:6144].rearrange("p (j c n) -> p j c n", j=3, c=DC)
        wod = ring[:, 0, 6144:8192].rearrange("p (h n) -> p h n", h=H)
        vP, kP, qP, kbP = (ring[:, 1, 2048 * i:2048 * i + 2048].rearrange("p (h n) -> p h n", h=H) for i in range(4))
        plane = [vP, kP, qP]
        mt, lt, tt, att = (ring[:, 2, 2048 * i:2048 * i + 2048].rearrange("p (h n) -> p h n", h=H) for i in range(4))
        tm, yy, bv = (ring[:, 3, 2048 * i:2048 * i + 2048].rearrange("p (h n) -> p h n", h=H) for i in range(3))
        sq2 = ring[:, 3, 6144:7168].rearrange("p (i n) -> p i n", i=2)
        ct = back[0:24]
        diag = rows[:, R_BO:R_BO + 512].rearrange("p (i n) -> p i n", i=4)
        turn_numbers = consts[:, K_TURN:K_TURN + GB]
        slots = consts[:, K_SLOT:K_SLOT + GB]
        branch = [part[:, i] for i in range(3)]

        at = [0]

        def take(n):
            at[0] += n
            assert at[0] <= 1330
            return small[:, at[0] - n:at[0]]
        stats = take(NT * 6).rearrange("p (t n) -> p t n", t=NT)
        mv = take(NT * 2).rearrange("p (t n) -> p t n", t=NT)
        rs_in, rs_y, rs_a, rs_b = take(32), take(32), take(32), take(32)
        half = take(32)
        ones = take(2)
        mx, mc, nb, c0s, sm, rsm = (take(NT) for _ in range(6))
        lg = take(NT * 24).rearrange("p (t n) -> p t n", t=NT)
        gt = take(NT * 20).rearrange("p (t n) -> p t n", t=NT)
        gtm = take(NT * H)
        beta = take(NT * H).rearrange("p (t h) -> p t h", t=NT)
        itemp, epsc, epsm = take(H), take(H), take(H)
        ktr = take(32)
        cc = take(NT * 24).rearrange("p (t n) -> p t n", t=NT)
        orr = take(H * NT)
        rl = take(NT * NE).rearrange("p (t n) -> p t n", t=NT)
        prio = take(NE)
        hot = [take(NT * NE).rearrange("p (t n) -> p t n", t=NT) for _ in range(TOPK)]
        sel, base = (take(NT * NE).rearrange("p (t n) -> p t n", t=NT) for _ in range(2))
        gated = take(NT * NE).rearrange("p (t n) -> p t n", t=NT)
        cnt, nblk, end, start_b = (take(NE) for _ in range(4))
        over = take(NE * NT).rearrange("p (e n) -> p e n", e=NE)
        slot = take(TOPK * NT).rearrange("p (k t) -> p k t", k=TOPK)
        slotg = take(TOPK * NT).rearrange("p (k t) -> p k t", k=TOPK)
        owner = take(MAXB * NE).rearrange("p (j e) -> p j e", j=MAXB)
        owner4 = take(GB * NE).rearrange("p (j e) -> p j e", j=GB)
        expert4 = take(GB)
        expert = take(MAXB + GB)
        gg = take(GB * 2 * NE)
        gw2 = take(2 * NE).rearrange("p (i n) -> p i n", i=2)
        gw = take(GB)
        rw1, rw2 = (take(NT * NE).rearrange("p (t n) -> p t n", t=NT) for _ in range(2))
        rq = take(NT)

        ld_x = [sem(f"ld_x{t}") for t in range(NT)]
        ld_masks, ld_cols, ld_rows, ld_wg, ld_wox, ld_wqkv, ld_wod = (
            sem(n) for n in ("ld_masks", "ld_cols", "ld_rows", "ld_wg", "ld_wox", "ld_wqkv", "ld_wod"))
        ld_ctxT = [sem(f"ld_ctxT{t}") for t in range(NT)]
        ld_ctx = [sem(f"ld_ctx{t}") for t in range(NT)]
        ld_bg = sem("ld_bg")
        ld_raw = [sem(f"ld_raw{i}") for i in range(3)]
        w_hi = [sem(f"w_hi{i}") for i in range(3)]
        w_lo = [sem(f"w_lo{i}") for i in range(3)]
        ld_iota = sem("ld_iota")
        stored = sem("stored")
        dve_step, act_step, pool_step = sem("dve_step"), sem("act_step"), sem("pool_step")
        names = ("pow_wanted", "pow_done", "pool_consts", "xn_ready", "xT_done", "xnT_ready", "y_done", "yT_ready",
                 "s_done", "bias_ready", "exp_done", "pT_done", "pT_ready",
                 "oT_done", "oT_ready", "proj_done", "x1_done", "gate_done", "gate_read", "gate_exp_wanted",
                 "gate_exp_done", "qkv_done", "lag0_done", "conv_done", "silu_done", "sq_done", "sumsq_done",
                 "vt_done", "bv_ready", "cc_ready", "ct_done", "ct_ready", "kb_done", "kb_ready", "kk_done",
                 "mt_ready", "at_done", "at_ready", "tt1_ready", "t1_done", "t1_ready", "lt_ready", "yl_done",
                 "yl_ready", "z_done", "zt_done", "t_upd", "tt_upd", "u_done", "u_ready", "o_done", "d_ready",
                 "bc_done", "weighted", "o_ready", "osq_ready", "osum_done", "m_done", "x2_done", "rout_done",
                 "rout_read", "rexp_wanted", "rexp_done", "h1_done", "h3_done", "fsilu_done", "wod_scaled",
                 "xr_hi", "xr_lo", "sel_ready", "pos_done", "expert_ready", "slot_ready",
                 "plane_done", "plane_ready", "prod_ready", "sh_hi", "sh_lo", "sd_done", "pick_ready", "gx_done",
                 "gx_ready", "hr_done", "hT_hi", "hT_lo", "ye_done", "gw_ready", "ye_hi", "ye_lo", "back_ready",
                 "c_done", "acc_done", "c0_ready", "identr_ready", "rs_ready", "pv_done",
                 "o_kept", "ct_lo", "fir_even", "fir_odd", "firpe_kept", "firpe_added", "diag_ready",
                 "diag_used", "gg_done", "gg_ready", "turn_step", "slots_step", "gate_step", "pick_step", "back_step",
                 "slotg_ready")
        S = {n: sem(n) for n in names}
        for_count = {}

        def signal(ins, s):
            for_count[s.name] = for_count.get(s.name, 0) + 1
            ins.then_inc(s, 1)
            return for_count[s.name]

        def after(eng, ins, s):
            eng.wait_ge(s, signal(ins, s))

        def parts(which, r):
            if which == 0 and r % 2 == 1:
                return xe[:, 1].rearrange("p i c n -> p i (c n)")
            return wsp[:, (2, 3, r % 2)[which]]

        def piece(which, r):
            return parts(which, r).rearrange("p i (c n) -> p i c n", c=DC)

        def fir_diags(n):
            steps = H * len(LEVELS)
            return range(H * LAGS_PE * n // steps, H * LAGS_PE * (n + 1) // steps)

        def expert_of(eng, j):
            return eng.value_load(expert_i[0:1, bass.ds(j, 1)], min_val=0, max_val=NE - 1)

        def first_of_last(eng):
            eng.wait_ge(S["expert_ready"], 1)
            return eng.value_load(expert_i[0:1, MAXB + GB - 1:], min_val=MINB - GB, max_val=MAXB - GB)


        block = stack.enter_context(nc.Block())

        @block.sync
        def _(sp):
            sp.dma_start(x[:, 0], x_in[0]).then_inc(ld_x[0], 16)
            sp.dma_start(consts[:], masks_in).then_inc(ld_masks, 16)
            for t in range(1, NT):
                sp.dma_start(x[:, t], x_in[t]).then_inc(ld_x[t], 16)
            sp.dma_start(wgT, wg_in).then_inc(ld_wg, 16)
            sp.dma_start(cols[:], cols_in).then_inc(ld_cols, 16)
            sp.dma_start(rows[:], rows_in).then_inc(ld_rows, 16)
            sp.dma_start(bgrow, bg_in).then_inc(ld_bg, 16)
            for t in range(NT):
                sp.dma_start(ring[:, t, 0:4096], ctxT_in[t]).then_inc(ld_ctxT[t], 16)
                sp.dma_start(ring[:, t, 4096:8192], ctx_in[t]).then_inc(ld_ctx[t], 16)
                if t == 0:
                    sp.dma_start(wox, wox_in).then_inc(ld_wox, 16)
            sp.wait_ge(S["oT_done"], 1)
            sp.dma_start(ring[:, 0, 0:6144], wqkv_in).then_inc(ld_wqkv, 16)
            sp.dma_start(ring[:, 0, 6144:8192], wod_in).then_inc(ld_wod, 16)
            sp.wait_ge(S["sumsq_done"], 2 * H)
            sp.wait_ge(S["proj_done"], NT)

            def load(which, n, expert):
                if not isinstance(n, int) or n >= 1:
                    sp.wait_ge(w_lo[which], n)
                if isinstance(expert, int):
                    src = wffn_in[expert, :, 2048 * which:2048 * (which + 1)]
                else:
                    src = wffn_in[bass.ds(expert, 1), :, 2048 * which:2048 * (which + 1)]
                    src = src.rearrange("o p n -> (o p) n")
                sp.dma_start(early[:, which, :], src).then_inc(ld_raw[which], 16)

            for e in range(NSH):
                for which in range(3):
                    load(which, e, NE + e)
                    if e == 1 and which == 0:
                        sp.wait_ge(S["xr_lo"], 2 * NT)
                        sp.dma_start(iota[:], iota_in).then_inc(ld_iota, 16)
            last_group = first_of_last(sp)

            def load_block(j):
                expert = expert_of(sp, j)
                for which in range(3):
                    load(which, NSH + j, expert)

            for j in range(3):
                load_block(j)
            with sp.Fori(0, last_group, GB) as done:
                for r in (-2, -1, 0, 1):
                    load_block(done + GB + r + 1)
            load_block(last_group + GB - 1)
            for t in range(NT):
                sp.wait_ge(S["acc_done"], t + 1)
                sp.dma_start(out[t], x[:, t]).then_inc(stored, 16)
            sp.wait_ge(stored, 16 * NT)

        @block.gpsimd
        def _(pool):
            pool.memset(half[:], -0.5).then_inc(S["pool_consts"], 1)
            pool.memset(ones[:], 1.0).then_inc(S["pool_consts"], 1)
            pool.wait_ge(S["pool_consts"], 2)

            def power(n, lo, width):
                pool.wait_ge(S["pow_wanted"], n)
                pool.tensor_tensor(rs_y[:, lo:lo + width], rs_in[:, lo:lo + width], half[:, 0:width],
                                   ALU.pow).then_inc(S["pow_done"], 1)
            for t in range(2 * NT):
                power(t + 1, t % NT, 1)
            power(2 * NT + 1, 0, 32)
            for l in range(len(LEVELS)):
                for h in range(H):
                    if l == 0:
                        pool.wait_ge(S["mt_ready"], h + 1)
                    else:
                        pool.wait_ge(S["yl_done"], H * (l - 1) + h + 1)
                    m = masks[:, M_L1 + 1 + l, :].unsqueeze(1).broadcast_to([P, NT, P])
                    pool.tensor_tensor(lt[:, h].rearrange("p (t n) -> p t n", t=NT),
                                       mt[:, h].rearrange("p (t n) -> p t n", t=NT), m,
                                       ALU.mult).then_inc(S["lt_ready"], 1)
            for h in range(H):
                pool.wait_ge(S["weighted"], NPROB * (h + 1))
                after(pool, pool.tensor_tensor(branch[0][:, h], branch[0][:, h], branch[1][:, h], ALU.add), pool_step)
                after(pool, pool.tensor_tensor(branch[2][:, h], branch[2][:, h], tm[:, h], ALU.add), pool_step)
                after(pool, pool.tensor_tensor(branch[0][:, h], branch[0][:, h], branch[2][:, h], ALU.add), pool_step)
                pool.tensor_tensor(branch[0][:, h], branch[0][:, h], vP[:, h], ALU.add).then_inc(S["o_ready"], 1)
            power(2 * NT + 2, 0, 16)
            for t in range(NT):
                power(2 * NT + 3 + t, t, 1)

            def low(n, r):
                pool.wait_ge(w_hi[2], n + 1)
                split = parts(2, r)
                pool.tensor_tensor(split[:, 1, :], early[:, 2, :], split[:, 0, :].bitcast(F32),
                                   ALU.subtract).then_inc(w_lo[2], 1)

            for n in range(NSH + 3):
                low(n, n)
            last_group = first_of_last(pool)
            with pool.Fori(0, last_group, GB) as done:
                for r in (-2, -1, 0, 1):
                    low(NSH + done + GB + r + 1, r + 1)
            low(NSH + last_group + GB - 1, -1)

        @block.tensor
        def _(pe):
            def transpose_tile(layer, t):
                pe.wait_ge(S["xn_ready"], layer * NT + t + 1)
                if layer == 0 and t == 0:
                    pe.wait_ge(ld_masks, 16)
                if t >= 2:
                    pe.wait_ge(S["xnT_ready"], layer * NT + t - 1)
                for c in range(DC):
                    last = pe.transpose(bank[t % 2][:, c * P:(c + 1) * P], xn[:, t, c * P:(c + 1) * P], ident)
                last.then_inc(S["xT_done"], 1)

            for t in range(NT):
                transpose_tile(0, t)
            pe.wait_ge(ld_wg, 16)
            pe.wait_ge(ld_cols, 16)
            for t in range(NT):
                pe.wait_ge(S["xnT_ready"], t + 1)
                if t >= 2:
                    pe.wait_ge(S["yT_ready"], t - 1)
                for c in range(DC):
                    for e in range(DC):
                        last = pe.matmul(bank[2 + t % 2][:, c * P:(c + 1) * P], wgT[:, e, c * P:(c + 1) * P],
                                         xnT[:, e, t * P:(t + 1) * P], start=(e == 0), stop=(e == DC - 1))
                last.then_inc(S["y_done"], 1)
            def scores(t):
                pe.wait_ge(S["yT_ready"], t + 1)
                pe.wait_ge(ld_ctxT[t], 16)
                if t >= 2:
                    pe.wait_ge(S["exp_done"], t - 1)
                for c in range(DC):
                    for b in range(PAIR):
                        last = pe.matmul(bank[5 + t % 2][b * L:(b + 1) * L, :],
                                         yT[:, c, t * P + b * L:t * P + (b + 1) * L], ctxT[t][:, b, c, :],
                                         start=(c == 0), stop=(c == DC - 1))
                last.then_inc(S["s_done"], 1)

            def values(t):
                pe.wait_ge(S["exp_done"], t + 1)
                if t >= 1:
                    pe.wait_ge(S["pT_ready"], t)
                for k in range(TK // P):
                    last = pe.transpose(bank[7][:, k * P:(k + 1) * P], probs_b[:, t % 2, k * P:(k + 1) * P], ident)
                last.then_inc(S["pT_done"], 1)
                pe.wait_ge(S["pT_ready"], t + 1)
                pe.wait_ge(ld_ctx[t], 16)
                if t < 2:
                    pe.wait_ge(S["xnT_ready"], NT)
                else:
                    pe.wait_ge(S["o_kept"], t - 1)
                for k in range(TK // P):
                    for b in range(PAIR):
                        last = pe.matmul(bank[t % 2][b * L:(b + 1) * L, :],
                                         probsT_b[:, t % 2, k * P + b * L:k * P + (b + 1) * L], ctx[t][:, b, k, :],
                                         start=(k == 0), stop=(k == TK // P - 1))
                last.then_inc(S["pv_done"], 1)

            def turn_values(t):
                pe.wait_ge(S["o_kept"], t + 1)
                if t >= 1:
                    pe.wait_ge(S["oT_ready"], t)
                for c in range(DC):
                    last = pe.transpose(bank[4][:, c * P:(c + 1) * P], o_b[:, t % 2, c * P:(c + 1) * P], ident)
                last.then_inc(S["oT_done"], 1)

            def project(t):
                pe.wait_ge(S["oT_ready"], t + 1)
                pe.wait_ge(ld_wox, 16)
                if t < 2:
                    pe.wait_ge(S["yT_ready"], NT)
                else:
                    pe.wait_ge(S["x1_done"], t - 1)
                for c in range(DC):
                    last = pe.matmul(bank[2 + t % 2][:, :], oT_b[:, t % 2, c * P:(c + 1) * P], wox[:, c, :],
                                     start=(c == 0), stop=(c == DC - 1))
                last.then_inc(S["proj_done"], 1)

            scores(0)
            scores(1)
            for t in range(NT):
                values(t)
                if t + 2 < NT:
                    scores(t + 2)
                if t >= 1:
                    project(t - 1)
                turn_values(t)
            project(NT - 1)

            pe.wait_ge(S["o_kept"], NT)
            for t in range(NT):
                transpose_tile(1, t)
            pe.wait_ge(S["xnT_ready"], 2 * NT)

            def gate_logits():
                pe.wait_ge(S["x1_done"], NT)
                for t in range(NT):
                    for c in range(DC):
                        last = pe.matmul(bank[3][:, 24 * t:24 * (t + 1)], xnT[:, c, t * P:(t + 1) * P],
                                         cols[:, C_GATE + 24 * c:C_GATE + 24 * (c + 1)],
                                         start=(c == 0), stop=(c == DC - 1))
                    last.then_inc(S["gate_done"], 1)

            pe.wait_ge(ld_wqkv, 16)

            def sumsq(i):
                pe.wait_ge(S["sq_done"], i + 1)
                for t in range(NT):
                    last = pe.matmul(bank[4][:, 256 + NT * i + t:257 + NT * i + t], sq_b[:, i % 2, t * P:(t + 1) * P],
                                     ones[:, 0:1], start=True, stop=True)
                last.then_inc(S["sumsq_done"], 1)

            for g in range(3 * H):
                j, h = g // H, g % H
                if g >= 3:
                    pe.wait_ge(S["conv_done"], g - 2)
                for c in range(DC):
                    last = pe.matmul(bank[5 + g % 3][:, :], wqkv[:, j, c, h * P:(h + 1) * P], xnT[:, c, :],
                                     start=(c == 0), stop=(c == DC - 1))
                last.then_inc(S["qkv_done"], 1)
                if g == H:
                    gate_logits()
                if g >= H + 2:
                    sumsq(g - H - 2)
            for h in range(H):
                pe.wait_ge(S["silu_done"], h + 1)
                if h >= 2:
                    pe.wait_ge(S["bv_ready"], h - 1)
                for t in range(NT):
                    last = pe.transpose(bank[h % 2][:, t * P:(t + 1) * P], vP[:, h, t * P:(t + 1) * P], ident)
                last.then_inc(S["vt_done"], 1)
            sumsq(2 * H - 2)
            sumsq(2 * H - 1)
            pe.wait_ge(S["cc_ready"], 1)
            for t in range(NT):
                last = pe.transpose(bank[3][0:24, t * P:(t + 1) * P], cc[:, t, :], ident)
            last.then_inc(S["ct_done"], 1)
            pe.wait_ge(S["ct_lo"], 1)

            def spread(dst, row):
                pick_row = ident_r[0:24, row:row + 1].broadcast_to([24, P])
                pe.wait_ge(S["identr_ready"], 1)
                pe.matmul(dst, pick_row, ct[:, 0, :], start=True, stop=False)
                return pe.matmul(dst, pick_row, ct[:, 1, :], start=False, stop=True)

            for h in range(H):
                pe.wait_ge(S["conv_done"], 3 * H)
                if h >= 3:
                    pe.wait_ge(S["kb_ready"], h - 2)
                spread(bank[5 + h % 3][:, :], H * NPROB + h).then_inc(S["kb_done"], 1)
            pe.wait_ge(S["bv_ready"], H)
            for h in range(H):
                pe.wait_ge(S["kb_ready"], h + 1)
                for t in range(NT):
                    s = slice(t * P, (t + 1) * P)
                    last = pe.matmul(bank[h][:, s], kP[:, h, s], kbP[:, h, s], start=True, stop=True)
                last.then_inc(S["kk_done"], 1)
            pe.wait_ge(S["kb_ready"], H)
            for h in range(H):
                for t in range(NT):
                    s = slice(t * P, (t + 1) * P)
                    last = pe.matmul(bank[4 + h][:, s], kP[:, h, s], qP[:, h, s], start=True, stop=True)
                last.then_inc(S["at_done"], 1)
            for h in range(H):
                pe.wait_ge(S["tt1_ready"], h + 1)
                for t in range(NT):
                    s = slice(t * P, (t + 1) * P)
                    last = pe.transpose(bank[h][:, s], tt[:, h, s], ident)
                last.then_inc(S["t1_done"], 1)
            pe.wait_ge(S["at_ready"], H)
            for l in range(len(LEVELS)):
                final = l == len(LEVELS) - 1
                for h in range(H):
                    pe.wait_ge(S["lt_ready"], H * l + h + 1)
                    if l == 0:
                        pe.wait_ge(S["t1_ready"], h + 1)
                    else:
                        pe.wait_ge(S["t_upd"], H * (l - 1) + h + 1)
                    n = H * l + h
                    if n >= 3:
                        pe.wait_ge(S["yl_ready"], n - 2)
                    for t in range(NT):
                        s = slice(t * P, (t + 1) * P)
                        last = pe.matmul(bank[n % 3][:, s], lt[:, h, s], tm[:, h, s], start=True, stop=True)
                    last.then_inc(S["yl_done"], 1)
                for h in range(H):
                    n = H * l + h
                    pe.wait_ge(S["yl_ready"], n + 1)
                    if n >= 2:
                        pe.wait_ge(S["tt_upd"], n - 1)
                    else:
                        pe.wait_ge(S["t1_ready"], H)
                    for t in range(NT):
                        s = slice(t * P, (t + 1) * P)
                        last = pe.matmul(bank[4 + 2 * (h % 2)][:, s], yy[:, h, s], tt[:, h, s], start=True, stop=True)
                    last.then_inc(S["zt_done"], 1)
                    if not final:
                        for t in range(NT):
                            s = slice(t * P, (t + 1) * P)
                            last = pe.matmul(bank[3 + 2 * (h % 2)][:, s], tt[:, h, s], yy[:, h, s],
                                             start=True, stop=True)
                        last.then_inc(S["z_done"], 1)
                    for k in fir_diags(n):
                        hh, lag = k // LAGS_PE, k % LAGS_PE + 1
                        if lag == 1 and hh > 0:
                            pe.wait_ge(S["firpe_kept"], hh)
                        pe.wait_ge(S["diag_ready"], k + 1)
                        d = bank[7][:, :].rearrange("p (b l) -> p b l", b=B)[:, :, lag:L]
                        v = vP[:, hh].rearrange("p (b l) -> p b l", b=B)[:, :, 0:L - lag]
                        last = pe.matmul(d, diag[:, k % 4, :], v, start=(lag == 1), stop=(lag == LAGS_PE))
                        last.then_inc(S["diag_used"], 1)
            for h in range(H):
                pe.wait_ge(S["tt_upd"], H * (len(LEVELS) - 1) + h + 1)
                for t in range(NT):
                    s = slice(t * P, (t + 1) * P)
                    last = pe.matmul(bank[h][:, s], tt[:, h, s], bv[:, h, s], start=True, stop=True)
                last.then_inc(S["u_done"], 1)
            pe.wait_ge(S["firpe_kept"], H)
            for h in range(H):
                pe.wait_ge(S["u_ready"], h + 1)
                for t in range(NT):
                    s = slice(t * P, (t + 1) * P)
                    last = pe.matmul(bank[4 + h][:, s], yy[:, h, s], att[:, h, s], start=True, stop=True)
                last.then_inc(S["o_done"], 1)
            for n in range(H * NPROB):
                if n >= 4:
                    pe.wait_ge(S["weighted"], n - 3)
                else:
                    pe.wait_ge(S["u_ready"], H)
                spread(bank[n % 4][:, :], n).then_inc(S["bc_done"], 1)
            pe.wait_ge(S["d_ready"], H)
            for h in range(H):
                pe.wait_ge(S["osq_ready"], h + 1)
                for t in range(NT):
                    last = pe.matmul(bank[7][:, H * t + h:H * t + h + 1], sq2[:, h % 2, t * P:(t + 1) * P],
                                     ones[:, 0:1], start=True, stop=True)
                last.then_inc(S["osum_done"], 1)
            pe.wait_ge(S["wod_scaled"], H)
            for n in range(NT * H):
                t, h = n // H, n % H
                if n >= 4:
                    pe.wait_ge(S["x2_done"], n - 3)
                pe.matmul(bank[3 + n % 4][:, :], branch[0][:, h, t * P:(t + 1) * P], wod[:, h, :],
                          start=True, stop=True).then_inc(S["m_done"], 1)

            pe.wait_ge(S["weighted"], H * NPROB)
            for t in range(NT):
                transpose_tile(2, t)
            pe.wait_ge(S["x2_done"], NT * H)
            for t in range(NT):
                pe.wait_ge(S["xnT_ready"], 2 * NT + t + 1)
                for c in range(DC):
                    last = pe.matmul(bank[4][:, NE * t:NE * (t + 1)], xnT[:, c, t * P:(t + 1) * P],
                                     cols[:, C_ROUT + NE * c:C_ROUT + NE * (c + 1)], start=(c == 0), stop=(c == DC - 1))
                last.then_inc(S["rout_done"], 1)

            def products(dst, terms, first=True, final=True):
                for n, (lhsT, rhs) in enumerate(terms):
                    last = pe.matmul(dst, lhsT, rhs, start=(first and n == 0), stop=(final and n == len(terms) - 1))
                return last

            def use_piece(which, n, r):
                pe.wait_ge(w_lo[which], n + 1)
                return piece(which, r)

            def shared_up(e, f):
                n = e * FC + f
                if n >= 2:
                    pe.wait_ge(S["prod_ready"], n - 1)
                for j, name in ((0, "h1_done"), (1, "h3_done")):
                    w = use_piece(j, e, 0)
                    fs = slice(f * P, (f + 1) * P)
                    products(bank[2 * (n % 2) + j][:, :],
                             [(w[:, wi, c, fs], xe[:, 0, xi, c, :]) for wi, xi in ((0, 0), (0, 1), (1, 0))
                              for c in range(DC)]).then_inc(S[name], 1)

            def shared_down(e):
                w = use_piece(2, e, e)
                pe.wait_ge(S["sh_lo"], FC * (e + 1))
                for t in range(NT):
                    ts = slice(t * P, (t + 1) * P)
                    last = products(bank[4 + t][:, :],
                                    [(xe[:, 1, hi, f, ts], w[:, wi, f, :]) for f in range(FC)
                                     for hi, wi in ((0, 0), (0, 1), (1, 0))], first=(e == 0), final=False)
                last.then_inc(S["sd_done"], 1)

            pe.wait_ge(S["xr_lo"], 2 * NT)
            shared_up(0, 0)
            shared_up(0, 1)
            pe.wait_ge(S["sel_ready"], 1)
            anyone = ones[:, 0:1].broadcast_to([P, P])
            for t in range(NT):
                products(bank[5][:, NE * t:NE * (t + 1)],
                         [(masks[:, M_BEFORE, :], sel[:, t, :])] + [(anyone, sel[:, i, :]) for i in range(t)])
            products(bank[5][:, NE * NT:NE * (NT + 1)],
                     [(anyone, sel[:, i, :]) for i in range(NT)]).then_inc(S["pos_done"], 1)
            shared_up(0, 2)
            shared_up(0, 3)
            pe.wait_ge(S["slot_ready"], 1)
            for k in range(TOPK):
                for t in range(NT):
                    last = pe.matmul(bank[6 + k][:, t * P:(t + 1) * P], slot[:, k, t:t + 1].broadcast_to([P, P]), ident,
                                     start=True, stop=True)
                last.then_inc(S["plane_done"], 1)
            pe.wait_ge(S["plane_ready"], TOPK)
            shared_down(0)
            for f in range(FC):
                if f == 0:
                    pe.wait_ge(S["sd_done"], 1)
                shared_up(1, f)
            shared_down(1)

            def gather(J):
                pe.wait_ge(S["pick_ready"], J + NT)
                for u in range(2 * DC):
                    c, i = u // 2, u % 2
                    if u >= 2:
                        pe.wait_ge(S["gx_ready"], 2 * DC // GB * J + u - 1)
                    elif not isinstance(J, int):
                        pe.wait_ge((S["hT_lo"], S["ye_lo"])[u], J - 1)
                    products(bank[2 + i][:, :],
                             [(xnr[:, i, t, c * P:(c + 1) * P], pick[:, t, :])
                              for t in range(NT)]).then_inc(S["gx_done"], 1)
                pe.wait_ge(S["gx_ready"], 2 * DC // GB * J + 2 * DC - 1)
                for b in range(GB):
                    products(bank[2][:, 2 * NE * b:2 * NE * (b + 1)],
                             [(pick[:, t, b * P:(b + 1) * P], gate_r[:, t, :])
                              for t in range(NT)]).then_inc(S["gg_done"], 1)

            def routed_up(j, r, which, name):
                w = use_piece(which, NSH + j, r)
                bs = slice((r % GB) * P, (r % GB + 1) * P)
                if which == 0:
                    pe.wait_ge(S["fsilu_done"], NSH * FC + j)
                    if r % GB == 0:
                        pe.wait_ge(S["gg_ready"], j + GB)
                else:
                    pe.wait_ge(S["prod_ready"], NSH * FC + j)
                products(bank[which][:, :],
                         [(xe[:, 0, xi, c, bs], w[:, wi, c, :]) for c in range(DC)
                          for xi, wi in ((0, 0), (0, 1), (1, 0))]).then_inc(S[name], 1)

            def turn(j, r):
                pe.wait_ge(S["prod_ready"], NSH * FC + j + 1)
                if not isinstance(j, int) or j >= 1:
                    pe.wait_ge(S["hT_lo"], j)
                for f in range(FC):
                    last = pe.transpose(bank[2][:, f * P:(f + 1) * P], hraw[:, r % 2, f * P:(f + 1) * P], ident)
                last.then_inc(S["hr_done"], 1)

            def routed_down(j, r):
                w = use_piece(2, NSH + j, r)
                pe.wait_ge(S["hT_lo"], j + 1)
                if not isinstance(j, int) or j >= 1:
                    pe.wait_ge(S["ye_lo"], j)
                products(bank[3][:, :],
                         [(hTs[:, r % 2, hi, f * P:(f + 1) * P], w[:, wi, f, :]) for f in range(FC)
                          for hi, wi in ((0, 0), (0, 1), (1, 0))]).then_inc(S["ye_done"], 1)

            def give_back(j, r, final=False):
                pe.wait_ge(S["ye_lo"], j + 1)
                pe.wait_ge(S["back_ready"], j + 1)
                for t in range(NT):
                    last = products(bank[4 + t][:, :],
                                    [(back[:, r % 2, t * P:(t + 1) * P], yes[:, r % 2, i, :]) for i in range(2)],
                                    first=False, final=final)
                last.then_inc(S["c_done"], 1)

            def step(j, r):
                routed_up(j, r, 0, "h1_done")
                if not isinstance(j, int) or j >= 1:
                    turn(j - 1, r - 1)
                routed_up(j, r, 1, "h3_done")
                if not isinstance(j, int) or j >= 1:
                    routed_down(j - 1, r - 1)
                if not isinstance(j, int):
                    give_back(j - 2, r - 2)

            last_group = first_of_last(pe)
            gather(0)
            for j in range(2):
                step(j, j)
            with pe.Fori(0, last_group, GB) as done:
                J = done + GB
                step(J - 2, -2)
                step(J - 1, -1)
                gather(J)
                step(J, 0)
                step(J + 1, 1)
            step(last_group + GB - 2, -2)
            step(last_group + GB - 1, -1)
            turn(last_group + GB - 1, -1)
            routed_down(last_group + GB - 1, -1)
            give_back(last_group + GB - 2, -2)
            give_back(last_group + GB - 1, -1, final=True)

        @block.scalar
        def _(act):
            def store_xnT(layer, t):
                act.wait_ge(S["xT_done"], layer * NT + t + 1)
                if layer == 1:
                    act.wait_ge(S["y_done"], NT)
                if layer == 2:
                    act.wait_ge(S["qkv_done"], 3 * H)
                act.activation(xnT[:, :, t * P:(t + 1) * P], bank[t % 2][:, :].rearrange("p (c n) -> p c n", c=DC),
                               ACT.Copy).then_inc(S["xnT_ready"], 1)

            for t in range(NT):
                store_xnT(0, t)

            def exponentials(t):
                act.wait_ge(S["bias_ready"], t + 1)
                if t >= 2:
                    act.wait_ge(S["pT_done"], t - 1)
                act.activation(probs_b[:, t % 2, :], bank[5 + t % 2][:, :], ACT.Exp, bias=nb[:, t:t + 1],
                               accum_out=sm[:, t:t + 1]).then_inc(S["exp_done"], 1)

            exponentials(0)
            for t in range(NT):
                if t + 1 < NT:
                    exponentials(t + 1)
                act.wait_ge(S["pT_done"], t + 1)
                if t >= 2:
                    act.wait_ge(S["pv_done"], t - 1)
                act.activation(probsT_b[:, t % 2, :], bank[7][:, :], ACT.Copy).then_inc(S["pT_ready"], 1)
                act.wait_ge(S["pv_done"], t + 1)
                act.wait_ge(S["rs_ready"], t + 1)
                if t >= 2:
                    act.wait_ge(S["oT_done"], t - 1)
                act.activation(o_b[:, t % 2, :], bank[t % 2][:, :], ACT.Copy,
                               scale=rsm[:, t:t + 1]).then_inc(S["o_kept"], 1)
            for t in range(NT):
                store_xnT(1, t)

            def gate_exp(n):
                act.wait_ge(S["gate_exp_wanted"], n)
                if n == 1:
                    after(act, act.activation(itemp, rows[:, R_TEMP:R_TEMP + H], ACT.Exp, scale=-1.0), act_step)
                    act.activation(beta, lg[:, :, 20:24], ACT.Exp, scale=-1.0).then_inc(S["gate_exp_done"], 1)
                else:
                    act.activation(gt, gt, ACT.Exp).then_inc(S["gate_exp_done"], 1)

            def lag0(g):
                act.wait_ge(S["qkv_done"], g + 1)
                if g == 0:
                    act.wait_ge(S["oT_done"], NT)
                j, h = g // H, g % H
                w = C_CONV + (j * H + h) * KC + KC - 1
                act.activation(plane[j][:, h], bank[5 + g % 3][:, :], ACT.Copy,
                               scale=cols[:, w:w + 1]).then_inc(S["lag0_done"], 1)

            def silu(g):
                j, h = g // H, g % H
                act.wait_ge(S["conv_done"], g + 1)
                act.activation(plane[j][:, h], plane[j][:, h], ACT.Silu).then_inc(S["silu_done"], 1)
                if j > 0:
                    i = g - H
                    act.wait_ge(S["silu_done"], g + 1)
                    if i >= 2:
                        act.wait_ge(S["sumsq_done"], i - 1)
                    act.activation(sq_b[:, i % 2, :], plane[j][:, h], ACT.Square).then_inc(S["sq_done"], 1)

            lag0(0)
            for g in range(1, 3 * H):
                lag0(g)
                silu(g - 1)
                if g in (H + 2, H + 3):
                    gate_exp(g - H - 1)
            silu(3 * H - 1)
            act.wait_ge(S["ct_done"], 1)
            act.activation(ct[:, 0, :], bank[3][0:24, :], ACT.Copy).then_inc(S["ct_ready"], 1)
            for h in range(H):
                act.wait_ge(S["t1_done"], h + 1)
                act.activation(tm[:, h], bank[h][:, :], ACT.Copy).then_inc(S["t1_ready"], 1)
            for l in range(len(LEVELS)):
                for h in range(H):
                    n = H * l + h
                    act.wait_ge(S["yl_done"], n + 1)
                    if l >= 1:
                        act.wait_ge(S["z_done"], n - H + 1)
                    act.activation(yy[:, h], bank[n % 3][:, :], ACT.Copy).then_inc(S["yl_ready"], 1)
                    for k in fir_diags(n):
                        hh, lag = k // LAGS_PE, k % LAGS_PE + 1
                        w = C_FIR + hh * (KS + KM + KL) + KS + KM + KL - 1 - lag
                        if k >= 4:
                            act.wait_ge(S["diag_used"], k - 3)
                        act.activation(diag[:, k % 4, :], ident, ACT.Copy,
                                       scale=cols[:, w:w + 1]).then_inc(S["diag_ready"], 1)
                        if lag == LAGS_PE:
                            act.wait_ge(S["diag_used"], k + 1)
                            act.wait_ge(S["kk_done"], H)
                            act.activation(kbP[:, hh], bank[7][:, :], ACT.Copy).then_inc(S["firpe_kept"], 1)
            for h in range(H):
                act.wait_ge(S["u_done"], h + 1)
                act.wait_ge(S["zt_done"], H * len(LEVELS))
                act.activation(yy[:, h], bank[h][:, :], ACT.Copy).then_inc(S["u_ready"], 1)
            for h in range(H):
                act.wait_ge(S["o_done"], h + 1)
                act.activation(tm[:, h], bank[4 + h][:, :], ACT.Copy).then_inc(S["d_ready"], 1)
            for h in range(H):
                act.wait_ge(S["o_ready"], h + 1)
                if h >= 2:
                    act.wait_ge(S["osum_done"], h - 1)
                act.activation(sq2[:, h % 2, :], branch[0][:, h], ACT.Square).then_inc(S["osq_ready"], 1)

            def high(which, n, r):
                act.wait_ge(ld_raw[which], 16 * (n + 1))
                act.activation(parts(which, r)[:, 0, :], early[:, which, :], ACT.Copy).then_inc(w_hi[which], 1)

            act.wait_ge(S["o_done"], H)
            high(0, 0, 0)
            high(1, 0, 0)
            act.wait_ge(S["osum_done"], H)
            act.wait_ge(S["m_done"], NT * H)
            for t in range(NT):
                act.wait_ge(S["xn_ready"], 2 * NT + t + 1)
                act.activation(xnr[:, 0, t, :], xn[:, t, :], ACT.Copy).then_inc(S["xr_hi"], 1)
                store_xnT(2, t)
                act.wait_ge(S["xnT_ready"], 2 * NT + t + 1)
                act.activation(xe[:, 0, 0, :, t * P:(t + 1) * P], xnT[:, :, t * P:(t + 1) * P],
                               ACT.Copy).then_inc(S["xr_hi"], 1)
            high(2, 0, 0)
            high(2, 1, 1)
            act.wait_ge(S["rexp_wanted"], 1)
            act.activation(rl, rl, ACT.Exp).then_inc(S["rexp_done"], 1)

            def silu_of(n, b):
                act.wait_ge(S["h1_done"], n + 1)
                if not isinstance(n, int) or n >= 1:
                    act.wait_ge(S["prod_ready"], n)
                else:
                    act.wait_ge(S["xr_lo"], 2 * NT)
                act.activation(sil[:], bank[b][:, :], ACT.Silu).then_inc(S["fsilu_done"], 1)

            for e in range(NSH):
                for f in range(FC):
                    n = e * FC + f
                    silu_of(n, 2 * (n % 2))
                    act.wait_ge(S["prod_ready"], n + 1)
                    if e == 1:
                        act.wait_ge(S["sd_done"], 1)
                    act.activation(xe[:, 1, 0, f, :], hraw[:, n % 2, :], ACT.Copy).then_inc(S["sh_hi"], 1)
                if e == 0:
                    act.wait_ge(S["h1_done"], FC)
                    high(0, 1, 0)
                    act.wait_ge(S["h3_done"], FC)
                    high(1, 1, 1)

            def high_up(j, r, which):
                if which == 1:
                    act.wait_ge(S["h3_done"], NSH * FC + j)
                elif isinstance(j, int) and j == 1:
                    act.wait_ge(S["sd_done"], NSH)
                else:
                    act.wait_ge(S["h1_done"], NSH * FC + (0 if isinstance(j, int) and j == 0 else j - 1))
                high(which, NSH + j, r)

            def high_down(j, r):
                if isinstance(j, int) and j < NSH:
                    act.wait_ge(S["sd_done"], j + 1)
                else:
                    act.wait_ge(S["ye_done"], j - 1)
                high(2, NSH + j, r)

            high_up(0, 0, 0)
            high_up(0, 0, 1)
            high_down(0, 0)

            def keep_gathered(J):
                for u in range(2 * DC):
                    act.wait_ge(S["gx_done"], 2 * DC // GB * J + u + 1)
                    act.activation(xe[:, 0, u % 2, u // 2, :], bank[2 + u % 2][:, :],
                                   ACT.Copy).then_inc(S["gx_ready"], 1)
                act.wait_ge(S["gg_done"], J + GB)
                if not isinstance(J, int):
                    act.wait_ge(S["gw_ready"], J)
                act.activation(gg, bank[2][:, 0:GB * 2 * NE], ACT.Copy).then_inc(S["gg_ready"], GB)

            def turned(j, r):
                act.wait_ge(S["hr_done"], j + 1)
                if not isinstance(j, int):
                    act.wait_ge(S["ye_done"], j - 1)
                act.activation(hTs[:, r % 2, 0, :], bank[2][:, :], ACT.Copy).then_inc(S["hT_hi"], 1)

            def gated_output(j, r):
                act.wait_ge(S["ye_done"], j + 1)
                act.wait_ge(S["gw_ready"], j + 1)
                if not isinstance(j, int):
                    act.wait_ge(S["c_done"], j - 1)
                act.activation(yes[:, r % 2, 0, :], bank[3][:, :], ACT.Copy,
                               scale=gw[:, r % GB:r % GB + 1]).then_inc(S["ye_hi"], 1)

            def step(j, r, more=True):
                silu_of(NSH * FC + j, 0)
                if not isinstance(j, int) or j >= 1:
                    turned(j - 1, r - 1)
                if more:
                    high_up(j + 1, r + 1, 0)
                    high_up(j + 1, r + 1, 1)
                if not isinstance(j, int) or j >= 1:
                    gated_output(j - 1, r - 1)
                if more:
                    high_down(j + 1, r + 1)

            last_group = first_of_last(act)
            keep_gathered(0)
            for j in range(2):
                step(j, j)
            with act.Fori(0, last_group, GB) as done:
                J = done + GB
                step(J - 2, -2)
                step(J - 1, -1)
                keep_gathered(J)
                step(J, 0)
                step(J + 1, 1)
            step(last_group + GB - 2, -2)
            step(last_group + GB - 1, -1, more=False)
            turned(last_group + GB - 1, -1)
            gated_output(last_group + GB - 1, -1)

        @block.vector
        def _(dve):
            pow_count = [0]

            def do(ins):
                after(dve, ins, dve_step)

            def rsqrt(dst, lo, width):
                a, b, v, y = (r[:, lo:lo + width] for r in (rs_a, rs_b, rs_in, rs_y))
                pow_count[0] += 1
                dve.wait_ge(S["pow_done"], pow_count[0])
                do(dve.tensor_tensor(a, v, y, ALU.mult))
                do(dve.tensor_tensor(b, a, y, ALU.mult))
                do(dve.tensor_scalar(a, b, -0.5, 1.5, ALU.mult, ALU.add))
                do(dve.tensor_tensor(dst, a, y, ALU.mult))

            def begin_norm(t):
                do(dve.bn_stats(stats[:, t, :], x[:, t, :]))
                do(dve.bn_aggr(mv[:, t, :], stats[:, t, :]))
                dve.tensor_scalar(rs_in[:, t:t + 1], mv[:, t, 1:2], 1e-5, None, ALU.add).then_inc(S["pow_wanted"], 1)

            def end_norm(layer, t):
                rsqrt(rq[:, t:t + 1], t, 1)
                if layer >= 1:
                    dve.wait_ge(S["xT_done"], (layer - 1) * NT + t + 1)
                dve.tensor_scalar(xn[:, t, :], x[:, t, :], mv[:, t, 0:1], rq[:, t:t + 1], ALU.subtract,
                                  ALU.mult).then_inc(S["xn_ready"], 1)

            for t in range(NT):
                dve.wait_ge(ld_x[t], 16)
                begin_norm(t)
                if t >= 1:
                    end_norm(0, t - 1)
            end_norm(0, NT - 1)
            dve.wait_ge(ld_bg, 16)
            dve.wait_ge(S["xn_ready"], NT)
            for t in range(NT):
                after(dve, dve.tensor_tensor_reduce(out=bgprod, in0=xn[:, t, :], in1=bgrow, scale=1.0, scalar=0.0,
                                                    op0=ALU.mult, op1=ALU.add, accum_out=c0s[:, t:t + 1]),
                      S["c0_ready"])
            dve.wait_ge(ld_masks, 16)
            dve.tensor_copy(ident_r[:], ident[:, 0:24]).then_inc(S["identr_ready"], 1)
            for t in range(NT):
                dve.wait_ge(S["y_done"], t + 1)
                dve.tensor_copy(yT[:, :, t * P:(t + 1) * P],
                                bank[2 + t % 2][:, :].rearrange("p (c n) -> p c n", c=DC)).then_inc(S["yT_ready"], 1)
            dve.wait_ge(ld_rows, 16)
            for t in range(NT):
                dve.wait_ge(S["xn_ready"], NT)
                do(dve.tensor_tensor(x[:, t, :], x[:, t, :], rows[:, R_BO:R_BO + D], ALU.add))

            def score_bias(t):
                dve.wait_ge(S["s_done"], t + 1)
                do(dve.tensor_reduce(mx[:, t:t + 1], bank[5 + t % 2][:, :], AX, ALU.max))
                do(dve.tensor_tensor(mc[:, t:t + 1], mx[:, t:t + 1], c0s[:, t:t + 1], ALU.add))
                dve.tensor_tensor(nb[:, t:t + 1], c0s[:, t:t + 1], mc[:, t:t + 1],
                                  ALU.subtract).then_inc(S["bias_ready"], 1)

            def add_projection(t):
                dve.wait_ge(S["proj_done"], t + 1)
                after(dve, dve.tensor_tensor(x[:, t, :], x[:, t, :], bank[2 + t % 2][:, :], ALU.add), S["x1_done"])
                begin_norm(t)

            def normalise(t):
                dve.wait_ge(S["exp_done"], t + 1)
                dve.reciprocal(rsm[:, t:t + 1], sm[:, t:t + 1]).then_inc(S["rs_ready"], 1)

            score_bias(0)
            normalise(0)
            score_bias(1)
            for t in range(NT):
                if t + 1 < NT:
                    normalise(t + 1)
                if t + 2 < NT:
                    score_bias(t + 2)
                dve.wait_ge(S["oT_done"], t + 1)
                if t >= 2:
                    dve.wait_ge(S["proj_done"], t - 1)
                dve.tensor_copy(oT_b[:, t % 2, :], bank[4][:, :]).then_inc(S["oT_ready"], 1)
                if t >= 1:
                    add_projection(t - 1)
                if t >= 2:
                    end_norm(1, t - 2)
            add_projection(NT - 1)
            end_norm(1, NT - 2)
            end_norm(1, NT - 1)

            def over_tokens(ap, n):
                return ap.unsqueeze(1).broadcast_to([P, NT, n])
            gth = gt.rearrange("p t (h n) -> p (t h) n", h=H)
            spreadm = gtm.unsqueeze(2).broadcast_to([P, NT * H, NPROB])

            def gating_1():
                dve.wait_ge(S["gate_done"], NT)
                after(dve, dve.tensor_copy(lg, bank[3][:, 0:24 * NT].rearrange("p (t n) -> p t n", t=NT)),
                      S["gate_exp_wanted"])

            def gating_2():
                dve.wait_ge(S["gate_exp_done"], 1)
                do(dve.tensor_scalar(beta, beta, 1.0, None, ALU.add))
                do(dve.reciprocal(beta, beta))
                do(dve.tensor_tensor(gt, lg[:, :, 0:20], over_tokens(rows[:, R_GB:R_GB + 20], 20), ALU.add))
                for t in range(NT):
                    g3 = gt[:, t, :].rearrange("p (h n) -> p h n", h=H)
                    do(dve.tensor_tensor(g3, g3, itemp.unsqueeze(2).broadcast_to([P, H, NPROB]), ALU.mult))
                do(dve.tensor_reduce(gtm, gth, AX, ALU.max))
                after(dve, dve.tensor_tensor(gth, gth, spreadm, ALU.subtract), S["gate_exp_wanted"])

            def gating_3():
                dve.wait_ge(S["gate_exp_done"], 2)
                do(dve.tensor_reduce(gtm, gth, AX, ALU.add))
                do(dve.reciprocal(gtm, gtm))
                do(dve.tensor_tensor(gth, gth, spreadm, ALU.mult))
                do(dve.tensor_scalar(epsc, rows[:, R_EPS:R_EPS + H], 0.0, 0.2, ALU.max, ALU.min))
                do(dve.tensor_scalar(epsm, epsc, -float(NPROB), 1.0, ALU.mult, ALU.add))
                for t in range(NT):
                    g3 = gt[:, t, :].rearrange("p (h n) -> p h n", h=H)
                    do(dve.tensor_tensor(g3, g3, epsm.unsqueeze(2).broadcast_to([P, H, NPROB]), ALU.mult))
                    do(dve.tensor_tensor(g3, g3, epsc.unsqueeze(2).broadcast_to([P, H, NPROB]), ALU.add))

            for h in range(H):
                dve.wait_ge(ld_wod, 16)
                dve.tensor_scalar(wod[:, h, :], wod[:, h, :], cols[:, C_NORM:C_NORM + 1], None,
                                  ALU.mult).then_inc(S["wod_scaled"], 1)

            def lagged(dst, src, w, lag):
                d = dst.rearrange("p (b l) -> p b l", b=B)[:, :, lag:L]
                s = src.rearrange("p (b l) -> p b l", b=B)[:, :, 0:L - lag]
                return dve.scalar_tensor_tensor(out=d, in0=s, scalar=w, in1=d, op0=ALU.mult, op1=ALU.add)

            def fir_steps(step, heads):
                n = 0
                dve.wait_ge(S["xT_done"], 2 * NT)
                for h in heads:
                    dve.wait_ge(S["silu_done"], h + 1)
                    for i, (taps, off) in enumerate(FIRS):
                        w0 = C_FIR + h * (KS + KM + KL) + off
                        for lag in range(taps):
                            if i == 2 and 1 <= lag <= LAGS_PE:
                                continue
                            if n:
                                dve.wait_ge(step, n)
                            w = cols[:, w0 + taps - 1 - lag:w0 + taps - lag]
                            if lag == 0:
                                ins = dve.tensor_scalar(branch[i][:, h], vP[:, h], w, None, ALU.mult)
                            else:
                                ins = lagged(branch[i][:, h], vP[:, h], w, lag)
                            ins.then_inc(step, 1)
                            n += 1
                            yield
                    fir_end[h] = (step, n)
            fir_end = {}
            streams = [fir_steps(S["fir_even"], (0, 2)), fir_steps(S["fir_odd"], (1, 3))]

            def fir(n):
                for _ in range(n):
                    for stream in streams:
                        next(stream, None)

            def add_fir_pe(h):
                dve.wait_ge(S["firpe_kept"], h + 1)
                dve.wait_ge(*fir_end[h])
                d, src = (v.rearrange("p (b l) -> p b l", b=B)[:, :, 1:] for v in (branch[2][:, h], kbP[:, h]))
                dve.tensor_tensor(d, d, src, ALU.add).then_inc(S["firpe_added"], 1)

            for g in range(3 * H):
                j, h = g // H, g % H
                dve.wait_ge(S["lag0_done"], g + 1)
                for lag in range(1, KC):
                    w = C_CONV + (j * H + h) * KC + KC - 1 - lag
                    ins = lagged(plane[j][:, h], bank[5 + g % 3][:, :], cols[:, w:w + 1], lag)
                    if lag < KC - 1:
                        do(ins)
                    else:
                        ins.then_inc(S["conv_done"], 1)
                if g >= 3:
                    fir(1)
                if g == H + 1:
                    gating_1()
                if g == H + 2:
                    gating_2()
                if g == H + 3:
                    gating_3()
            fir(4)
            for h in range(H):
                dve.wait_ge(S["vt_done"], h + 1)
                dve.tensor_tensor(bv[:, h].rearrange("p (t n) -> p t n", t=NT),
                                  bank[h % 2][:, :].rearrange("p (t n) -> p t n", t=NT),
                                  beta[:, :, h:h + 1].broadcast_to([P, NT, P]), ALU.mult).then_inc(S["bv_ready"], 1)
            dve.wait_ge(S["sumsq_done"], 2 * H)
            after(dve, dve.tensor_scalar(rs_in[:, 0:32], bank[4][:, 256:288], 1e-6, None, ALU.add), S["pow_wanted"])
            fir(5)
            rsqrt(ktr, 0, 32)
            ktr3 = ktr.rearrange("p (i t) -> p t i", t=NT)
            for t in range(NT):
                do(dve.tensor_tensor(cc[:, t, 20:24], beta[:, t, :], ktr3[:, t, 0:H], ALU.mult))
                do(dve.tensor_copy(cc[:, t, 0:20], gt[:, t, :]))
                ins = dve.tensor_tensor(cc[:, t, 3:20:NPROB], gt[:, t, 3:20:NPROB], ktr3[:, t, H:2 * H], ALU.mult)
                if t < NT - 1:
                    do(ins)
                else:
                    ins.then_inc(S["cc_ready"], 1)
            for h in range(H):
                if h == 0:
                    dve.wait_ge(S["ct_ready"], 1)
                    dve.tensor_tensor(ct[:, 1, :], bank[3][0:24, :], ct[:, 0, :].bitcast(F32),
                                      ALU.subtract).then_inc(S["ct_lo"], 1)
                    fir(2)
                dve.wait_ge(S["kb_done"], h + 1)
                dve.tensor_tensor(kbP[:, h], kP[:, h], bank[5 + h % 3][:, :], ALU.mult).then_inc(S["kb_ready"], 1)
            for h in range(H):
                dve.wait_ge(S["kk_done"], h + 1)
                for t in range(NT):
                    s = slice(t * P, (t + 1) * P)
                    ins = dve.scalar_tensor_tensor(out=mt[:, h, s], in0=bank[h][:, s],
                                                   scalar=ktr[:, NT * h + t:NT * h + t + 1],
                                                   in1=masks[:, M_STRICT, :], op0=ALU.mult, op1=ALU.mult)
                    if t < NT - 1:
                        do(ins)
                    else:
                        after(dve, ins, S["mt_ready"])
                m1 = masks[:, M_L1, :].unsqueeze(1).broadcast_to([P, NT, P])
                eye = ident.unsqueeze(1).broadcast_to([P, NT, P])
                t3 = tt[:, h].rearrange("p (t n) -> p t n", t=NT)
                do(dve.tensor_tensor(t3, mt[:, h].rearrange("p (t n) -> p t n", t=NT), m1, ALU.mult))
                dve.tensor_tensor(t3, eye, t3, ALU.subtract).then_inc(S["tt1_ready"], 1)
            for h in range(H):
                dve.wait_ge(S["at_done"], h + 1)
                for t in range(NT):
                    s = slice(t * P, (t + 1) * P)
                    ins = dve.scalar_tensor_tensor(out=att[:, h, s], in0=bank[4 + h][:, s],
                                                   scalar=ktr[:, NT * h + t:NT * h + t + 1],
                                                   in1=masks[:, M_INCL, :], op0=ALU.mult, op1=ALU.mult)
                    if t < NT - 1:
                        do(ins)
                    else:
                        ins.then_inc(S["at_ready"], 1)
            for l in range(len(LEVELS)):
                for h in range(H):
                    fir(FIR_PACE)
                    n = H * l + h
                    if l < len(LEVELS) - 1:
                        dve.wait_ge(S["z_done"], n + 1)
                        dve.tensor_tensor(tm[:, h], tm[:, h], bank[3 + 2 * (h % 2)][:, :],
                                          ALU.subtract).then_inc(S["t_upd"], 1)
                    dve.wait_ge(S["zt_done"], n + 1)
                    dve.tensor_tensor(tt[:, h], tt[:, h], bank[4 + 2 * (h % 2)][:, :],
                                      ALU.subtract).then_inc(S["tt_upd"], 1)
            fir(10 ** 6)
            for h in range(H):
                add_fir_pe(h)
            dve.wait_ge(S["firpe_added"], H)
            for h in range(H):
                for i, dst in enumerate((branch[0], branch[1], branch[2], tm, vP)):
                    if i == 3:
                        dve.wait_ge(S["d_ready"], h + 1)
                    dve.wait_ge(S["bc_done"], h * NPROB + i + 1)
                    dve.tensor_tensor(dst[:, h], dst[:, h], bank[(h * NPROB + i) % 4][:, :],
                                      ALU.mult).then_inc(S["weighted"], 1)

            def low(which, n, r):
                dve.wait_ge(w_hi[which], n + 1)
                split = parts(which, r)
                dve.tensor_tensor(split[:, 1, :], early[:, which, :], split[:, 0, :].bitcast(F32),
                                  ALU.subtract).then_inc(w_lo[which], 1)

            dve.wait_ge(S["osum_done"], H)
            after(dve, dve.tensor_scalar(rs_in[:, 0:16], bank[7][:, 0:16], 1.0 / DV, 1e-5, ALU.mult, ALU.add),
                  S["pow_wanted"])
            rsqrt(orr, 0, 16)
            for t in range(NT):
                for h in range(H):
                    n = t * H + h
                    dve.wait_ge(S["m_done"], n + 1)
                    after(dve, dve.scalar_tensor_tensor(out=x[:, t, :], in0=bank[3 + n % 4][:, :],
                                                        scalar=orr[:, n:n + 1], in1=x[:, t, :], op0=ALU.mult,
                                                        op1=ALU.add), S["x2_done"])
                begin_norm(t)
                if t >= 1:
                    end_norm(2, t - 1)
            low(0, 0, 0)
            end_norm(2, NT - 1)
            low(1, 0, 0)

            for t in range(NT):
                ts = slice(t * P, (t + 1) * P)
                dve.wait_ge(S["xr_hi"], 2 * t + 1)
                dve.tensor_tensor(xnr[:, 1, t, :], xn[:, t, :], xnr[:, 0, t, :].bitcast(F32),
                                  ALU.subtract).then_inc(S["xr_lo"], 1)
                dve.wait_ge(S["xr_hi"], 2 * t + 2)
                dve.tensor_tensor(xe[:, 0, 1, :, ts], xnT[:, :, ts], xe[:, 0, 0, :, ts].bitcast(F32),
                                  ALU.subtract).then_inc(S["xr_lo"], 1)
            dve.wait_ge(S["rout_done"], NT)
            after(dve, dve.tensor_copy(rl, bank[4][:, 0:NT * NE].rearrange("p (t n) -> p t n", t=NT)), S["rout_read"])
            do(dve.tensor_reduce(mx, rl, AX, ALU.max))

            def per_tile(ap):
                return ap.unsqueeze(2).broadcast_to([P, NT, NE])
            after(dve, dve.tensor_tensor(rl, rl, per_tile(mx), ALU.subtract), S["rexp_wanted"])
            for e in range(NE):
                do(dve.memset(prio[:, e:e + 1], float(NE - e)))
            dve.wait_ge(S["rexp_done"], 1)
            do(dve.tensor_reduce(sm, rl, AX, ALU.add))
            do(dve.reciprocal(rsm, sm))
            do(dve.tensor_tensor(rl, rl, per_tile(rsm), ALU.mult))
            do(dve.tensor_tensor(rw1, rl, over_tokens(rows[:, R_RB:R_RB + NE], NE), ALU.add))
            for k in range(TOPK):
                do(dve.tensor_reduce(mx, rw1, AX, ALU.max))
                do(dve.tensor_tensor(rw2, rw1, per_tile(mx), ALU.is_equal))
                do(dve.tensor_tensor(rw2, rw2, over_tokens(prio, NE), ALU.mult))
                do(dve.tensor_reduce(mx, rw2, AX, ALU.max))
                do(dve.tensor_tensor(hot[k], rw2, per_tile(mx), ALU.is_equal))
                if k == 0:
                    do(dve.scalar_tensor_tensor(out=rw1, in0=hot[k], scalar=-1e30, in1=rw1, op0=ALU.mult, op1=ALU.add))
            after(dve, dve.tensor_tensor(sel, hot[0], hot[1], ALU.add), S["sel_ready"])

            def product(n, r, b):
                dve.wait_ge(S["fsilu_done"], n + 1)
                dve.wait_ge(S["h3_done"], n + 1)
                dve.tensor_tensor(hraw[:, r % 2, :], sil[:], bank[b][:, :], ALU.mult).then_inc(S["prod_ready"], 1)

            def shared_hidden(n):
                if n >= 2:
                    dve.wait_ge(S["sh_lo"], n - 1)
                product(n, n, 2 * (n % 2) + 1)
                dve.wait_ge(S["sh_hi"], n + 1)
                dve.tensor_tensor(xe[:, 1, 1, n % FC, :], hraw[:, n % 2, :], xe[:, 1, 0, n % FC, :].bitcast(F32),
                                  ALU.subtract).then_inc(S["sh_lo"], 1)

            shared_hidden(0)
            do(dve.tensor_tensor(gated, sel, rl, ALU.mult))
            do(dve.tensor_copy(gate_r[:, :, 0:NE], gated))
            do(dve.tensor_tensor(gate_r[:, :, NE:2 * NE], gated, gate_r[:, :, 0:NE].bitcast(F32), ALU.subtract))
            shared_hidden(1)
            dve.wait_ge(S["pos_done"], 1)
            do(dve.tensor_copy(cnt, bank[5][:, NE * NT:NE * (NT + 1)]))
            thr = consts[:, K_THR:K_THR + NT].unsqueeze(1).broadcast_to([P, NE, NT])
            do(dve.tensor_tensor(over, cnt.unsqueeze(2).broadcast_to([P, NE, NT]), thr, ALU.is_gt))
            do(dve.tensor_reduce(nblk, over, AX, ALU.add))
            do(dve.tensor_copy(end, nblk))
            for e in range(1, NE):
                do(dve.tensor_tensor(end[:, e:e + 1], end[:, e:e + 1], end[:, e - 1:e], ALU.add))
            do(dve.tensor_tensor(start_b, end, nblk, ALU.subtract))
            do(dve.scalar_tensor_tensor(out=base, in0=over_tokens(start_b, NE), scalar=float(P),
                                        in1=bank[5][:, 0:NE * NT].rearrange("p (t n) -> p t n", t=NT),
                                        op0=ALU.mult, op1=ALU.add))
            for k in range(TOPK):
                do(dve.tensor_tensor(rw1, hot[k], base, ALU.mult))
                ins = dve.tensor_reduce(slot[:, k, :], rw1, AX, ALU.add)
                if k == 0:
                    do(ins)
                else:
                    after(dve, ins, S["slot_ready"])
            nums = consts[:, K_NUM:K_NUM + MAXB]
            do(dve.tensor_tensor(owner, end.unsqueeze(1).broadcast_to([P, MAXB, NE]),
                                 nums.unsqueeze(2).broadcast_to([P, MAXB, NE]), ALU.is_le))
            do(dve.tensor_reduce(expert[:, 0:MAXB], owner, AX, ALU.add))
            do(dve.tensor_scalar(expert[:, 0:MAXB], expert[:, 0:MAXB], float(NE - 1), None, ALU.min))
            firsts = nums.rearrange("p (g b) -> p g b", b=GB)[:, :, 0]
            groups = owner[:, 0, 0:MAXB // GB]
            do(dve.tensor_tensor(groups, end[:, NE - 1:NE].broadcast_to([P, MAXB // GB]), firsts, ALU.is_gt))
            do(dve.tensor_reduce(expert4[:, 0:1], groups, AX, ALU.add))
            do(dve.tensor_scalar(expert[:, MAXB:], expert4[:, 0:1].broadcast_to([P, GB]), float(GB), -float(GB),
                                 ALU.mult, ALU.add))
            do(dve.tensor_scalar(slotg, slot, float(GB * P), None, ALU.add))
            after(dve, dve.tensor_copy(expert_i[:], expert), S["expert_ready"])
            shared_hidden(2)
            shared_hidden(3)
            for k in range(TOPK):
                dve.wait_ge(S["plane_done"], k + 1)
                after(dve, dve.tensor_copy(planes[:, k, :], bank[6 + k][:, :]), S["plane_ready"])

            def find_owners(J):
                def own(ins, n):
                    ins.then_inc(S["turn_step"], 1)
                    dve.wait_ge(S["turn_step"], J + n)
                own(dve.tensor_scalar(turn_numbers, turn_numbers, float(GB), None, ALU.add), 1)
                own(dve.tensor_tensor(owner4, end.unsqueeze(1).broadcast_to([P, GB, NE]),
                                      turn_numbers.unsqueeze(2).broadcast_to([P, GB, NE]), ALU.is_le), 2)
                own(dve.tensor_reduce(expert4, owner4, AX, ALU.add), 3)
                own(dve.tensor_tensor(owner4, expert4.unsqueeze(2).broadcast_to([P, GB, NE]),
                                      nums[:, 0:NE].unsqueeze(1).broadcast_to([P, GB, NE]), ALU.is_equal), 4)

            def make_gate(j, r):
                if r % GB == 0:
                    dve.wait_ge(S["gg_ready"], j + GB)
                b = r % GB
                dve.tensor_tensor(gw2, gg[:, 2 * NE * b:2 * NE * (b + 1)].rearrange("p (i n) -> p i n", i=2),
                                  owner4[:, (r + 2) % GB, :].unsqueeze(1).broadcast_to([P, 2, NE]),
                                  ALU.mult).then_inc(S["gate_step"], 1)
                dve.wait_ge(S["gate_step"], j + 1)
                dve.tensor_reduce(gw[:, b:b + 1], gw2.rearrange("p i n -> p (i n)"), AX,
                                  ALU.add).then_inc(S["gw_ready"], 1)

            dve.wait_ge(ld_iota, 16)

            def make_pick(J, tiles):
                if 0 in tiles:
                    if not isinstance(J, int):
                        dve.wait_ge(S["gg_done"], J)
                    dve.tensor_scalar(slotg, slotg, -float(GB * P), None, ALU.add).then_inc(S["slotg_ready"], GB)
                    dve.wait_ge(S["slotg_ready"], J + GB)
                for t in tiles:
                    dve.tensor_scalar(pick[:, t, :], iota[:], slotg[:, 0, t:t + 1], None,
                                      ALU.is_equal).then_inc(S["pick_step"], 1)
                for t in tiles:
                    dve.wait_ge(S["pick_step"], J + t + 1)
                    dve.scalar_tensor_tensor(out=pick[:, t, :], in0=iota[:], scalar=slotg[:, 1, t:t + 1],
                                             in1=pick[:, t, :].bitcast(F32), op0=ALU.is_equal,
                                             op1=ALU.add).then_inc(S["pick_ready"], 1)

            def next_slots(J):
                dve.tensor_scalar(slots, slots, float(GB * P), None, ALU.add).then_inc(S["slots_step"], GB)

            def begin_back(J, r):
                if not isinstance(J, int):
                    dve.wait_ge(S["c_done"], J + r - 1)
                if r in (-2, 0):
                    dve.wait_ge(S["slots_step"], J + GB)
                dve.tensor_scalar(back[:, r % 2, :], planes[:, 0, :], slots[:, (r + 2) % GB:(r + 2) % GB + 1], None,
                                  ALU.is_equal).then_inc(S["back_step"], 1)

            def end_back(J, r):
                dve.wait_ge(S["back_step"], J + r + 1)
                dve.scalar_tensor_tensor(out=back[:, r % 2, :], in0=planes[:, 1, :],
                                         scalar=slots[:, (r + 2) % GB:(r + 2) % GB + 1],
                                         in1=back[:, r % 2, :].bitcast(F32), op0=ALU.is_equal,
                                         op1=ALU.add).then_inc(S["back_ready"], 1)

            def turned(j, r):
                dve.wait_ge(S["hT_hi"], j + 1)
                dve.tensor_tensor(hTs[:, r % 2, 1, :], bank[2][:, :], hTs[:, r % 2, 0, :].bitcast(F32),
                                  ALU.subtract).then_inc(S["hT_lo"], 1)

            def gated_output(j, r):
                dve.wait_ge(S["ye_hi"], j + 1)
                dve.scalar_tensor_tensor(out=yes[:, r % 2, 1, :], in0=bank[3][:, :], scalar=gw[:, r % GB:r % GB + 1],
                                         in1=yes[:, r % 2, 0, :].bitcast(F32), op0=ALU.mult,
                                         op1=ALU.subtract).then_inc(S["ye_lo"], 1)

            def step(J, r, more=True, picks=False):
                j = J + r
                if not isinstance(j, int) or j >= 1:
                    turned(j - 1, r - 1)
                if not isinstance(j, int):
                    dve.wait_ge(S["hr_done"], j - 1)
                product(NSH * FC + j, r, 1)
                if more:
                    low(0, NSH + j + 1, r + 1)
                if picks:
                    make_pick(J, (0,) if r == -2 else (2, 3))
                make_gate(j, r)
                if more:
                    low(1, NSH + j + 1, r + 1)
                if not isinstance(j, int) or j >= 1:
                    gated_output(j - 1, r - 1)
                if picks and r == -2:
                    make_pick(J, (1,))
                begin_back(J, r)
                end_back(J, r)

            make_pick(0, (0, 1, 2, 3))
            low(0, 1, 0)
            low(1, 1, 1)
            for n in range(FC, 2 * FC):
                shared_hidden(n)
            low(0, NSH, 0)
            low(1, NSH, 0)
            last_group = first_of_last(dve)
            find_owners(0)
            next_slots(0)
            for j in range(2):
                step(0, j)
            with dve.Fori(0, last_group, GB) as done:
                J = done + GB
                find_owners(J)
                next_slots(J)
                step(J, -2, picks=True)
                step(J, -1, picks=True)
                step(J, 0)
                step(J, 1)
            find_owners(last_group + GB)
            next_slots(last_group + GB)
            step(last_group + GB, -2)
            step(last_group + GB, -1, more=False)
            turned(last_group + GB - 1, -1)
            gated_output(last_group + GB - 1, -1)
            dve.wait_ge(S["c_done"], last_group + GB)
            for t in range(NT):
                dve.tensor_tensor(x[:, t, :], x[:, t, :], bank[4 + t][:, :], ALU.add).then_inc(S["acc_done"], 1)


def kernel(**inputs):
    import concourse.bacc as bacc
    from concourse.bass_utils import run_bass_kernel_spmd

    a = {k: np.asarray(v) for k, v in inputs.items()}

    def chunks(w):
        return w.reshape(-1, P, w.shape[1]).transpose(1, 0, 2).reshape(P, -1)

    ctx = a["ctx_1024"]
    by_tile = ctx.reshape(NT, PAIR, TK // P, P, D).transpose(0, 3, 1, 2, 4).reshape(NT, P, -1)
    byT = ctx.transpose(0, 2, 1).reshape(NT, PAIR, DC, P, TK).transpose(0, 3, 1, 2, 4).reshape(NT, P, -1)
    fir = np.concatenate([a[f"L0_attn_fir_{s}"].transpose(1, 0, 2) for s in "sml"], axis=2)
    conv = np.stack([a[f"L0_attn_conv_{s}"].reshape(H, P, KC) for s in "vkq"]).transpose(2, 0, 1, 3)
    wgate = np.concatenate([a["L0_attn_gate_w"].reshape(H * NPROB, D), a["L0_attn_Wb"]]).T
    cols = np.concatenate([conv.reshape(P, -1), fir.reshape(P, -1), a["L0_attn_norm_w"].reshape(P, 1),
                           chunks(wgate), chunks(a["L0_ffn_gate_w"].T)], axis=1)
    row = np.concatenate([a["L0_xattn_bo"], a["L0_attn_gate_b"].ravel(), a["L0_attn_log_temp"].ravel(),
                          a["L0_attn_eps_param"].ravel(), a["L0_ffn_gate_bias"]])
    w1 = list(a["L0_ffn_w1"]) + list(a["L0_ffn_sw1"].reshape(NSH, FF, D))
    w3 = list(a["L0_ffn_w3"]) + list(a["L0_ffn_sw3"].reshape(NSH, FF, D))
    w2 = list(a["L0_ffn_w2"]) + list(a["L0_ffn_sw2"].reshape(D, NSH, FF).transpose(1, 0, 2))
    i, j = np.meshgrid(np.arange(P), np.arange(P), indexing="ij")
    same = i // L == j // L
    merge = [(i // (2 * m) == j // (2 * m)) & (i // m % 2 == 0) & (j // m % 2 == 1) for m in (1,) + LEVELS]
    masks = np.stack([i == j, same & (i < j), same & (i <= j)] + merge + [i < j], axis=1).reshape(P, -1)
    row_no = np.arange(P)[:, None]
    masks = np.concatenate([masks, np.broadcast_to(P * np.arange(NT), (P, NT)),
                            np.broadcast_to(np.arange(MAXB), (P, MAXB)),
                            np.broadcast_to(np.arange(GB) - 2 - GB, (P, GB)),
                            row_no + P * (np.arange(GB) - 2 - GB)[None, :]], axis=1).astype(np.float32)
    arrays = {
        "x_in": a["x"].reshape(NT, P, D),
        "ctx_in": by_tile,
        "ctxT_in": byT,
        "wg_in": chunks(a["L0_xattn_Wg"].T).reshape(P, DC, D),
        "wox_in": chunks(a["L0_xattn_Wo"]).reshape(P, DC, D),
        "wqkv_in": np.concatenate([chunks(a[f"L0_attn_W{s}"].T) for s in "vkq"], axis=1),
        "wod_in": chunks(a["L0_attn_Wo"].T),
        "wffn_in": np.stack([np.concatenate([chunks(p.T), chunks(q.T), chunks(r.T)], axis=1)
                             for p, q, r in zip(w1, w3, w2)]),
        "cols_in": cols,
        "rows_in": np.broadcast_to(row, (P, NROW)),
        "masks_in": masks,
        "iota_in": np.broadcast_to(np.arange(512, dtype=np.float32), (P, 512)),
        "bg_in": np.broadcast_to(a["L0_xattn_bg"], (P, D)),
    }
    arrays = {k: np.ascontiguousarray(v) for k, v in arrays.items()}
    nc = bacc.Bacc("TRN2", target_bir_lowering=False, num_devices=1)
    args = [nc.dram_tensor(k, v.shape, mybir.dt.from_np(v.dtype), kind="ExternalInput").ap() for k, v in arrays.items()]
    args.append(nc.dram_tensor("out", (NT, P, D), F32, kind="ExternalOutput").ap())
    perceiver_block(nc, *args)
    r = run_bass_kernel_spmd(nc, [arrays], core_ids=[0])
    return r.results[0]["out"].reshape(B, L, D)
```
